# Optimizing a Trainium2 kernel written in Bass

```python
import numpy as np
import jax
import jax.numpy as jnp

def _softmax(x, axis=-1):
    return jax.nn.softmax(x, axis=axis)

def _gelu(x):
    return jax.nn.gelu(x, approximate=True)

def _silu(x):
    return jax.nn.silu(x)

def _sigmoid(x):
    return jax.nn.sigmoid(x)

def _layernorm(x, axis=-1, eps=1e-05):
    m = jnp.mean(x, axis=axis, keepdims=True)
    v = jnp.var(x, axis=axis, keepdims=True)
    return (x - m) / jnp.sqrt(v + eps)

def _scatter_add(tgt, idx, src, axis=0):
    return tgt.at[idx].add(src)

def _segment_sum(src, seg, n):
    return jax.ops.segment_sum(src, seg, n)
kernel_name = 'mk_gnn_ffn_d1_gnn_r64_2a4c4d'

def setup_inputs(seed: int=0):
    np.random.seed(seed)
    _w = jnp.asarray

    def _rec_inputs():
        import jax
        import jax.numpy as jnp
        _gk = jax.random.key(seed)
        x = -0.0003713 + 1 * jax.random.normal(jax.random.fold_in(_gk, 1), (50000, 256), jnp.float32)
        src = jax.random.randint(jax.random.fold_in(_gk, 2), (25000,), 0, 50000, jnp.int32)
        dst = jnp.minimum((50000 * jax.random.uniform(jax.random.fold_in(_gk, 3), (25000,)) ** 2.0).astype(jnp.int32), 49999)
        _o = jnp.argsort(dst, stable=True)
        src = src[_o]
        dst = dst[_o]
        return (x, src, dst)
    x, src, dst = _rec_inputs()

    def _L0_gnn_setup():
        import jax, jax.numpy as jnp
        import numpy as np
        N, E = (50000, 12500)
        IN_C, HID_C, OUT_C = (256, 256, 256)

        def _gcn_prep(edge_index, n_nodes):
            src = jnp.concatenate([edge_index[0], jnp.arange(n_nodes, dtype=edge_index.dtype)])
            dst = jnp.concatenate([edge_index[1], jnp.arange(n_nodes, dtype=edge_index.dtype)])
            deg = jax.ops.segment_sum(jnp.ones_like(dst, dtype=jnp.float32), dst, num_segments=n_nodes)
            deg_inv_sqrt = jnp.where(deg > 0, jax.lax.rsqrt(jnp.maximum(deg, 1.0)), 0.0)
            norm = deg_inv_sqrt[src] * deg_inv_sqrt[dst]
            return (src, dst, norm)

        def _gcn_layer(x, src, dst, norm, W, b, n_nodes):
            h = x @ W
            msg = h[src] * norm[:, None]
            out = jax.ops.segment_sum(msg, dst, num_segments=n_nodes)
            return out + b
        key = jax.random.key(seed)
        ks = jax.random.split(key, 8)
        x_piece = jax.random.normal(ks[0], (N, IN_C), dtype=jnp.float32)
        edge_index_piece = jax.random.randint(ks[1], (2, E), 0, N, dtype=jnp.int64)
        batch = jnp.zeros((N,), dtype=jnp.int64)

        def glorot(k, fan_in, fan_out):
            s = jnp.sqrt(6.0 / (fan_in + fan_out)).astype(jnp.float32)
            return jax.random.uniform(k, (fan_in, fan_out), jnp.float32, -s, s)
        return {'x_piece': x_piece, 'edge_index_piece': edge_index_piece, 'batch': batch, 'W1': glorot(ks[2], IN_C, HID_C), 'b1': jnp.zeros((HID_C,), jnp.float32), 'W2': glorot(ks[3], HID_C, HID_C), 'b2': jnp.zeros((HID_C,), jnp.float32), 'W3': glorot(ks[4], HID_C, OUT_C), 'b3': jnp.zeros((OUT_C,), jnp.float32)}
    _L0_gnn_all = _L0_gnn_setup()
    _L0_gnn_in = {k: v for k, v in _L0_gnn_all.items() if k in ('W1', 'b1', 'W2', 'b2', 'W3', 'b3')}
    del _L0_gnn_all

    def _L0_ffn_setup():
        import jax, jax.numpy as jnp
        import numpy as np
        B, S, D = (8, 64, 256)
        H = 4 * D
        CAPACITY = 0.5
        key = jax.random.key(seed)
        ks = jax.random.split(key, 6)
        x = jax.random.normal(ks[0], (B, S, D), dtype=jnp.float32)
        attention_mask = jnp.zeros((B, 1, 1, S), dtype=jnp.float32)
        wr = jax.random.normal(ks[1], (D, 1), dtype=jnp.float32) * 0.02
        br = jnp.zeros((1,), dtype=jnp.float32)
        w1 = jax.random.normal(ks[2], (D, H), dtype=jnp.float32) * 0.02
        b1 = jnp.zeros((H,), dtype=jnp.float32)
        w2 = jax.random.normal(ks[3], (H, D), dtype=jnp.float32) * 0.02
        b2 = jnp.zeros((D,), dtype=jnp.float32)
        return {'x': x, 'attention_mask': attention_mask, 'wr': wr, 'br': br, 'w1': w1, 'b1': b1, 'w2': w2, 'b2': b2}
    _L0_ffn_all = _L0_ffn_setup()
    _L0_ffn_in = {k: v for k, v in _L0_ffn_all.items() if k in ('attention_mask', 'wr', 'br', 'w1', 'b1', 'w2', 'b2')}
    del _L0_ffn_all
    return {'x': x, 'src': src, 'dst': dst, 'L0_gnn_W1': _L0_gnn_in['W1'], 'L0_gnn_b1': _L0_gnn_in['b1'], 'L0_gnn_W2': _L0_gnn_in['W2'], 'L0_gnn_b2': _L0_gnn_in['b2'], 'L0_gnn_W3': _L0_gnn_in['W3'], 'L0_gnn_b3': _L0_gnn_in['b3'], 'L0_ffn_attention_mask': _L0_ffn_in['attention_mask'], 'L0_ffn_wr': _L0_ffn_in['wr'], 'L0_ffn_br': _L0_ffn_in['br'], 'L0_ffn_w1': _L0_ffn_in['w1'], 'L0_ffn_b1': _L0_ffn_in['b1'], 'L0_ffn_w2': _L0_ffn_in['w2'], 'L0_ffn_b2': _L0_ffn_in['b2']}

def reference(x, src, dst, L0_gnn_W1, L0_gnn_b1, L0_gnn_W2, L0_gnn_b2, L0_gnn_W3, L0_gnn_b3, L0_ffn_attention_mask, L0_ffn_wr, L0_ffn_br, L0_ffn_w1, L0_ffn_b1, L0_ffn_w2, L0_ffn_b2):
    import jax
    import jax.numpy as jnp

    def _L0_gnn_ref(x_piece, edge_index_piece, batch, W1, b1, W2, b2, W3, b3):
        import jax, jax.numpy as jnp
        import numpy as np
        N, E = (50000, 12500)
        IN_C, HID_C, OUT_C = (256, 256, 256)

        def _gcn_prep(edge_index, n_nodes):
            src = jnp.concatenate([edge_index[0], jnp.arange(n_nodes, dtype=edge_index.dtype)])
            dst = jnp.concatenate([edge_index[1], jnp.arange(n_nodes, dtype=edge_index.dtype)])
            deg = jax.ops.segment_sum(jnp.ones_like(dst, dtype=jnp.float32), dst, num_segments=n_nodes)
            deg_inv_sqrt = jnp.where(deg > 0, jax.lax.rsqrt(jnp.maximum(deg, 1.0)), 0.0)
            norm = deg_inv_sqrt[src] * deg_inv_sqrt[dst]
            return (src, dst, norm)

        def _gcn_layer(x, src, dst, norm, W, b, n_nodes):
            h = x @ W
            msg = h[src] * norm[:, None]
            out = jax.ops.segment_sum(msg, dst, num_segments=n_nodes)
            return out + b
        n_nodes = x_piece.shape[0]
        src, dst, norm = _gcn_prep(edge_index_piece, n_nodes)
        x = _gcn_layer(x_piece, src, dst, norm, W1, b1, n_nodes)
        x = jax.nn.gelu(x)
        x = _gcn_layer(x, src, dst, norm, W2, b2, n_nodes)
        x = jax.nn.gelu(x)
        x = _gcn_layer(x, src, dst, norm, W3, b3, n_nodes)
        return x

    def _L0_ffn_ref(x, attention_mask, wr, br, w1, b1, w2, b2):
        import jax, jax.numpy as jnp
        import numpy as np
        B, S, D = (8, 64, 256)
        H = 4 * D
        CAPACITY = 0.5
        b, s, d = x.shape
        weights = (jnp.einsum('bsd,do->bso', x, wr) + br)[..., 0]
        k = max(1, int(CAPACITY * s))
        kk = k - 1 if k > 1 else 1
        _, idx = jax.lax.top_k(weights, k)
        sel_idx = idx[:, :kk]
        sel = jnp.take_along_axis(x, sel_idx[:, :, None], axis=1)
        h = jax.nn.gelu(jnp.einsum('bkd,dh->bkh', sel, w1) + b1)
        y = jnp.einsum('bkh,hd->bkd', h, w2) + b2
        w_sel = jnp.take_along_axis(weights, sel_idx, axis=1)
        y = y * w_sel[..., None]
        batch_idx = jnp.arange(b)[:, None]
        processed = jnp.zeros_like(x).at[batch_idx, sel_idx].set(y)
        return processed + x
    edge_index = jnp.stack([src, dst])
    batch0 = jnp.zeros((50000,), jnp.int32)
    x = x + _L0_gnn_ref(_layernorm(x, axis=-1), edge_index, batch0, L0_gnn_W1, L0_gnn_b1, L0_gnn_W2, L0_gnn_b2, L0_gnn_W3, L0_gnn_b3)
    x = x + _L0_ffn_ref(_layernorm(x, axis=-1)[None], L0_ffn_attention_mask, L0_ffn_wr, L0_ffn_br, L0_ffn_w1, L0_ffn_b1, L0_ffn_w2, L0_ffn_b2)[0]
    return x

_drawn_inputs = setup_inputs


def setup_inputs(seed=0):
    import zlib

    import numpy as np

    out = dict(_drawn_inputs(seed))
    spreads = {'L0_gnn_b1': (0.0, 0.1),
     'L0_gnn_b2': (0.0, 0.1),
     'L0_gnn_b3': (0.0, 0.1),
     'L0_ffn_b1': (0.0, 0.8),
     'L0_ffn_b2': (0.0, 0.777)}
    factors = {'L0_ffn_wr': 4.306, 'L0_ffn_w1': 4.902, 'L0_ffn_w2': 4.56}
    for name, (base, spread) in spreads.items():
        noise = np.random.default_rng([zlib.crc32(name.encode()), seed]).standard_normal(out[name].shape)
        drawn = base * np.exp(spread * noise) if base else spread * noise
        out[name] = jnp.asarray(drawn.astype(out[name].dtype))
    for name, factor in factors.items():
        out[name] = (out[name] * factor).astype(out[name].dtype)
    return out
```

```python
from contextlib import ExitStack

import concourse.bass as bass
from concourse import mybir

ALU = mybir.AluOpType
ACT = mybir.ActivationFunctionType
AX_X = mybir.AxisListType.X
F32 = mybir.dt.float32
F32R = mybir.dt.float32r
F16 = mybir.dt.float16
I32 = mybir.dt.int32
RMAX = bass.bass_isa.ReduceOp.max

P = 128
RING = 4
WARM = 12
EPS = 1e-5
FAR = 1 << 20


class At:

    def __init__(self, group, off):
        self.n = group * RING + off
        self.slot = off % RING
        self.two = off % 2
        self.round = group + off // RING


def steps(eng, count, stages, peel=0):
    stages = [s if len(s) == 3 else (*s, None) for s in stages]

    def one(group, off, static):
        for stage, lag, only in stages:
            if only is not None and (off - lag) % RING != only:
                continue
            if static and not 0 <= off - lag < count:
                continue
            stage(At(group, off - lag))

    for v in range(WARM):
        one(0, v, True)
    with eng.Fori(WARM // RING, count // RING - peel) as group:
        for off in range(RING):
            one(group, off, False)
    lags = max(lag for _, lag, _ in stages)
    for v in range(count - RING * peel, count + lags):
        one(0, v, True)


def at_least(eng, sem, value):
    if not isinstance(value, int) or value > 0:
        eng.wait_ge(sem, value)


def alone(eng, sem, value):
    if not isinstance(value, int):
        eng.wait_ge(sem, value)
        eng.sem_inc(PASSED[0], 1)
    elif value > 0:
        eng.wait_ge(sem, value)


PASSED = [None]


def gnn_ffn(nc, x, src, dst, W1, b1, W2, b2, W3, b3, wr, br, w1, fb1, w2, fb2, out):
    N, D = x.shape
    E = src.shape[0]
    H = w1.shape[1]
    K_SEL = N // 2 - 1
    ET = -(-E // P)
    NP = -(-N // (2 * P))
    EXT = NP * 2 * P
    ROWS = EXT + ET * P
    COLS = 2 * NP
    HC = COLS // 4
    LAST_P = (N - (NP - 1) * 2 * P) // 2
    TC = ET // 2
    LAST_E = E - (ET - 1) * P
    KC = D // P
    FH = H // P
    DW = D + 8
    PAD_DST = 70000
    assert D == 256 and ET == NP and ET % RING == 0 and TC % 2 == 0 and COLS <= 512 and PAD_DST > ROWS - ET * P

    with ExitStack() as ctx:
        def sb(name, shape, dt=F32):
            return ctx.enter_context(nc.sbuf_tensor(name, shape, dt))

        def pb(name, shape=(P, 512), dt=F32):
            return ctx.enter_context(nc.psum_tensor(name, list(shape), dt))

        semaphores = []

        def sem(name):
            semaphores.append(nc.alloc_semaphore(name=name))
            return semaphores[-1]

        def sems(name):
            return [sem(f"{name}{i}") for i in range(RING)]

        def dram(name, shape, dt=F32):
            return nc.dram_tensor(name, shape, dt, kind="Internal").ap()

        rows = [dram(f"rows{l}", (ROWS if l else EXT, D)) for l in range(3)]
        normed = dram("normed", (ROWS, DW))
        ext_out = dram("ext_out", (ET * P, D))
        same_dram = dram("same_dram", (ET, P, P))
        turned_dst = dram("turned_dst", (ET, P))
        inv_root = dram("inv_root", (COLS * P, 1))
        row_of = dram("row_of", (EXT, 1), I32)

        ident = sb("ident", [P, P])
        turn = sb("turn", [P, P])
        ones = sb("ones", [P, P])
        below = sb("below", [P, P])
        iota_p16 = sb("iota_p16", [P, P], F16)
        iota_c16 = sb("iota_c16", [P, COLS], F16)
        iota_i = sb("iota_i", [P, COLS], I32)
        node_i = sb("node_i", [P, COLS], I32)
        ext_id = sb("ext_id", [P, ET], I32)
        lin_id = sb("lin_id", [P, COLS], I32)
        eps_t = sb("eps_t", [P, 1])
        half = sb("half", [P, COLS])
        iota_f = sb("iota_f", [P, COLS])

        nat_i = sb("nat_i", [P, 3, 2, P], I32)
        prev_i = sb("prev_i", [P, 2], I32)
        nat_f = sb("nat_f", [P, 4, 2, P])
        nat_next = sb("nat_next", [P, 2, P])
        prev_f = sb("prev_f", [P, 2])
        turned = sb("turned", [P, 4, ET])
        src_i = sb("src_i", [P, ET], I32)
        emit_i = sb("emit_i", [P, ET], I32)
        dst_i = sb("dst_i", [P, ET], I32)
        dst_safe = sb("dst_safe", [P, ET], I32)
        lo_i = sb("lo_i", [P, ET], I32)
        hi_i = sb("hi_i", [P, ET], I32)
        odd_i = sb("odd_i", [P, ET], I32)
        lo_f = sb("lo_f", [P, ET])
        hi_f = sb("hi_f", [P, ET])
        table_i = sb("table_i", [P, ET], I32)
        table_f = sb("table_f", [P, ET])
        hot_lo = sb("hot_lo", [P, RING, P], F16)
        hot_hi = sb("hot_hi", [P, RING, COLS], F16)
        back = sb("back", [P, 2, P])
        root = sb("root", [P, COLS])
        inv = sb("inv", [P, COLS])
        inv_t = sb("inv_t", [P, 4, P])
        inv_dst = sb("inv_dst", [P, ET])

        w_all = sb("w_all", [P, COLS])

        rings = ctx.enter_context(ExitStack())

        def ring(name, shape, dt=F32):
            return rings.enter_context(nc.sbuf_tensor(name, shape, dt))

        xin = ring("xin", [P, RING, 2 * D])
        gout = ring("gout", [P, RING, 2 * D])
        stats = ring("stats", [P, RING, 2, 6])
        mv = ring("mv", [P, RING, 2, 2])
        veps = ring("veps", [P, RING, 2])
        rstd = ring("rstd", [P, RING, 2])
        rs = ring("rs", [P, RING, 2])
        dst_row = ring("dst_row", [P, RING * P])
        same_out = ring("same_out", [P, RING, P])
        idx_a = ring("idx_a", [P, RING], I32)
        got_a = ring("got_a", [P, RING])

        w_in = ring("w_in", [P, KC, D])
        w_hi = ring("w_hi", [P, 3, KC, D], F32R)
        w_lo = ring("w_lo", [P, 3, KC, D], F32R)
        bias = ring("bias", [P, 3, 2 * D])
        wr_row = ring("wr_row", [P, D])
        br_col = ring("br_col", [P, 1])
        xt_hi = ring("xt_hi", [P, 2, 2, KC, P], F32R)
        xt_lo = ring("xt_lo", [P, 2, 2, KC, P], F32R)
        zb = ring("zb", [P, 2, 2 * D])
        same_t = ring("same_t", [P, RING, P])
        idx_m = ring("idx_m", [P, RING], I32)
        idx_s = ring("idx_s", [P, RING], I32)
        idx_r = ring("idx_r", [P, RING], I32)
        val_r = ring("val_r", [P, RING], I32)
        got_r = ring("got_r", [P, RING], I32)
        src_row = ring("src_row", [P, ET], I32)
        msg = ring("msg", [P, RING, D])
        own = ring("own", [P, RING, D])
        tot = ring("tot", [P, 2, D])
        et_hi = ring("et_hi", [P, 2, KC, P], F32R)
        et_lo = ring("et_lo", [P, 2, KC, P], F32R)
        ez = ring("ez", [P, 2, D])
        eh = ring("eh", [P, 2, D])
        eo = ring("eo", [P, RING, D])


        xres = ring("xres", [P, RING, 2 * D])
        x2 = ring("x2", [P, RING, 2 * D])
        nb = ring("nb", [P, RING, 2, DW])
        dot = ring("dot", [P, RING, 2])
        junk = ring("junk", [P, 3, D])
        xe = ring("xe", [P, RING, D])
        x2e = ring("x2e", [P, RING, D])
        nbe = ring("nbe", [P, RING, DW])
        dote = ring("dote", [P, RING])
        we = ring("we", [P, RING])
        stats_e = ring("stats_e", [P, RING, 6])
        mv_e = ring("mv_e", [P, RING, 2])
        veps_e = ring("veps_e", [P, RING])
        rs_e = ring("rs_e", [P, RING])
        oute = ring("oute", [P, RING, D])
        emit_f = ring("emit_f", [P, ET])
        hi_emit = ring("hi_emit", [P, ET])
        hot_lo_f = ring("hot_lo_f", [P, 2, P])
        hot_w = ring("hot_w", [P, 2, COLS])

        pT = [pb("pT0"), pb("pT1")]
        pO = [pb("pO0"), pb("pO1")]
        pS, pE, pZ, pW = pb("pS"), pb("pE"), pb("pZ"), pb("pW")

        PASSED[0] = sem("passed")
        s_const = sem("s_const")
        s_pad = sem("s_pad")
        s_nat = sem("s_nat")
        s_nat2 = sem("s_nat2")
        s_pro = sem("s_pro")
        s_flip = sem("s_flip")
        s_flipped = sem("s_flipped")
        s_back = sem("s_back")
        s_turned_st = sem("s_turned_st")
        s_hot = sem("s_hot")
        s_count = sem("s_count")
        s_root = sem("s_root")
        s_inv_t = sem("s_inv_t")
        s_inv_st = sem("s_inv_st")
        s_lin = sem("s_lin")


        def phase():
            return nc.Block()

        with phase() as block:
            def pair_rows(dram_rows, n, width=D):
                return dram_rows.rearrange("(j p s) d -> j p (s d)", p=P, s=2)[n]

            src_v, dst_v = src, dst
            ext3 = [None] + [r[EXT:ROWS, :].rearrange("(t p) d -> t p d", p=P) for r in rows[1:]]
            node3 = [r[0:EXT, :] for r in rows]

            p0_ld, p0_st = sems("p0_ld"), sems("p0_st")
            p0_free, p0_stats, p0_mv, p0_sd, p0_rs, p0_rstd, p0_norm = (sem(f"p0_{k}") for k in
                ("free", "stats", "mv", "sd", "rs", "rstd", "norm"))
            dr_ld, so_st = sem("dr_ld"), sem("so_st")
            so_done = sem("so_done")
            da_got = sems("da_got")
            da_idx, da_kept = sem("da_idx"), sem("da_kept")

            x_last = x[(NP - 1) * 2 * P:N, :].rearrange("(p s) d -> p (s d)", s=2)
            x_full = x[0:(NP - 1) * 2 * P, :]

            @block.sync
            def _(sp):
                sp.wait_ge(s_pad, 3)
                full = (ET - 1 - TC) * P
                for k, a in ((0, src_v), (1, dst_v)):
                    sp.dma_start(nat_i[0:TC, k, 0, :], a[0:TC * P].rearrange("(t e) -> t e", e=P)).then_inc(s_nat, 16)
                    sp.dma_start(nat_i[0:TC - 1, k, 1, :], a[TC * P:TC * P + full].rearrange("(t e) -> t e", e=P)).then_inc(s_nat, 16)
                    sp.dma_start(nat_i[TC - 1:TC, k, 1, 0:LAST_E], a[TC * P + full:E].rearrange("(t e) -> t e", t=1)).then_inc(s_nat, 16)
                sp.dma_start(nat_i[0:TC, 2, 0, :], dst_v[1:TC * P + 1].rearrange("(t e) -> t e", e=P)).then_inc(s_nat, 16)
                sp.dma_start(nat_i[0:TC - 1, 2, 1, :], dst_v[TC * P + 1:TC * P + full + 1].rearrange("(t e) -> t e", e=P)).then_inc(s_nat, 16)
                sp.dma_start(nat_i[TC - 1:TC, 2, 1, 0:LAST_E - 1], dst_v[TC * P + full + 1:E].rearrange("(t e) -> t e", t=1)).then_inc(s_nat, 16)
                with nc.allow_non_contiguous_dma(reason="one edge of each tile"):
                    sp.dma_start(prev_i[1:TC, 0:1],
                                 dst_v[0:(TC - 1) * P].rearrange("(t e) -> t e", e=P)[:, P - 1:P]).then_inc(s_nat, 16)
                    sp.dma_start(prev_i[0:TC, 1:2],
                                 dst_v[(TC - 1) * P:(2 * TC - 1) * P].rearrange("(t e) -> t e", e=P)[:, P - 1:P]).then_inc(s_nat, 16)

                def load_x(v):
                    at_least(sp, p0_norm, v.n - RING + 1)
                    if isinstance(v.n, int) and v.n == NP - 1:
                        sp.dma_start(xin[0:LAST_P, v.slot, :], x_last).then_inc(p0_ld[v.slot], 16)
                    else:
                        sp.dma_start(xin[:, v.slot, :], pair_rows(x_full, v.n)).then_inc(p0_ld[v.slot], 16)

                def load_dst_rows(v):
                    at_least(sp, so_done, v.round)
                    sp.dma_start(dst_row[:, :], bcast_rows(v)).then_inc(dr_ld, 16)

                td = turned_dst.rearrange("(g r) e -> g (r e)", r=RING)

                def bcast_rows(v):
                    return td[v.round].rearrange("(o f) -> o f", o=1).to_broadcast([P, RING * P])

                for v in range(RING):
                    load_x(At(0, v))
                sp.wait_ge(s_back, 1)
                sp.dma_start(turned_dst.rearrange("(c t) e -> t c e", c=2), back[0:TC, :, :]).then_inc(s_turned_st, 16)
                sp.wait_ge(s_turned_st, 16)
                sp.wait_ge(s_lin, 1)
                sp.dma_start(row_of.rearrange("(p c) o -> p (c o)", p=P), lin_id[:, :]).then_inc(s_lin, 16)
                sp.wait_ge(s_inv_t, 2)
                sp.dma_start(inv_root.rearrange("(c t e) o -> t c (e o)", c=4, e=P), inv_t[0:HC, :, :]).then_inc(s_inv_st, 16)

                def load_x_later(v):
                    if not (isinstance(v.n, int) and v.n < RING):
                        load_x(v)
                steps(sp, NP, [(load_dst_rows, 0, 0), (load_x_later, 0)], peel=1)

            @block.gpsimd
            def _(pool):
                g = nc.gpsimd
                g.memset(nat_i[:, 0, :, :], 0).then_inc(s_pad, 1)
                g.memset(nat_i[:, 1:3, :, :], PAD_DST).then_inc(s_pad, 1)
                g.memset(prev_i[:, :], -1).then_inc(s_pad, 1)
                g.memset(ident[:, :], 0.0).then_inc(s_const, 1)
                g.memset(turn[:, :], 0.0).then_inc(s_const, 1)
                g.memset(ones[:, :], 1.0).then_inc(s_const, 1)
                pool.wait_ge(s_const, 3)
                g.affine_select(out=ident[:, :], in_=ident[:, :], compare_op=ALU.not_equal, fill=1.0, base=0,
                                pattern=[[-1, P]], channel_multiplier=1).then_inc(s_const, 1)
                g.affine_select(out=turn[:, :], in_=turn[:, :], compare_op=ALU.not_equal, fill=1.0, base=-(P - 1),
                                pattern=[[1, P]], channel_multiplier=1).then_inc(s_const, 1)
                g.affine_select(out=below[:, :], in_=ones[:, :], compare_op=ALU.is_gt, fill=0.0, base=0,
                                pattern=[[1, P]], channel_multiplier=-1).then_inc(s_const, 1)
                g.iota(iota_i[:, :], pattern=[[1, COLS]], base=0, channel_multiplier=0).then_inc(s_const, 1)
                g.iota(node_i[:, :], pattern=[[2 * P, NP], [1, 2]], base=1, channel_multiplier=2).then_inc(s_const, 1)
                g.iota(ext_id[:, :], pattern=[[P, ET]], base=EXT, channel_multiplier=1).then_inc(s_const, 1)
                g.memset(eps_t[:, :], EPS).then_inc(s_const, 1)
                g.iota(lin_id[:, :], pattern=[[1, COLS]], base=0, channel_multiplier=COLS).then_inc(s_lin, 1)

                pool.wait_ge(s_inv_st, 16)

                def ask(v):
                    at_least(pool, da_kept, v.n - RING + 1)
                    g.tensor_copy(idx_a[:, v.slot:v.slot + 1], table_i[:, bass.ds(v.n, 1)]).then_inc(da_idx, 1)
                    alone(pool, da_idx, v.n + 1)
                    g.indirect_dma_start(out=got_a[:, v.slot:v.slot + 1], out_offset=None, in_=inv_root,
                                         in_offset=bass.IndirectOffsetOnAxis(ap=idx_a[:, v.slot:v.slot + 1], axis=0)
                                         ).then_inc(da_got[v.slot], 16)

                def keep(v):
                    pool.wait_ge(da_got[v.slot], 16 * (v.round + 1))
                    g.tensor_copy(inv_dst[:, bass.ds(v.n, 1)], got_a[:, v.slot:v.slot + 1]).then_inc(da_kept, 1)

                def root_of(v):
                    pool.wait_ge(p0_sd, v.n + 1)
                    g.tensor_tensor(rs[:, v.slot, :], veps[:, v.slot, :], half[:, 0:2], ALU.pow).then_inc(p0_rs, 1)

                steps(pool, ET, [(root_of, 0), (keep, 3), (ask, 0)])

            @block.scalar
            def _(act):
                act.wait_ge(s_root, 1)
                nc.scalar.activation(inv[:, :], root[:, :], ACT.Sqrt).then_inc(s_root, 1)

                def add_eps(v):
                    act.wait_ge(p0_mv, v.n + 1)
                    nc.scalar.activation(veps[:, v.slot, :], mv[:, v.slot, :, 1], ACT.Identity,
                                         bias=eps_t[:, 0:1]).then_inc(p0_sd, 1)

                def store(v):
                    act.wait_ge(p0_norm, v.n + 1)
                    act.dma_start(pair_rows(node3[0], v.n), gout[:, v.slot, :]).then_inc(p0_st[v.slot], 16)

                def store_same(v):
                    act.wait_ge(so_done, v.round + 1)
                    act.dma_start(same_dram.rearrange("(g r) e f -> g e r f", r=RING)[v.round],
                                  same_out[:, :, :]).then_inc(so_st, 16)

                steps(act, NP, [(add_eps, 0), (store_same, 1, 1), (store, 3)])
                for s in range(RING):
                    act.wait_ge(p0_st[s], 16 * NP // RING)
                act.wait_ge(so_st, 16 * NP // RING)

            @block.vector
            def _(dve):
                v_ = nc.vector
                count = [0]

                def link(ins):
                    count[0] += 1
                    ins.then_inc(s_pro, 1)
                    dve.wait_ge(s_pro, count[0])

                link(v_.memset(pW[:, :], 0.0))
                dve.wait_ge(s_nat, 16 * 11)
                dve.wait_ge(s_const, 10)
                link(v_.tensor_copy(nat_f[:, 0:2, :, :], nat_i[:, 0:2, :, :]))
                link(v_.tensor_copy(nat_next[:, :, :], nat_i[:, 2, :, :]))
                link(v_.tensor_copy(prev_f[:, :], prev_i[:, :]))
                link(v_.tensor_tensor(nat_f[:, 2, :, :], nat_next[:, :, :], nat_f[:, 1, :, :], ALU.is_equal))
                link(v_.scalar_tensor_tensor(out=nat_f[:, 2, :, :], in0=nat_f[:, 2, :, :], scalar=float(FAR),
                                             in1=nat_f[:, 1, :, :], op0=ALU.mult, op1=ALU.add))
                link(v_.memset(nat_f[:, 3, :, :], 0.0))
                v_.tensor_tensor(nat_f[:, 3, :, 0], prev_f[:, :], nat_f[:, 1, :, 0], ALU.is_equal).then_inc(s_flip, 1)
                dve.wait_ge(s_flipped, 1)
                link(v_.tensor_copy(turned[:, 0:2, :], pT[0][:, 0:2 * ET]))
                v_.tensor_copy(turned[:, 2:4, :], pT[1][:, 0:2 * ET]).then_inc(s_flip, 1)
                dve.wait_ge(s_flipped, 2)
                for k in range(4):
                    ps = pO[k // 2][:, (k % 2) * ET:(k % 2 + 1) * ET].rearrange("p (t o) -> p t o", o=2)[:, :, 1]
                    last = v_.tensor_copy(turned[:, k, :].rearrange("p (t o) -> p t o", o=2)[:, :, 1], ps)
                last.then_inc(s_flip, 1)
                dve.wait_ge(s_flip, 3)
                v_.tensor_copy(src_i[:, :], turned[:, 0, :])
                v_.tensor_copy(emit_i[:, :], turned[:, 2, :])
                link(v_.tensor_copy(dst_i[:, :], turned[:, 1, :]))
                link(v_.tensor_scalar(lo_i[:, :], dst_i[:, :], 1, P - 1, ALU.logical_shift_right, ALU.bitwise_and))
                link(v_.tensor_scalar(hi_i[:, :], dst_i[:, :], 8, 1, ALU.logical_shift_right, ALU.logical_shift_left))
                link(v_.tensor_scalar(odd_i[:, :], dst_i[:, :], 1, None, ALU.bitwise_and))
                link(v_.tensor_tensor(hi_i[:, :], hi_i[:, :], odd_i[:, :], ALU.bitwise_or))
                link(v_.tensor_copy(lo_f[:, :], lo_i[:, :]))
                link(v_.tensor_copy(hi_f[:, :], hi_i[:, :]))
                link(v_.tensor_copy(iota_p16[:, :], iota_i[:, 0:P]))
                link(v_.tensor_copy(iota_c16[:, :], iota_i[:, :]))
                link(v_.tensor_copy(iota_f[:, :], iota_i[:, :]))
                link(v_.tensor_scalar(dst_safe[:, :], turned[:, 1, :], float(N - 1), None, ALU.min))
                link(v_.tensor_scalar(emit_f[:, :], turned[:, 2, :], float(N), 1024.0, ALU.is_ge, ALU.mult))
                link(v_.tensor_tensor(hi_emit[:, :], emit_f[:, :], hi_f[:, :], ALU.add))
                link(v_.scalar_tensor_tensor(out=table_f[:, :], in0=hi_f[:, :], scalar=float(P), in1=lo_f[:, :],
                                             op0=ALU.mult, op1=ALU.add))
                link(v_.tensor_scalar(table_i[:, :], table_f[:, :], float(COLS * P - 1), None, ALU.min))
                dve.wait_ge(s_flipped, 3)
                v_.tensor_copy(back[0:TC, :, :], pO[0][0:TC, 0:2 * P].rearrange("t (c e) -> t c e", c=2)).then_inc(s_back, 1)

                def hots(v):
                    at_least(dve, s_count, v.n - RING + 1)
                    v_.tensor_scalar(hot_lo[:, v.slot, :], iota_p16[:, :], lo_f[:, bass.ds(v.n, 1)], None, ALU.is_equal)
                    v_.tensor_scalar(hot_hi[:, v.slot, :], iota_c16[:, :], hi_f[:, bass.ds(v.n, 1)], None,
                                     ALU.is_equal).then_inc(s_hot, 1)

                steps(dve, ET, [(hots, 0)])
                dve.wait_ge(s_count, ET)
                v_.tensor_scalar(root[:, :], pW[:, 0:COLS], 1.0, None, ALU.add).then_inc(s_root, 1)
                dve.wait_ge(s_root, 2)
                link(v_.reciprocal(inv[:, :], inv[:, :]))
                link(v_.tensor_tensor(half[:, :], inv[:, :], inv[:, :], ALU.mult))
                link(v_.tensor_tensor(half[:, :], half[:, :], root[:, :], ALU.mult))
                link(v_.tensor_scalar(half[:, :], half[:, :], -0.5, 1.5, ALU.mult, ALU.add))
                link(v_.tensor_tensor(inv[:, :], inv[:, :], half[:, :], ALU.mult))
                v_.memset(half[:, :], -0.5).then_inc(s_inv_t, 1)
                dve.wait_ge(s_flipped, 4)
                v_.tensor_copy(inv_t[0:HC, :, :], pO[1][0:HC, 0:4 * P].rearrange("t (c e) -> t c e", c=4)).then_inc(s_inv_t, 1)

                def statistics(v):
                    dve.wait_ge(p0_ld[v.slot], 16 * (v.round + 1))
                    for s in range(2):
                        last = v_.bn_stats(stats[:, v.slot, s, :], xin[:, v.slot, s * D:(s + 1) * D])
                    last.then_inc(p0_stats, 1)
                    alone(dve, p0_stats, v.n + 1)
                    for s in range(2):
                        last = v_.bn_aggr(mv[:, v.slot, s, :], stats[:, v.slot, s, :])
                    last.then_inc(p0_mv, 1)

                def normalise(v):
                    dve.wait_ge(p0_rs, v.n + 1)
                    v_.tensor_tensor(rstd[:, v.slot, :], rs[:, v.slot, :], inv[:, bass.ds(v.n * 2, 2)],
                                     ALU.mult).then_inc(p0_rstd, 1)
                    dve.wait_ge(p0_rstd, v.n + 1)
                    at_least(dve, p0_st[v.slot], 16 * v.round)
                    for s in range(2):
                        last = v_.tensor_scalar(gout[:, v.slot, s * D:(s + 1) * D], xin[:, v.slot, s * D:(s + 1) * D],
                                                mv[:, v.slot, s, 0:1], rstd[:, v.slot, s:s + 1], ALU.subtract, ALU.mult)
                    last.then_inc(p0_norm, 1)

                def same(v):
                    dve.wait_ge(dr_ld, 16 * (v.round + 1))
                    at_least(dve, so_st, 16 * v.round)
                    v_.tensor_tensor(same_out[:, :, :], dst_row[:, :].rearrange("p (r e) -> p r e", r=RING),
                                     turned[:, 1, bass.ds(v.n, RING)].rearrange("p (r o) -> p r o", o=1).to_broadcast([P, RING, P]),
                                     ALU.is_equal).then_inc(so_done, 1)

                steps(dve, NP, [(statistics, 0), (normalise, 2), (same, 0, 0)])

            @block.tensor
            def _(pe):
                t_ = nc.tensor
                pe.wait_ge(s_const, 10)
                pe.wait_ge(s_flip, 1)
                for k in range(4):
                    for c in range(2):
                        o = (k % 2) * ET + c * TC
                        last = t_.transpose(pT[k // 2][:, o:o + TC], nat_f[0:TC, k, c, :], ident[0:TC, 0:TC])
                last.then_inc(s_flipped, 1)
                pe.wait_ge(s_flip, 2)
                for k in range(2):
                    last = t_.matmul(pO[k][:, 0:2 * ET], turn[:, :], turned[:, 2 * k:2 * k + 2, :], start=True, stop=True)
                last.then_inc(s_flipped, 1)
                pe.wait_ge(s_flip, 3)
                for c in range(2):
                    last = t_.transpose(pO[0][0:TC, c * P:(c + 1) * P], turned[:, 1, c * TC:(c + 1) * TC], ident[:, :])
                last.then_inc(s_flipped, 1)

                def tally(v):
                    pe.wait_ge(s_hot, v.n + 1)
                    t_.matmul(pW[:, 0:COLS], hot_lo[:, v.slot, :], hot_hi[:, v.slot, :], start=False, stop=False,
                              skip_group_check=True).then_inc(s_count, 1)

                steps(pe, ET, [(tally, 0)])
                pe.wait_ge(s_inv_t, 1)
                for c in range(4):
                    last = t_.transpose(pO[1][0:HC, c * P:(c + 1) * P], inv[:, c * HC:(c + 1) * HC], ident[:, :])
                last.then_inc(s_flipped, 1)

        G_LD, G_ST = sems("g_ld"), sems("g_st")
        E_ST = sems("e_st")
        S_LD, O_LD, OG_LD, M_LD = sems("s_ld"), sems("o_ld"), sems("og_ld"), sems("m_ld")
        R_ST, R_LD = sems("r_st"), sems("r_ld")
        (w_got, w_split, b_got, t_done, xh_done, xl_done, o_done, z_done, h_done, carry_done, sum_done, tot_done,
         et_done, eh_done, el_done, pz_done, ez_done, eg_done, eo_done, i_m, i_s, i_r, r_kept) = (sem(k) for k in (
            "w_got", "w_split", "b_got", "t_done", "xh_done", "xl_done", "o_done", "z_done", "h_done", "carry_done",
            "sum_done", "tot_done", "et_done", "eh_done", "el_done", "pz_done", "ez_done", "eg_done", "eo_done",
            "i_m", "i_s", "i_r", "r_kept"))

        (xb_done, x2_done, st_done, mv_done, ve_done, r2_done, n_done, d_done, w_done, on_done, i_x, xeb_done, x2e_done,
         ste_done, mve_done, vee_done, re_done, ne_done, de_done, we_done, oe_done, hot_done, w_tally, nb_zero) = (
            sem(k) for k in ("xb_done", "x2_done", "st_done", "mv_done", "ve_done", "r2_done", "n_done", "d_done",
                             "w_done", "on_done", "i_x", "xeb_done", "x2e_done", "ste_done", "mve_done", "vee_done",
                             "re_done", "ne_done", "de_done", "we_done", "oe_done", "hot_done", "w_tally", "nb_zero"))

        def total(layer, v):
            return v.n + layer * NP

        def rounds(layer, v):
            return v.round + layer * (NP // RING)

        def turn_pair(pe, layer):
            def stage(v):
                n = total(layer, v)
                pe.wait_ge(G_LD[v.slot], 16 * (rounds(layer, v) + 1))
                at_least(pe, xl_done, n - 1)
                for s in range(2):
                    for k in range(KC):
                        o = (s * KC + k) * P
                        last = nc.tensor.transpose(pT[v.two][:, o:o + P], xin[:, v.slot, o:o + P], ident[:, :])
                last.then_inc(t_done, 1)
            return stage

        def three_passes(out_ps, hi, lo, whi, wlo):
            for k in range(KC):
                nc.tensor.matmul(out_ps, hi(k), whi(k), start=(k == 0), stop=False)
                nc.tensor.matmul(out_ps, hi(k), wlo(k), start=False, stop=False)
                last = nc.tensor.matmul(out_ps, lo(k), whi(k), start=False, stop=(k == KC - 1))
            return last

        def multiply_pair(pe, layer):
            def stage(v):
                n = total(layer, v)
                pe.wait_ge(xl_done, n + 1)
                at_least(pe, z_done if layer < 2 else x2_done, n - 1 if layer < 2 else v.n - 1)
                if layer == 2 and isinstance(v.n, int) and v.n < 2:
                    pe.wait_ge(z_done, 2 * NP)
                for s in range(2):
                    last = three_passes(pO[v.two][:, s * D:(s + 1) * D],
                                        lambda k: xt_hi[:, v.two, s, k, :], lambda k: xt_lo[:, v.two, s, k, :],
                                        lambda k: w_hi[:, layer, k, :], lambda k: w_lo[:, layer, k, :])
                last.then_inc(o_done, 1)
            return stage

        def sum_tile(pe, layer):
            def stage(v):
                n = total(layer, v)
                pe.wait_ge(S_LD[v.slot], 16 * (rounds(layer, v) + 1))
                pe.wait_ge(carry_done, n + 1)
                at_least(pe, tot_done, n)
                nc.tensor.matmul(pS[:, 0:D], same_t[:, v.slot, :], msg[:, v.slot, :], start=True,
                                 stop=True).then_inc(sum_done, 1)
            return stage

        def turn_tile(pe, layer):
            def stage(v):
                n = total(layer, v)
                pe.wait_ge(tot_done, n + 1)
                at_least(pe, el_done, n)
                for k in range(KC):
                    last = nc.tensor.transpose(pE[:, k * P:(k + 1) * P], tot[:, v.two, k * P:(k + 1) * P], ident[:, :])
                last.then_inc(et_done, 1)
            return stage

        def multiply_tile(pe, layer):
            def stage(v):
                n = total(layer, v)
                pe.wait_ge(el_done, n + 1)
                at_least(pe, ez_done if layer < 2 else x2e_done, n if layer < 2 else v.n)
                three_passes(pZ[:, 0:D], lambda k: et_hi[:, v.two, k, :], lambda k: et_lo[:, v.two, k, :],
                             lambda k: w_hi[:, layer, k, :], lambda k: w_lo[:, layer, k, :]).then_inc(pz_done, 1)
            return stage

        def high_pair(act, layer):
            def stage(v):
                n = total(layer, v)
                act.wait_ge(t_done, n + 1)
                at_least(act, o_done, n - 1)
                nc.scalar.activation(xt_hi[:, v.two, :, :, :].rearrange("p s k c -> p (s k c)"), pT[v.two][:, :],
                                     ACT.Copy).then_inc(xh_done, 1)
            return stage

        def low_pair(dve, layer):
            def stage(v):
                n = total(layer, v)
                dve.wait_ge(xh_done, n + 1)
                nc.vector.tensor_tensor(xt_lo[:, v.two, :, :, :].rearrange("p s k c -> p (s k c)"), pT[v.two][:, :],
                                        xt_hi[:, v.two, :, :, :].rearrange("p s k c -> p (s k c)").bitcast(F32),
                                        ALU.subtract).then_inc(xl_done, 1)
            return stage

        def high_tile(act, layer):
            def stage(v):
                n = total(layer, v)
                act.wait_ge(et_done, n + 1)
                at_least(act, pz_done, n - 1)
                nc.scalar.activation(et_hi[:, v.two, :, :].rearrange("p k c -> p (k c)"), pE[:, 0:D],
                                     ACT.Copy).then_inc(eh_done, 1)
            return stage

        def low_tile(dve, layer):
            def stage(v):
                n = total(layer, v)
                dve.wait_ge(eh_done, n + 1)
                nc.vector.tensor_tensor(et_lo[:, v.two, :, :].rearrange("p k c -> p (k c)"), pE[:, 0:D],
                                        et_hi[:, v.two, :, :].rearrange("p k c -> p (k c)").bitcast(F32),
                                        ALU.subtract).then_inc(el_done, 1)
            return stage

        def carry(dve, layer):
            def stage(v):
                n = total(layer, v)
                dve.wait_ge(M_LD[v.slot], 16 * (rounds(layer, v) + 1))
                if isinstance(v.n, int) and v.n == 0:
                    nc.vector.engine_nop().then_inc(carry_done, 1)
                    return
                dve.wait_ge(sum_done, n)
                nc.vector.scalar_tensor_tensor(out=msg[:, v.slot, :], in0=pS[:, 0:D],
                                               scalar=turned[:, 3, bass.ds(v.n, 1)], in1=msg[:, v.slot, :],
                                               op0=ALU.mult, op1=ALU.add).then_inc(carry_done, 1)
            return stage

        def add_own(dve, layer):
            def stage(v):
                n = total(layer, v)
                if layer == 0:
                    dve.wait_ge(OG_LD[v.slot], 16 * (v.round + 1))
                else:
                    dve.wait_ge(O_LD[v.slot], 16 * (rounds(layer - 1, v) + 1))
                dve.wait_ge(sum_done, n + 1)
                at_least(dve, et_done, n - 1)
                nc.vector.tensor_tensor(tot[:, v.two, :], pS[:, 0:D], own[:, v.slot, :], ALU.add).then_inc(tot_done, 1)
            return stage

        def fetch_first(pool):
            def stage(v):
                g = nc.gpsimd
                at_least(pool, sum_done, v.n - RING + 1)
                g.tensor_copy(idx_m[:, v.slot:v.slot + 1], src_i[:, bass.ds(v.n, 1)]).then_inc(i_m, 1)
                at_least(pool, tot_done, v.n - RING + 1)
                g.tensor_copy(idx_s[:, v.slot:v.slot + 1], dst_safe[:, bass.ds(v.n, 1)]).then_inc(i_s, 1)
                at_least(pool, R_ST[v.slot], 16 * v.round)
                g.tensor_copy(idx_r[:, v.slot:v.slot + 1], emit_i[:, bass.ds(v.n, 1)])
                g.tensor_copy(val_r[:, v.slot:v.slot + 1], ext_id[:, bass.ds(v.n, 1)]).then_inc(i_r, 1)
                alone(pool, i_m, v.n + 1)
                g.indirect_dma_start(out=msg[:, v.slot, :], out_offset=None, in_=rows[0],
                                     in_offset=bass.IndirectOffsetOnAxis(ap=idx_m[:, v.slot:v.slot + 1], axis=0)
                                     ).then_inc(M_LD[v.slot], 16)
                alone(pool, i_s, v.n + 1)
                g.indirect_dma_start(out=own[:, v.slot, :], out_offset=None, in_=rows[0],
                                     in_offset=bass.IndirectOffsetOnAxis(ap=idx_s[:, v.slot:v.slot + 1], axis=0)
                                     ).then_inc(OG_LD[v.slot], 16)
                alone(pool, i_r, v.n + 1)
                g.indirect_dma_start(out=row_of, out_offset=bass.IndirectOffsetOnAxis(ap=idx_r[:, v.slot:v.slot + 1], axis=0),
                                     in_=val_r[:, v.slot:v.slot + 1], in_offset=None, bounds_check=N - 1,
                                     oob_is_err=False).then_inc(R_ST[v.slot], 16)
            return stage

        def ask_row(pool):
            def stage(v):
                g = nc.gpsimd
                at_least(pool, M_LD[v.slot], 16 * rounds(1, v))
                at_least(pool, r_kept, v.n - RING + 1)
                g.tensor_copy(idx_r[:, v.slot:v.slot + 1], src_i[:, bass.ds(v.n, 1)]).then_inc(i_r, 1)
                alone(pool, i_r, ET + v.n + 1)
                g.indirect_dma_start(out=got_r[:, v.slot:v.slot + 1], out_offset=None, in_=row_of,
                                     in_offset=bass.IndirectOffsetOnAxis(ap=idx_r[:, v.slot:v.slot + 1], axis=0)
                                     ).then_inc(R_LD[v.slot], 16)
            return stage

        def fetch_second(pool):
            def stage(v):
                g = nc.gpsimd
                pool.wait_ge(R_LD[v.slot], 16 * (v.round + 1))
                g.tensor_copy(src_row[:, bass.ds(v.n, 1)], got_r[:, v.slot:v.slot + 1]).then_inc(r_kept, 1)
                alone(pool, sum_done, ET + v.n - RING + 1)
                g.indirect_dma_start(out=msg[:, v.slot, :], out_offset=None, in_=rows[1],
                                     in_offset=bass.IndirectOffsetOnAxis(ap=got_r[:, v.slot:v.slot + 1], axis=0)
                                     ).then_inc(M_LD[v.slot], 16)
            return stage

        def load_pair(sp, layer):
            def stage(v):
                at_least(sp, t_done, total(layer, v) - RING + 1)
                sp.dma_start(xin[:, v.slot, :], pair_rows(node3[layer], v.n)).then_inc(G_LD[v.slot], 16)
            return stage

        def load_same(sp, layer):
            def stage(v):
                at_least(sp, sum_done, total(layer, v) - RING + 1)
                sp.dma_start(same_t[:, v.slot, :], same_dram[v.n]).then_inc(S_LD[v.slot], 16)
            return stage

        def load_own(sp, layer):
            def stage(v):
                at_least(sp, tot_done, total(layer, v) - RING + 1)
                sp.dma_start(own[:, v.slot, :], ext3[layer][v.n]).then_inc(O_LD[v.slot], 16)
            return stage

        def stored(eng, layer):
            for s in range(RING):
                if layer == 0:
                    eng.wait_ge(p0_st[s], 16 * NP // RING)
                else:
                    eng.wait_ge(G_ST[s], 16 * layer * NP // RING)
                    eng.wait_ge(E_ST[s], 16 * layer * ET // RING)

        def halves(w, k):
            return w.rearrange("(k p) n -> p k n", p=P)

        with phase() as block:
            @block.sync
            def _(sp):
                for l, w in enumerate((W1, W2, W3)):
                    at_least(sp, w_split, 2 * l)
                    sp.dma_start(w_in[:, :, :], halves(w, KC)).then_inc(w_got, 16)
                for l, b in enumerate((b1, b2, b3)):
                    for s in range(2):
                        sp.dma_start(bias[:, l, s * D:(s + 1) * D],
                                     b.rearrange("(o n) -> o n", o=1).to_broadcast([P, D])).then_inc(b_got, 16)
                sp.dma_start(wr_row[:, :], wr.rearrange("n o -> o n").to_broadcast([P, D])).then_inc(b_got, 16)
                sp.dma_start(br_col[:, :], br.rearrange("(o n) -> o n", o=1).to_broadcast([P, 1])).then_inc(b_got, 16)

                def store_tile(layer):
                    def stage(v):
                        sp.wait_ge(eo_done, total(layer, v) + 1)
                        sp.dma_start(ext3[layer + 1][v.n], eo[:, v.slot, :]).then_inc(E_ST[v.slot], 16)
                    return stage

                for layer in range(2):
                    stored(sp, layer)
                    own_stage = [(load_own(sp, layer), 0)] if layer else []
                    steps(sp, NP, [(load_pair(sp, layer), 0), (load_same(sp, layer), 0), *own_stage,
                                   (store_tile(layer), 6)])

            @block.gpsimd
            def _(pool):
                stored(pool, 0)
                steps(pool, ET, [(fetch_first(pool), 0)])
                for s in range(RING):
                    pool.wait_ge(R_ST[s], 16 * ET // RING)
                stored(pool, 1)
                steps(pool, ET, [(fetch_second(pool), 2), (ask_row(pool), 0)])

            @block.tensor
            def _(pe):
                for layer in range(2):
                    steps(pe, NP, [(turn_pair(pe, layer), 0), (multiply_pair(pe, layer), 1), (sum_tile(pe, layer), 0),
                                   (turn_tile(pe, layer), 1), (multiply_tile(pe, layer), 2)])

            @block.scalar
            def _(act):
                nc.scalar.preload_act_table(ACT.Gelu_apprx_tanh)

                def gelu_pair(layer):
                    def stage(v):
                        n = total(layer, v)
                        act.wait_ge(z_done, n + 1)
                        at_least(act, G_ST[v.slot], 16 * rounds(layer, v))
                        nc.scalar.activation(gout[:, v.slot, :], zb[:, v.two, :], ACT.Gelu_apprx_tanh).then_inc(h_done, 1)
                    return stage

                def store_pair(layer):
                    def stage(v):
                        act.wait_ge(h_done, total(layer, v) + 1)
                        act.dma_start(pair_rows(node3[layer + 1], v.n), gout[:, v.slot, :]).then_inc(G_ST[v.slot], 16)
                    return stage

                def gelu_tile(layer):
                    def stage(v):
                        n = total(layer, v)
                        act.wait_ge(ez_done, n + 1)
                        at_least(act, eo_done, n - 1)
                        nc.scalar.activation(eh[:, v.two, :], ez[:, v.two, :], ACT.Gelu_apprx_tanh).then_inc(eg_done, 1)
                    return stage

                for layer in range(2):
                    steps(act, NP, [(high_pair(act, layer), 0), (gelu_tile(layer), 4), (gelu_pair(layer), 3),
                                    (store_pair(layer), 4), (high_tile(act, layer), 1)])
                for s in range(RING):
                    act.wait_ge(G_ST[s], 16 * 2 * NP // RING)
                    act.wait_ge(E_ST[s], 16 * 2 * ET // RING)

            @block.vector
            def _(dve):
                v_ = nc.vector
                for l in range(3):
                    dve.wait_ge(w_got, 16 * (l + 1))
                    v_.tensor_copy(w_hi[:, l, :, :], w_in[:, :, :]).then_inc(w_split, 1)
                    dve.wait_ge(w_split, 2 * l + 1)
                    v_.tensor_tensor(w_lo[:, l, :, :], w_in[:, :, :], w_hi[:, l, :, :].bitcast(F32),
                                     ALU.subtract).then_inc(w_split, 1)
                dve.wait_ge(b_got, 16 * 8)

                def bias_pair(layer):
                    def stage(v):
                        n = total(layer, v)
                        dve.wait_ge(o_done, n + 1)
                        at_least(dve, h_done, n - 1)
                        v_.tensor_tensor(zb[:, v.two, :], pO[v.two][:, :], bias[:, layer, :], ALU.add).then_inc(z_done, 1)
                    return stage

                def bias_tile(layer):
                    def stage(v):
                        n = total(layer, v)
                        dve.wait_ge(pz_done, n + 1)
                        at_least(dve, eg_done, n - 1)
                        v_.scalar_tensor_tensor(out=ez[:, v.two, :], in0=pZ[:, 0:D], scalar=inv_dst[:, bass.ds(v.n, 1)],
                                                in1=bias[:, layer, 0:D], op0=ALU.mult, op1=ALU.add).then_inc(ez_done, 1)
                    return stage

                def scale_tile(layer):
                    def stage(v):
                        n = total(layer, v)
                        dve.wait_ge(eg_done, n + 1)
                        at_least(dve, E_ST[v.slot], 16 * rounds(layer, v))
                        v_.tensor_scalar(eo[:, v.slot, :], eh[:, v.two, :], inv_dst[:, bass.ds(v.n, 1)], None,
                                         ALU.mult).then_inc(eo_done, 1)
                    return stage

                for layer in range(2):
                    steps(dve, NP, [(add_own(dve, layer), 1), (carry(dve, layer), 0), (low_tile(dve, layer), 2),
                                    (low_pair(dve, layer), 0), (bias_tile(layer), 3), (bias_pair(layer), 2),
                                    (scale_tile(layer), 5)])

        X_LD, X_ST, N_ST, XE_LD, NE_ST, OE_ST = (sems("xr_ld"), sems("out_st"), sems("nb_st"), sems("xe_ld"),
                                                 sems("nbe_st"), sems("oute_st"))
        out_full = out[0:(NP - 1) * 2 * P, :]
        out_last = out[(NP - 1) * 2 * P:N, :].rearrange("(p s) d -> p (s d)", s=2)
        normed3 = normed[EXT:ROWS, :].rearrange("(t p) d -> t p d", p=P)
        ext_out3 = ext_out.rearrange("(t p) d -> t p d", p=P)
        L = 2

        def is_last(v):
            return isinstance(v.n, int) and v.n == NP - 1

        with phase() as block:
            @block.sync
            def _(sp):
                stored(sp, L)

                def load_x_pair(v):
                    at_least(sp, x2_done, v.n - RING + 1)
                    if is_last(v):
                        sp.dma_start(xres[0:LAST_P, v.slot, :], x_last).then_inc(X_LD[v.slot], 16)
                    else:
                        sp.dma_start(xres[:, v.slot, :], pair_rows(x_full, v.n)).then_inc(X_LD[v.slot], 16)

                def store_normed_tile(v):
                    sp.wait_ge(we_done, v.n + 1)
                    sp.dma_start(normed3[v.n], nbe[:, v.slot, :]).then_inc(NE_ST[v.slot], 16)

                def store_out_tile(v):
                    sp.wait_ge(oe_done, v.n + 1)
                    sp.dma_start(ext_out3[v.n], oute[:, v.slot, :]).then_inc(OE_ST[v.slot], 16)

                steps(sp, NP, [(load_pair(sp, L), 0), (load_same(sp, L), 0), (load_own(sp, L), 0), (load_x_pair, 0),
                               (store_normed_tile, 7), (store_out_tile, 7)], peel=1)
                for s in range(RING):
                    sp.wait_ge(NE_ST[s], 16 * ET // RING)
                    sp.wait_ge(OE_ST[s], 16 * ET // RING)

            @block.gpsimd
            def _(pool):
                g = nc.gpsimd
                stored(pool, L)

                def fetch_third(v):
                    alone(pool, sum_done, 2 * ET + v.n - RING + 1)
                    g.tensor_copy(idx_m[:, v.slot:v.slot + 1], src_row[:, bass.ds(v.n, 1)]).then_inc(i_m, 1)
                    alone(pool, i_m, ET + v.n + 1)
                    g.indirect_dma_start(out=msg[:, v.slot, :], out_offset=None, in_=rows[2],
                                         in_offset=bass.IndirectOffsetOnAxis(ap=idx_m[:, v.slot:v.slot + 1], axis=0)
                                         ).then_inc(M_LD[v.slot], 16)

                def fetch_residual(v):
                    alone(pool, x2e_done, v.n - RING + 1)
                    g.tensor_copy(idx_s[:, v.slot:v.slot + 1], dst_safe[:, bass.ds(v.n, 1)]).then_inc(i_s, 1)
                    alone(pool, i_s, ET + v.n + 1)
                    g.indirect_dma_start(out=xe[:, v.slot, :], out_offset=None, in_=x,
                                         in_offset=bass.IndirectOffsetOnAxis(ap=idx_s[:, v.slot:v.slot + 1], axis=0)
                                         ).then_inc(XE_LD[v.slot], 16)

                def root_pair(v):
                    pool.wait_ge(ve_done, v.n + 1)
                    g.tensor_tensor(rs[:, v.slot, :], veps[:, v.slot, :], half[:, 0:2], ALU.pow).then_inc(r2_done, 1)

                def root_tile(v):
                    pool.wait_ge(vee_done, v.n + 1)
                    g.tensor_tensor(rs_e[:, v.slot:v.slot + 1], veps_e[:, v.slot:v.slot + 1], half[:, 0:1],
                                    ALU.pow).then_inc(re_done, 1)

                steps(pool, ET, [(root_pair, 4), (root_tile, 5), (fetch_third, 0), (fetch_residual, 2)])

            @block.tensor
            def _(pe):
                def tally_w(v):
                    pe.wait_ge(hot_done, v.n + 1)
                    nc.tensor.matmul(pW[:, 0:COLS], hot_lo_f[:, v.two, :], hot_w[:, v.two, :], start=False, stop=False,
                                     skip_group_check=True).then_inc(w_tally, 1)

                steps(pe, NP, [(turn_pair(pe, L), 0), (multiply_pair(pe, L), 1), (sum_tile(pe, L), 0),
                               (turn_tile(pe, L), 1), (multiply_tile(pe, L), 2), (tally_w, 8)])

            @block.scalar
            def _(act):
                def eps_pair(v):
                    act.wait_ge(mv_done, v.n + 1)
                    nc.scalar.activation(veps[:, v.slot, :], mv[:, v.slot, :, 1], ACT.Identity,
                                         bias=eps_t[:, 0:1]).then_inc(ve_done, 1)

                def eps_tile(v):
                    act.wait_ge(mve_done, v.n + 1)
                    nc.scalar.activation(veps_e[:, v.slot:v.slot + 1], mv_e[:, v.slot, 1:2], ACT.Identity,
                                         bias=eps_t[:, 0:1]).then_inc(vee_done, 1)

                def weigh_pair(v):
                    act.wait_ge(d_done, v.n + 1)
                    nc.scalar.activation(w_all[:, bass.ds(v.n * 2, 2)], dot[:, v.slot, :], ACT.Identity,
                                         bias=br_col[:, 0:1])
                    nc.scalar.activation(nb[:, v.slot, :, D], dot[:, v.slot, :], ACT.Identity,
                                         bias=br_col[:, 0:1]).then_inc(w_done, 1)

                def weigh_tile(v):
                    act.wait_ge(de_done, v.n + 1)
                    at_least(act, hot_done, v.n - RING + 1)
                    nc.scalar.activation(we[:, v.slot:v.slot + 1], dote[:, v.slot:v.slot + 1], ACT.Identity,
                                         bias=br_col[:, 0:1])
                    nc.scalar.activation(nbe[:, v.slot, D:D + 1], dote[:, v.slot:v.slot + 1], ACT.Identity,
                                         bias=br_col[:, 0:1]).then_inc(we_done, 1)

                def store_normed(v):
                    act.wait_ge(w_done, v.n + 1)
                    act.dma_start(pair_rows(normed[0:EXT, :], v.n), nb[:, v.slot, :, :].rearrange("p s d -> p (s d)")
                                  ).then_inc(N_ST[v.slot], 16)

                def store_out(v):
                    act.wait_ge(on_done, v.n + 1)
                    if is_last(v):
                        act.dma_start(out_last, gout[0:LAST_P, v.slot, :]).then_inc(X_ST[v.slot], 16)
                    else:
                        act.dma_start(pair_rows(out_full, v.n), gout[:, v.slot, :]).then_inc(X_ST[v.slot], 16)

                steps(act, NP, [(high_pair(act, L), 0), (weigh_pair, 5), (weigh_tile, 6), (store_normed, 5),
                                (store_out, 5), (high_tile(act, L), 1), (eps_tile, 3), (eps_pair, 2)], peel=1)
                for s in range(RING):
                    act.wait_ge(X_ST[s], 16 * NP // RING)
                    act.wait_ge(N_ST[s], 16 * NP // RING)

            @block.vector
            def _(dve):
                v_ = nc.vector
                v_.memset(nb[:, :, :, :], 0.0)
                v_.memset(nbe[:, :, :], 0.0)
                v_.memset(pW[:, :], 0.0).then_inc(nb_zero, 1)
                dve.wait_ge(nb_zero, 1)

                def residual_pair(v):
                    n = total(L, v)
                    dve.wait_ge(X_LD[v.slot], 16 * (v.round + 1))
                    v_.tensor_tensor(xres[:, v.slot, :], xres[:, v.slot, :], bias[:, L, :], ALU.add).then_inc(xb_done, 1)
                    dve.wait_ge(o_done, n + 1)
                    dve.wait_ge(xb_done, v.n + 1)
                    v_.tensor_tensor(x2[:, v.slot, :], pO[v.two][:, :], xres[:, v.slot, :], ALU.add).then_inc(x2_done, 1)

                def statistics_pair(v):
                    dve.wait_ge(x2_done, v.n + 1)
                    for s in range(2):
                        last = v_.bn_stats(stats[:, v.slot, s, :], x2[:, v.slot, s * D:(s + 1) * D])
                    last.then_inc(st_done, 1)
                    alone(dve, st_done, v.n + 1)
                    for s in range(2):
                        last = v_.bn_aggr(mv[:, v.slot, s, :], stats[:, v.slot, s, :])
                    last.then_inc(mv_done, 1)

                def normalise_pair(v):
                    dve.wait_ge(r2_done, v.n + 1)
                    at_least(dve, N_ST[v.slot], 16 * v.round)
                    for s in range(2):
                        last = v_.tensor_scalar(nb[:, v.slot, s, 0:D], x2[:, v.slot, s * D:(s + 1) * D],
                                                mv[:, v.slot, s, 0:1], rs[:, v.slot, s:s + 1], ALU.subtract, ALU.mult)
                    last.then_inc(n_done, 1)
                    dve.wait_ge(n_done, v.n + 1)
                    at_least(dve, w_done, v.n - RING + 1)
                    for s in range(2):
                        last = v_.scalar_tensor_tensor(out=junk[:, s, :], in0=nb[:, v.slot, s, 0:D], scalar=1.0,
                                                       in1=wr_row[:, :], op0=ALU.mult, op1=ALU.mult,
                                                       accum_out=dot[:, v.slot, s:s + 1])
                    last.then_inc(d_done, 1)
                    at_least(dve, X_ST[v.slot], 16 * v.round)
                    v_.tensor_tensor(gout[:, v.slot, :].rearrange("p (s d) -> p s d", s=2),
                                     x2[:, v.slot, :].rearrange("p (s d) -> p s d", s=2), nb[:, v.slot, :, 0:D],
                                     ALU.add).then_inc(on_done, 1)

                def residual_tile(v):
                    n = total(L, v)
                    dve.wait_ge(XE_LD[v.slot], 16 * (v.round + 1))
                    v_.tensor_tensor(xe[:, v.slot, :], xe[:, v.slot, :], bias[:, L, 0:D], ALU.add).then_inc(xeb_done, 1)
                    dve.wait_ge(pz_done, n + 1)
                    dve.wait_ge(xeb_done, v.n + 1)
                    v_.scalar_tensor_tensor(out=x2e[:, v.slot, :], in0=pZ[:, 0:D], scalar=inv_dst[:, bass.ds(v.n, 1)],
                                            in1=xe[:, v.slot, :], op0=ALU.mult, op1=ALU.add).then_inc(x2e_done, 1)

                def statistics_tile(v):
                    dve.wait_ge(x2e_done, v.n + 1)
                    v_.bn_stats(stats_e[:, v.slot, :], x2e[:, v.slot, :]).then_inc(ste_done, 1)
                    alone(dve, ste_done, v.n + 1)
                    v_.bn_aggr(mv_e[:, v.slot, :], stats_e[:, v.slot, :]).then_inc(mve_done, 1)

                def normalise_tile(v):
                    dve.wait_ge(re_done, v.n + 1)
                    at_least(dve, NE_ST[v.slot], 16 * v.round)
                    v_.tensor_scalar(nbe[:, v.slot, 0:D], x2e[:, v.slot, :], mv_e[:, v.slot, 0:1],
                                     rs_e[:, v.slot:v.slot + 1], ALU.subtract, ALU.mult).then_inc(ne_done, 1)
                    dve.wait_ge(ne_done, v.n + 1)
                    at_least(dve, we_done, v.n - RING + 1)
                    v_.scalar_tensor_tensor(out=junk[:, 2, :], in0=nbe[:, v.slot, 0:D], scalar=1.0, in1=wr_row[:, :],
                                            op0=ALU.mult, op1=ALU.mult, accum_out=dote[:, v.slot:v.slot + 1]
                                            ).then_inc(de_done, 1)
                    at_least(dve, OE_ST[v.slot], 16 * v.round)
                    v_.tensor_tensor(oute[:, v.slot, :], x2e[:, v.slot, :], nbe[:, v.slot, 0:D],
                                     ALU.add).then_inc(oe_done, 1)

                def spread_w(v):
                    dve.wait_ge(we_done, v.n + 1)
                    at_least(dve, w_tally, v.n - 1)
                    v_.tensor_scalar(hot_lo_f[:, v.two, :], iota_f[:, 0:P], lo_f[:, bass.ds(v.n, 1)], None, ALU.is_equal)
                    v_.tensor_scalar(hot_w[:, v.two, :], iota_f[:, :], hi_emit[:, bass.ds(v.n, 1)],
                                     we[:, v.slot:v.slot + 1], ALU.is_equal, ALU.mult).then_inc(hot_done, 1)

                steps(dve, NP, [(add_own(dve, L), 1), (carry(dve, L), 0), (low_tile(dve, L), 2), (low_pair(dve, L), 0),
                                (normalise_pair, 4), (normalise_tile, 5), (residual_tile, 3), (residual_pair, 2),
                                (statistics_tile, 3), (statistics_pair, 2), (spread_w, 7)])

        rings.close()
        with phase() as block:
            @block.gpsimd
            def _(pool):
                nc.clear_and_free_semaphores(semaphores)

        PASSED[0] = sem("passed_on")

        w_sel = sb("w_sel", [P, COLS])
        w_flag = sb("w_flag", [P, COLS], I32)
        least = sb("least", [P, COLS])
        node_f = sb("node_f", [P, COLS])
        bits = sb("bits", [P, 32], I32)
        shifts = sb("shifts", [P, 32], I32)
        heavier = sb("heavier", [P, COLS])
        equal = sb("equal", [P, COLS])
        pair_eq = sb("pair_eq", [P, NP])
        pair_tot = sb("pair_tot", [P, NP])
        pair_run = sb("pair_run", [P, NP])
        pair_one = sb("pair_one", [P, NP])
        rank = sb("rank", [P, NP, 2])
        need = sb("need", [P, 1])
        cnt = sb("cnt", [P, 1])
        best = sb("best", [P, 1], I32)
        cand = sb("cand", [P, 1], I32)
        flip = sb("flip", [P, 1], I32)
        thresh = sb("thresh", [P, 1], I32)
        enough = sb("enough", [P, 1], I32)
        keys = sb("keys", [P, COLS])
        most = sb("most", [P, 1])
        turns_i = sb("turns_i", [P, 1], I32)
        ext_t = sb("ext_t", [P, 2, RING, D])
        idx_o = sb("idx_o", [P, 2 * RING], I32)
        f1_in = sb("f1_in", [P, KC, H])
        f1_hi = sb("f1_hi", [P, KC, H], F32R)
        f1_lo = sb("f1_lo", [P, KC, H], F32R)
        f2_in = sb("f2_in", [P, FH, D])
        f2_hi = sb("f2_hi", [P, FH, D], F32R)
        f2_lo = sb("f2_lo", [P, FH, D], F32R)
        fb1_col = sb("fb1_col", [P, FH])
        fb2_row = sb("fb2_row", [P, D])
        top8 = sb("top8", [P, 8])
        none8 = sb("none8", [P, 8])
        list_i = sb("list_i", [P, 8], I32)
        ask_i = sb("ask_i", [P, 2, RING], I32)
        put_i = sb("put_i", [P, 2, RING], I32)
        at_row = sb("at_row", [P, 2, RING], I32)
        nx = sb("nx", [P, 2, RING, DW])
        wq = sb("wq", [P, 2, RING])
        fx_hi = sb("fx_hi", [P, 2, KC, 4 * P], F32R)
        fx_lo = sb("fx_lo", [P, 2, KC, 4 * P], F32R)
        hid = sb("hid", [P, 2, 4 * P])
        hid_hi = sb("hid_hi", [P, 4, 4 * P], F32R)
        hid_lo = sb("hid_lo", [P, 4, 4 * P], F32R)
        y_sum = sb("y_sum", [P, 2, D])
        y = sb("y", [P, 2, RING, D])

        OX_LD, OI, OX_ST = sems("ox_ld"), sem("ox_i"), sems("ox_st")
        f_got, f_split, c_step, c_cnt, c_tot, c_bits, c_ready = (sem(k) for k in (
            "f_got", "f_split", "c_step", "c_cnt", "c_tot", "c_bits", "c_ready"))
        ext_quads = ext_out.rearrange("(g r p) d -> g p r d", r=RING, p=P)
        QUADS = ET // RING

        with phase() as block:
            @block.sync
            def _(sp):
                sp.dma_start(f1_in[:, :, :], w1.rearrange("(k p) n -> p k n", p=P)).then_inc(f_got, 16)
                sp.dma_start(f2_in[:, :, :], w2.rearrange("(k p) n -> p k n", p=P)).then_inc(f_got, 16)
                with nc.allow_non_contiguous_dma(reason="a bias to columns"):
                    sp.dma_start(fb1_col[:, :], fb1.rearrange("(k p) -> p k", p=P)).then_inc(f_got, 16)
                sp.dma_start(fb2_row[:, :], fb2.rearrange("(o n) -> o n", o=1).to_broadcast([P, D])).then_inc(f_got, 16)
                for q in range(2):
                    sp.dma_start(ext_t[:, q, :, :], ext_quads[q]).then_inc(OX_LD[q], 16)
                with sp.Fori(1, QUADS // 2) as two:
                    for q in range(2):
                        sp.wait_ge(OX_ST[q], two * 16 * RING)
                        sp.dma_start(ext_t[:, q, :, :], ext_quads[two * 2 + q]).then_inc(OX_LD[q], 16)
                if QUADS % 2:
                    sp.wait_ge(OX_ST[0], QUADS // 2 * 16 * RING)
                    sp.dma_start(ext_t[:, 0, :, :], ext_quads[QUADS - 1]).then_inc(OX_LD[0], 16)

            @block.gpsimd
            def _(pool):
                g = nc.gpsimd
                g.memset(bits[:, :], 1).then_inc(c_bits, 1)
                g.iota(shifts[:, :], pattern=[[-1, 32]], base=31, channel_multiplier=0).then_inc(c_bits, 1)

                def put_quad(q, uses, n):
                    pool.wait_ge(OX_LD[q], (uses + 1) * 16)
                    if not isinstance(uses, int) or uses:
                        pool.wait_ge(OX_ST[q], uses * 16 * RING)
                    for r in range(RING):
                        slot = q * RING + r
                        g.tensor_copy(idx_o[:, slot:slot + 1], emit_i[:, bass.ds(n * RING + r, 1)]).then_inc(OI, 1)
                    alone(pool, OI, (n + 1) * RING)
                    for r in range(RING):
                        slot = q * RING + r
                        g.indirect_dma_start(out=out, out_offset=bass.IndirectOffsetOnAxis(ap=idx_o[:, slot:slot + 1], axis=0),
                                             in_=ext_t[:, q, r, :], in_offset=None, bounds_check=N - 1,
                                             oob_is_err=False).then_inc(OX_ST[q], 16)

                for q in range(2):
                    put_quad(q, 0, q)
                with pool.Fori(1, QUADS // 2) as two:
                    for q in range(2):
                        put_quad(q, two, two * 2 + q)
                if QUADS % 2:
                    put_quad(0, QUADS // 2, QUADS - 1)
                for q in range(2):
                    pool.wait_ge(OX_ST[q], (QUADS + 1 - q) // 2 * 16 * RING)

            @block.scalar
            def _(act):
                act.wait_ge(f_got, 16 * 4)
                nc.scalar.activation(f1_hi[:, :, :].rearrange("p k n -> p (k n)"),
                                     f1_in[:, :, :].rearrange("p k n -> p (k n)"), ACT.Copy).then_inc(f_split, 1)
                nc.scalar.activation(f2_hi[:, :, :].rearrange("p k n -> p (k n)"),
                                     f2_in[:, :, :].rearrange("p k n -> p (k n)"), ACT.Copy).then_inc(f_split, 1)

            @block.tensor
            def _(pe):
                t_ = nc.tensor
                with pe.Fori(0, 32) as b:
                    pe.wait_ge(c_cnt, b + 1)
                    t_.matmul(pS[:, 0:1], ones[:, :], cnt[:, 0:1], start=True, stop=True).then_inc(c_tot, 1)
                pe.wait_ge(c_cnt, 33)
                t_.matmul(pS[:, 0:1], ones[:, :], cnt[:, 0:1], start=True, stop=True)
                t_.matmul(pE[:, 0:NP], below[:, :], pair_eq[:, :], start=True, stop=True)
                t_.matmul(pZ[:, 0:NP], ones[:, :], pair_eq[:, :], start=True, stop=True).then_inc(c_tot, 1)
                pe.wait_ge(c_cnt, 34)
                t_.transpose(pT[0][0:1, 0:P], cnt[:, 0:1], ident[:, :]).then_inc(c_tot, 1)

            @block.vector
            def _(dve):
                v_ = nc.vector
                count = [0]

                def link(ins):
                    count[0] += 1
                    ins.then_inc(c_step, 1)
                    dve.wait_ge(c_step, count[0])

                dve.wait_ge(c_bits, 2)
                link(v_.tensor_tensor(bits[:, :], bits[:, :], shifts[:, :], ALU.logical_shift_left))
                v_.memset(best[:, :], 0)
                v_.memset(least[:, :], -3.0e38)
                v_.memset(pair_one[:, :], 1.0)
                v_.tensor_copy(node_f[:, :], node_i[:, :])
                v_.tensor_copy(w_sel[:, :], w_all[:, :])
                link(v_.tensor_scalar(w_flag[:, :], root[:, :], 1.5, None, ALU.is_ge))
                link(v_.copy_predicated(w_sel[:, :], w_flag[:, :], pW[:, 0:COLS]))
                link(v_.tensor_scalar(w_flag[:, :], node_f[:, :], float(N), None, ALU.is_gt))
                link(v_.copy_predicated(w_sel[:, :], w_flag[:, :], least[:, :]))

                def as_float():
                    yield v_.tensor_scalar(flip[:, :], cand[:, :], 31, -1, ALU.arith_shift_right, ALU.bitwise_xor)
                    yield v_.tensor_scalar(flip[:, :], flip[:, :], -2147483648, None, ALU.bitwise_or)
                    yield v_.tensor_tensor(thresh[:, :], cand[:, :], flip[:, :], ALU.bitwise_xor)

                SEARCH = 5
                with dve.Fori(0, 32) as b:
                    before = b * SEARCH + count[0]
                    v_.tensor_tensor(cand[:, :], best[:, :], bits[:, bass.ds(b, 1)], ALU.bitwise_or).then_inc(c_step, 1)
                    alone(dve, c_step, before + 1)
                    for k, ins in enumerate(as_float()):
                        ins.then_inc(c_step, 1)
                        alone(dve, c_step, before + 2 + k)
                    v_.tensor_scalar(heavier[:, :], w_sel[:, :], thresh[:, 0:1].bitcast(F32), 0.0, ALU.is_ge, ALU.add,
                                     accum_out=cnt[:, 0:1]).then_inc(c_cnt, 1)
                    alone(dve, c_tot, b + 1)
                    v_.tensor_scalar(enough[:, :], pS[:, 0:1], float(K_SEL), None, ALU.is_ge).then_inc(c_ready, 1)
                    alone(dve, c_ready, b + 1)
                    v_.copy_predicated(best[:, :], enough[:, :], cand[:, :]).then_inc(c_step, 1)
                    alone(dve, c_step, before + SEARCH)
                count[0] += 32 * SEARCH
                link(v_.tensor_copy(cand[:, :], best[:, :]))
                for ins in as_float():
                    link(ins)
                v_.tensor_scalar(heavier[:, :], w_sel[:, :], thresh[:, 0:1].bitcast(F32), 0.0, ALU.is_gt, ALU.add,
                                 accum_out=cnt[:, 0:1])
                link(v_.tensor_scalar(equal[:, :], w_sel[:, :], thresh[:, 0:1].bitcast(F32), None, ALU.is_equal))
                eq3 = equal[:, :].rearrange("p (j s) -> p j s", s=2)
                v_.tensor_tensor(pair_eq[:, :], eq3[:, :, 0], eq3[:, :, 1], ALU.add).then_inc(c_cnt, 1)
                dve.wait_ge(c_tot, 33)
                v_.tensor_scalar(need[:, :], pS[:, 0:1], -1.0, float(K_SEL), ALU.mult, ALU.add)
                link(v_.tensor_copy(pair_tot[:, :], pZ[:, 0:NP]))
                link(v_.tensor_tensor_scan(pair_run[:, :], pair_one[:, :], pair_tot[:, :], 0.0, ALU.mult, ALU.add))
                link(v_.tensor_tensor(pair_run[:, :], pair_run[:, :], pair_tot[:, :], ALU.subtract))
                link(v_.tensor_tensor(rank[:, :, 0], pair_run[:, :], pE[:, 0:NP], ALU.add))
                link(v_.tensor_tensor(rank[:, :, 1], rank[:, :, 0], eq3[:, :, 0], ALU.add))
                rank2 = rank[:, :, :].rearrange("p j s -> p (j s)")
                link(v_.tensor_scalar(rank2, rank2, need[:, 0:1], None, ALU.is_lt))
                link(v_.tensor_tensor(equal[:, :], equal[:, :], rank2, ALU.mult))
                link(v_.tensor_tensor(heavier[:, :], heavier[:, :], equal[:, :], ALU.add))
                link(v_.tensor_tensor(keys[:, :], heavier[:, :], node_f[:, :], ALU.mult))
                v_.tensor_scalar(equal[:, :], heavier[:, :], 0.0, 0.0, ALU.add, ALU.add,
                                 accum_out=cnt[:, 0:1]).then_inc(c_cnt, 1)
                dve.wait_ge(c_tot, 34)
                link(v_.reduce_max(most[0:1, :], pT[0][0:1, 0:P], axis=AX_X))
                link(v_.tensor_scalar(turns_i[0:1, :], most[0:1, :], -1.0, None, ALU.add))
                link(v_.tensor_scalar(turns_i[0:1, :], turns_i[0:1, :], 3, None, ALU.logical_shift_right))
                v_.memset(nx[:, :, :, :], 0.0)
                v_.memset(at_row[:, :, :], 0)
                dve.wait_ge(f_split, 2)
                v_.tensor_tensor(f1_lo[:, :, :], f1_in[:, :, :], f1_hi[:, :, :].bitcast(F32), ALU.subtract)
                v_.tensor_tensor(f2_lo[:, :, :], f2_in[:, :, :], f2_hi[:, :, :].bitcast(F32), ALU.subtract)

        QR = 4 * P
        NX_LD, RO_LD, Y_ST = [sem("nx_ld0"), sem("nx_ld1")], [sem("ro_ld0"), sem("ro_ld1")], [sem("y_st0"), sem("y_st1")]
        (l_step, l_ready, l_taken, q_idx, q_put, x_turned, x_hi, x_lo, l1_done, act_done, hh_done, hl_done, l2_done, y_add,
         y_done) = (sem(k) for k in ("l_step", "l_ready", "l_taken", "q_idx", "q_put", "x_turned", "x_hi", "x_lo",
                                     "l1_done", "act_done", "hh_done", "hl_done", "l2_done", "y_add", "y_done"))
        pA = [pS, pE]
        pY = [[pO[0], pO[1]], [pZ, pW]]
        CH = 2 * FH
        Y_FREE = [sem("y_free0"), sem("y_free1")]
        MIN_TURNS = -(-K_SEL // (P * 8))
        MAX_TURNS = -(-COLS // 8)

        def turns(eng, body):
            n = eng.value_load(turns_i[0:1, 0:1], min_val=MIN_TURNS - 1, max_val=MAX_TURNS - 1)
            body(0)
            with eng.Fori(0, n) as t:
                body(t + 1)
            return n

        with phase() as block:
            @block.gpsimd
            def _(pool):
                g = nc.gpsimd

                def fetch(t, k):
                    if not (isinstance(t, int) and t == 0):
                        alone(pool, Y_ST[k], (t - 1) * 16 * RING)
                        pool.sem_inc(Y_FREE[k], 1)
                        g.tensor_copy(put_i[:, k, :], ask_i[:, k, :]).then_inc(q_put, 1)
                        alone(pool, q_put, (t - 1) * 2 + k + 1)
                    alone(pool, l_ready, t + 1)
                    g.tensor_copy(ask_i[:, k, :], list_i[:, k * RING:(k + 1) * RING]).then_inc(q_idx, 1)
                    alone(pool, q_idx, t * 2 + k + 1)
                    if k:
                        pool.sem_inc(l_taken, 1)
                    for r in range(RING):
                        g.indirect_dma_start(out=at_row[:, k, r:r + 1], out_offset=None, in_=row_of,
                                             in_offset=bass.IndirectOffsetOnAxis(ap=ask_i[:, k, r:r + 1], axis=0),
                                             bounds_check=EXT - 1, oob_is_err=False).then_inc(RO_LD[k], 16)
                    alone(pool, RO_LD[k], (t + 1) * 16 * RING)
                    if not (isinstance(t, int) and t == 0):
                        alone(pool, x_lo, t * 2 + k - 1)
                    for r in range(RING):
                        g.indirect_dma_start(out=nx[:, k, r, :], out_offset=None, in_=normed,
                                             in_offset=bass.IndirectOffsetOnAxis(ap=at_row[:, k, r:r + 1], axis=0)
                                             ).then_inc(NX_LD[k], 16)

                def put(t, k):
                    for r in range(RING):
                        alone(pool, y_done, (t * 2 + k) * RING + r + 1)
                        g.indirect_dma_start(out=out, out_offset=bass.IndirectOffsetOnAxis(ap=put_i[:, k, r:r + 1], axis=0),
                                             in_=y[:, k, r, :], in_offset=None, bounds_check=N - 1, oob_is_err=False,
                                             compute_op=ALU.add).then_inc(Y_ST[k], 16)

                for k in range(2):
                    fetch(0, k)

                def turn_body(t):
                    for k in range(2):
                        fetch(t + 1, k)
                        put(t, k)

                last_turn = turns(pool, turn_body)
                for k in range(2):
                    pool.wait_ge(Y_ST[k], (last_turn + 1) * (16 * RING))
                    pool.wait_ge(NX_LD[k], (last_turn + 2) * (16 * RING))

            @block.tensor
            def _(pe):
                t_ = nc.tensor

                def turn_rows(t, k):
                    q = t * 2 + k
                    pe.wait_ge(NX_LD[k], (t + 1) * 16 * RING)
                    at_least(pe, x_lo, q)
                    for c in range(KC):
                        for r in range(RING):
                            last = t_.transpose(pT[c][:, r * P:(r + 1) * P], nx[:, k, r, c * P:(c + 1) * P], ident[:, :])
                    last.then_inc(x_turned, 1)

                def hidden(t, k, f):
                    c = t * CH + k * FH + f
                    if f == 0:
                        pe.wait_ge(x_lo, t * 2 + k + 1)
                    at_least(pe, act_done, c - 1)
                    u = slice(f * P, (f + 1) * P)
                    for i in range(KC):
                        t_.matmul(pA[f % 2][:, :], f1_hi[:, i, u], fx_hi[:, k, i, :], start=(i == 0), stop=False)
                        t_.matmul(pA[f % 2][:, :], f1_lo[:, i, u], fx_hi[:, k, i, :], start=False, stop=False)
                        last = t_.matmul(pA[f % 2][:, :], f1_hi[:, i, u], fx_lo[:, k, i, :], start=False, stop=(i == KC - 1))
                    last.then_inc(l1_done, 1)

                def output(t, k, f):
                    c = t * CH + k * FH + f
                    pe.wait_ge(hl_done, c + 1)
                    if f == 0:
                        at_least(pe, y_add, (t * 2 + k - 1) * RING)
                    for r in range(RING):
                        bank = pY[k][r // 2][:, (r % 2) * D:(r % 2 + 1) * D]
                        rr = slice(r * P, (r + 1) * P)
                        s = f % 4
                        last_f = f == FH - 1
                        t_.matmul(bank, hid_hi[:, s, rr], f2_hi[:, f, :], start=(f == 0 and r % 2 == 0), stop=False,
                                  skip_group_check=True)
                        t_.matmul(bank, hid_lo[:, s, rr], f2_hi[:, f, :], start=False, stop=False, skip_group_check=True)
                        last = t_.matmul(bank, hid_hi[:, s, rr], f2_lo[:, f, :], start=False, stop=last_f,
                                         skip_group_check=True)
                    last.then_inc(l2_done, 1)

                turn_rows(0, 0)

                def turn_body(t):
                    for k in range(2):
                        for f in range(FH):
                            hidden(t, k, f)
                            if f == FH // 2:
                                turn_rows(t + k, 1 - k)
                            if f >= 2:
                                output(t, k, f - 2)
                            elif k:
                                output(t, 0, FH - 2 + f)
                            elif not isinstance(t, int):
                                output(t - 1, 1, FH - 2 + f)

                last_turn = turns(pe, turn_body)
                for f in range(FH - 2, FH):
                    output(last_turn, 1, f)

            @block.scalar
            def _(act):
                nc.scalar.preload_act_table(ACT.Gelu_apprx_tanh)

                def high_rows(t, k):
                    act.wait_ge(x_turned, t * 2 + k + 1)
                    for c in range(KC):
                        last = nc.scalar.activation(fx_hi[:, k, c, :], pT[c][:, :], ACT.Copy)
                    last.then_inc(x_hi, 1)

                def gelu(t, k, f):
                    c = t * CH + k * FH + f
                    act.wait_ge(l1_done, c + 1)
                    at_least(act, hl_done, c - 1)
                    nc.scalar.activation(hid[:, f % 2, :], pA[f % 2][:, :], ACT.Gelu_apprx_tanh,
                                         bias=fb1_col[:, f:f + 1]).then_inc(act_done, 1)
                    act.wait_ge(act_done, c + 1)
                    at_least(act, l2_done, c - 3)
                    nc.scalar.activation(hid_hi[:, f % 4, :], hid[:, f % 2, :], ACT.Copy).then_inc(hh_done, 1)

                high_rows(0, 0)

                def turn_body(t):
                    for k in range(2):
                        for f in range(FH):
                            gelu(t, k, f)
                            if f == FH // 2:
                                high_rows(t + k, 1 - k)

                turns(act, turn_body)

            @block.vector
            def _(dve):
                v_ = nc.vector

                def make_list(t):
                    alone(dve, l_taken, t)
                    v_.max(top8[:, :], keys[:, :]).then_inc(l_step, 1)
                    alone(dve, l_step, t * 3 + 1)
                    v_.match_replace(keys[:, :], top8[:, :], keys[:, :], 0.0)
                    v_.tensor_scalar(none8[:, :], top8[:, :], 0.0, float(FAR), ALU.is_equal, ALU.mult).then_inc(l_step, 1)
                    alone(dve, l_step, t * 3 + 2)
                    v_.scalar_tensor_tensor(out=list_i[:, :], in0=top8[:, :], scalar=-1.0, in1=none8[:, :],
                                            op0=ALU.add, op1=ALU.add).then_inc(l_step, 1)
                    alone(dve, l_step, t * 3 + 3)
                    dve.sem_inc(l_ready, 1)

                def low_rows(t, k):
                    q = t * 2 + k
                    dve.wait_ge(x_hi, q + 1)
                    for c in range(KC):
                        v_.tensor_tensor(fx_lo[:, k, c, :], pT[c][:, :], fx_hi[:, k, c, :].bitcast(F32), ALU.subtract)
                    at_least(dve, y_done, (q - 1) * RING)
                    v_.tensor_copy(wq[:, k, :], nx[:, k, :, D]).then_inc(x_lo, 1)

                def low_hidden(t, k, f):
                    c = t * CH + k * FH + f
                    dve.wait_ge(hh_done, c + 1)
                    v_.tensor_tensor(hid_lo[:, f % 4, :], hid[:, f % 2, :], hid_hi[:, f % 4, :].bitcast(F32),
                                     ALU.subtract).then_inc(hl_done, 1)

                def weigh(t, k):
                    q = t * 2 + k
                    dve.wait_ge(l2_done, (q + 1) * FH)
                    dve.wait_ge(Y_FREE[k], t + 1)
                    for r in range(RING):
                        bank = pY[k][r // 2][:, (r % 2) * D:(r % 2 + 1) * D]
                        v_.tensor_tensor(y_sum[:, r % 2, :], bank, fb2_row[:, :], ALU.add).then_inc(y_add, 1)
                        alone(dve, y_add, q * RING + r + 1)
                        v_.tensor_scalar(y[:, k, r, :], y_sum[:, r % 2, :], wq[:, k, r:r + 1], None,
                                         ALU.mult).then_inc(y_done, 1)

                make_list(0)
                make_list(1)
                low_rows(0, 0)

                def turn_body(t):
                    for k in range(2):
                        for f in range(FH):
                            low_hidden(t, k, f)
                            if f == 2:
                                if k:
                                    weigh(t, 0)
                                elif not isinstance(t, int):
                                    weigh(t - 1, 1)
                            if f == FH // 2:
                                low_rows(t + k, 1 - k)
                    make_list(t + 2)

                last_turn = turns(dve, turn_body)
                weigh(last_turn, 1)


_INS = ['x', 'src', 'dst', 'L0_gnn_W1', 'L0_gnn_b1', 'L0_gnn_W2', 'L0_gnn_b2', 'L0_gnn_W3', 'L0_gnn_b3',
        'L0_ffn_wr', 'L0_ffn_br', 'L0_ffn_w1', 'L0_ffn_b1', 'L0_ffn_w2', 'L0_ffn_b2']


def kernel(**inputs):
    import numpy as _np
    import concourse.bacc as _bacc
    from concourse import mybir as _mybir
    from concourse.bass_utils import run_bass_kernel_spmd as _run

    nc = _bacc.Bacc("TRN2", target_bir_lowering=False, num_devices=1)
    arrays, args = {}, []
    for name in _INS:
        a = _np.ascontiguousarray(inputs[name])
        arrays[f"in_{name}_dram"] = a
        args.append(nc.dram_tensor(f"in_{name}_dram", a.shape, _mybir.dt.from_np(a.dtype), kind="ExternalInput").ap())
    args.append(nc.dram_tensor("out_0_dram", inputs['x'].shape, _mybir.dt.float32, kind="ExternalOutput").ap())
    gnn_ffn(nc, *args)
    r = _run(nc, [arrays], core_ids=[0])
    return r.results[0]["out_0_dram"]
```

```python
from contextlib import ExitStack

import concourse.bass as bass
from concourse import mybir

ALU = mybir.AluOpType
ACT = mybir.ActivationFunctionType
AX_X = mybir.AxisListType.X
F32 = mybir.dt.float32
F32R = mybir.dt.float32r
F16 = mybir.dt.float16
I32 = mybir.dt.int32
RMAX = bass.bass_isa.ReduceOp.max

P = 128
RING = 4
WARM = 12
EPS = 1e-5
FAR = 1 << 20


class At:

    def __init__(self, group, off):
        self.n = group * RING + off
        self.slot = off % RING
        self.two = off % 2
        self.round = group + off // RING


def steps(eng, count, stages, peel=0):
    stages = [s if len(s) == 3 else (*s, None) for s in stages]

    def one(group, off, static):
        for stage, lag, only in stages:
            if only is not None and (off - lag) % RING != only:
                continue
            if static and not 0 <= off - lag < count:
                continue
            stage(At(group, off - lag))

    for v in range(WARM):
        one(0, v, True)
    with eng.Fori(WARM // RING, count // RING - peel) as group:
        for off in range(RING):
            one(group, off, False)
    lags = max(lag for _, lag, _ in stages)
    for v in range(count - RING * peel, count + lags):
        one(0, v, True)


def at_least(eng, sem, value):
    if not isinstance(value, int) or value > 0:
        eng.wait_ge(sem, value)


def alone(eng, sem, value):
    if not isinstance(value, int):
        eng.wait_ge(sem, value)
        eng.sem_inc(PASSED[0], 1)
    elif value > 0:
        eng.wait_ge(sem, value)


PASSED = [None]


def gnn_ffn(nc, x, src, dst, W1, b1, W2, b2, W3, b3, wr, br, w1, fb1, w2, fb2, out):
    N, D = x.shape
    E = src.shape[0]
    H = w1.shape[1]
    K_SEL = N // 2 - 1
    ET = -(-E // P)
    NP = -(-N // (2 * P))
    EXT = NP * 2 * P
    ROWS = EXT + ET * P
    COLS = 2 * NP
    HC = COLS // 4
    LAST_P = (N - (NP - 1) * 2 * P) // 2
    TC = ET // 2
    LAST_E = E - (ET - 1) * P
    KC = D // P
    FH = H // P
    DW = D + 8
    PAD_DST = 70000
    assert D == 256 and ET == NP and ET % RING == 0 and TC % 2 == 0 and COLS <= 512 and PAD_DST > ROWS - ET * P

    with ExitStack() as ctx:
        def sb(name, shape, dt=F32):
            return ctx.enter_context(nc.sbuf_tensor(name, shape, dt))

        def pb(name, shape=(P, 512), dt=F32):
            return ctx.enter_context(nc.psum_tensor(name, list(shape), dt))

        semaphores = []

        def sem(name):
            semaphores.append(nc.alloc_semaphore(name=name))
            return semaphores[-1]

        def sems(name):
            return [sem(f"{name}{i}") for i in range(RING)]

        def dram(name, shape, dt=F32):
            return nc.dram_tensor(name, shape, dt, kind="Internal").ap()

        rows = [dram(f"rows{l}", (ROWS if l else EXT, D)) for l in range(3)]
        normed = dram("normed", (ROWS, DW))
        ext_out = dram("ext_out", (ET * P, D))
        same_dram = dram("same_dram", (ET, P, P))
        turned_dst = dram("turned_dst", (ET, P))
        inv_root = dram("inv_root", (COLS * P, 1))
        row_of = dram("row_of", (EXT, 1), I32)
        edge_src2 = dram("edge_src", (E, 1), I32)
        edge_dst2 = dram("edge_dst", (E, 1), I32)
        edge_src, edge_dst = (a.rearrange("e o -> (e o)") for a in (edge_src2, edge_dst2))

        ident = sb("ident", [P, P])
        turn = sb("turn", [P, P])
        ones = sb("ones", [P, P])
        below = sb("below", [P, P])
        iota_p16 = sb("iota_p16", [P, P], F16)
        iota_c16 = sb("iota_c16", [P, COLS], F16)
        iota_i = sb("iota_i", [P, COLS], I32)
        node_i = sb("node_i", [P, COLS], I32)
        ext_id = sb("ext_id", [P, ET], I32)
        lin_id = sb("lin_id", [P, COLS], I32)
        eps_t = sb("eps_t", [P, 1])
        half = sb("half", [P, COLS])
        iota_f = sb("iota_f", [P, COLS])

        nat_i = sb("nat_i", [P, 3, 2, P], I32)
        prev_i = sb("prev_i", [P, 2], I32)
        nat_f = sb("nat_f", [P, 4, 2, P])
        nat_next = sb("nat_next", [P, 2, P])
        prev_f = sb("prev_f", [P, 2])
        turned = sb("turned", [P, 4, ET])
        src_i = sb("src_i", [P, ET], I32)
        emit_i = sb("emit_i", [P, ET], I32)
        dst_i = sb("dst_i", [P, ET], I32)
        dst_safe = sb("dst_safe", [P, ET], I32)
        lo_i = sb("lo_i", [P, ET], I32)
        hi_i = sb("hi_i", [P, ET], I32)
        odd_i = sb("odd_i", [P, ET], I32)
        lo_f = sb("lo_f", [P, ET])
        hi_f = sb("hi_f", [P, ET])
        table_i = sb("table_i", [P, ET], I32)
        table_f = sb("table_f", [P, ET])
        hot_lo = sb("hot_lo", [P, RING, P], F16)
        hot_hi = sb("hot_hi", [P, RING, COLS], F16)
        back = sb("back", [P, 2, P])
        root = sb("root", [P, COLS])
        inv = sb("inv", [P, COLS])
        inv_t = sb("inv_t", [P, 4, P])
        inv_dst = sb("inv_dst", [P, ET])

        w_all = sb("w_all", [P, COLS])

        rings = ctx.enter_context(ExitStack())

        def ring(name, shape, dt=F32):
            return rings.enter_context(nc.sbuf_tensor(name, shape, dt))

        xin = ring("xin", [P, RING, 2 * D])
        gout = ring("gout", [P, RING, 2 * D])
        stats = ring("stats", [P, RING, 2, 6])
        mv = ring("mv", [P, RING, 2, 2])
        veps = ring("veps", [P, RING, 2])
        rstd = ring("rstd", [P, RING, 2])
        rs = ring("rs", [P, RING, 2])
        dst_row = ring("dst_row", [P, RING * P])
        same_out = ring("same_out", [P, RING, P])
        idx_a = ring("idx_a", [P, RING], I32)
        got_a = ring("got_a", [P, RING])

        w_in = ring("w_in", [P, KC, D])
        w_hi = ring("w_hi", [P, 3, KC, D], F32R)
        w_lo = ring("w_lo", [P, 3, KC, D], F32R)
        bias = ring("bias", [P, 3, 2 * D])
        wr_row = ring("wr_row", [P, D])
        br_col = ring("br_col", [P, 1])
        xt_hi = ring("xt_hi", [P, 2, 2, KC, P], F32R)
        xt_lo = ring("xt_lo", [P, 2, 2, KC, P], F32R)
        zb = ring("zb", [P, 2, 2 * D])
        same_t = ring("same_t", [P, RING, P])
        idx_m = ring("idx_m", [P, RING], I32)
        idx_s = ring("idx_s", [P, RING], I32)
        idx_r = ring("idx_r", [P, RING], I32)
        val_r = ring("val_r", [P, RING], I32)
        got_r = ring("got_r", [P, RING], I32)
        src_row = ring("src_row", [P, ET], I32)
        msg = ring("msg", [P, RING, D])
        own = ring("own", [P, RING, D])
        tot = ring("tot", [P, 2, D])
        et_hi = ring("et_hi", [P, 2, KC, P], F32R)
        et_lo = ring("et_lo", [P, 2, KC, P], F32R)
        ez = ring("ez", [P, 2, D])
        eh = ring("eh", [P, 2, D])
        eo = ring("eo", [P, RING, D])


        xres = ring("xres", [P, RING, 2 * D])
        xe = ring("xe", [P, RING, D])
        x2 = ring("x2", [P, RING, 3, D])
        stats3 = ring("stats3", [P, RING, 3, 6])
        mv3 = ring("mv3", [P, RING, 3, 2])
        veps3 = ring("veps3", [P, RING, 3])
        rs3 = ring("rs3", [P, RING, 3])
        one_rs3 = ring("one_rs3", [P, RING, 3])
        shift3 = ring("shift3", [P, RING, 3])
        nb = ring("nb", [P, RING, 3, DW])
        x2n = ring("x2n", [P, RING, 3, D])
        dot3 = ring("dot3", [P, RING, 3])
        junk = ring("junk", [P, 3, D])
        one_r = ring("one_r", [P, P], F32R)
        bias_hi = ring("bias_hi", [P, 2 * D], F32R)
        bias_mix = ring("bias_mix", [P, 2 * D], F32R)
        emit_f = ring("emit_f", [P, ET])
        hi_emit = ring("hi_emit", [P, ET])
        hot_lo_f = ring("hot_lo_f", [P, 2, P])
        hot_w = ring("hot_w", [P, 2, COLS])

        pT = [pb("pT0"), pb("pT1")]
        pO = [pb("pO0"), pb("pO1")]
        pS, pE, pZ, pW = pb("pS"), pb("pE"), pb("pZ"), pb("pW")

        PASSED[0] = sem("passed")
        s_const = sem("s_const")
        s_pad = sem("s_pad")
        s_nat = sem("s_nat")
        s_nat2 = sem("s_nat2")
        s_pro = sem("s_pro")
        s_flip = sem("s_flip")
        s_flipped = sem("s_flipped")
        s_back = sem("s_back")
        s_turned_st = sem("s_turned_st")
        s_hot = sem("s_hot")
        s_count = sem("s_count")
        s_root = sem("s_root")
        s_inv_t = sem("s_inv_t")
        s_inv_st = sem("s_inv_st")
        s_lin = sem("s_lin")


        def phase():
            return nc.Block()

        EC = next(c for c in range(-(-E // P), E + 1) if E % c == 0)
        EP = E // EC
        CHUNK = next(c for c in range(700, 0, -1) if E % c == 0)
        sort_mem = ctx.enter_context(ExitStack())

        def tmp(name, shape, dt=F32):
            return sort_mem.enter_context(nc.sbuf_tensor(name, shape, dt))

        e_src, e_dst, e_next = tmp("e_src", [P, EC], I32), tmp("e_dst", [P, EC], I32), tmp("e_next", [P, EC], I32)
        e_dst_f, e_next_f, e_number = tmp("e_dst_f", [P, EC]), tmp("e_next_f", [P, EC]), tmp("e_number", [P, EC])
        e_number_i = tmp("e_number_i", [P, EC], I32)
        falls = tmp("falls", [P, 1])
        unsorted_i = tmp("unsorted_i", [P, 1], I32)
        all_one = tmp("all_one", [P, P])
        rank_f, rank_i = tmp("rank_f", [P, EC]), tmp("rank_i", [P, EC], I32)
        other_i, other_n = tmp("other_i", [P, CHUNK], I32), tmp("other_n", [P, CHUNK], I32)
        other_f, other_nf = tmp("other_f", [P, CHUNK]), tmp("other_nf", [P, CHUNK])
        less, before_it = tmp("less", [P, CHUNK]), tmp("before_it", [P, CHUNK])
        n_less, n_same = tmp("n_less", [P, 1]), tmp("n_same", [P, 1])
        put_at = tmp("put_at", [P, 1], I32)
        put_src, put_dst = tmp("put_src", [P, 1], I32), tmp("put_dst", [P, 1], I32)
        (u_copy, u_ld, u_set, u_step, u_sum, u_ready, o_ld, o_num, o_ready, o_used, u_rank, u_pos, u_put) = (
            sem(k) for k in ("u_copy", "u_ld", "u_set", "u_step", "u_sum", "u_ready", "o_ld", "o_num", "o_ready",
                             "o_used", "u_rank", "u_pos", "u_put"))

        with phase() as block:
            @block.sync
            def _(sp):
                def line(a, n):
                    return a.rearrange("(o n) -> o n", o=1)[:, 0:n]

                sp.dma_start(e_dst[0:EP, :], dst.rearrange("(p c) -> p c", c=EC)).then_inc(u_ld, 16)
                sp.wait_ge(u_set, 1)
                sp.dma_start(e_next[0:EP - 1, :], dst[1:E - EC + 1].rearrange("(p c) -> p c", c=EC)).then_inc(u_ld, 16)
                sp.dma_start(e_next[EP - 1:EP, 0:EC - 1], line(dst[E - EC + 1:E], EC - 1)).then_inc(u_ld, 16)
                sp.dma_start(e_src[0:EP, :], src.rearrange("(p c) -> p c", c=EC)).then_inc(u_ld, 16)
                sp.dma_start(edge_dst.rearrange("(p c) -> p c", c=EC), dst.rearrange("(p c) -> p c", c=EC)).then_inc(u_copy, 16)
                sp.dma_start(edge_src.rearrange("(p c) -> p c", c=EC), src.rearrange("(p c) -> p c", c=EC)).then_inc(u_copy, 16)
                sp.wait_ge(u_copy, 32)
                sp.wait_ge(u_ready, 1)
                unsorted = sp.value_load(unsorted_i[0:1, 0:1], min_val=0, max_val=1)
                with sp.If(unsorted > 0):
                    with sp.Fori(0, E // CHUNK) as b:
                        sp.wait_ge(o_used, b + 1)
                        sp.dma_start(other_i[:, :], dst.rearrange("(b f) -> b f", f=CHUNK)[b].rearrange("(o f) -> o f", o=1)
                                     .to_broadcast([P, CHUNK])).then_inc(o_ld, 16)

            @block.gpsimd
            def _(pool):
                g = nc.gpsimd
                g.memset(e_next[:, :], PAD_DST).then_inc(u_set, 1)
                g.memset(all_one[:, :], 1.0).then_inc(u_set, 1)
                g.iota(e_number_i[:, :], pattern=[[1, EC]], base=0, channel_multiplier=EC).then_inc(u_set, 1)
                pool.wait_ge(u_ready, 1)
                unsorted = pool.value_load(unsorted_i[0:1, 0:1], min_val=0, max_val=1)
                with pool.If(unsorted > 0):
                    g.iota(other_n[:, :], pattern=[[1, CHUNK]], base=0, channel_multiplier=0).then_inc(o_num, 1)
                    pool.wait_ge(u_rank, 1)
                    pool.wait_ge(u_copy, 32)
                    with pool.Fori(0, EC) as c:
                        g.tensor_copy(put_at[0:EP, :], rank_i[0:EP, bass.ds(c, 1)])
                        g.tensor_copy(put_src[0:EP, :], e_src[0:EP, bass.ds(c, 1)])
                        g.tensor_copy(put_dst[0:EP, :], e_dst[0:EP, bass.ds(c, 1)]).then_inc(u_pos, 1)
                        alone(pool, u_pos, c + 1)
                        for table, value in ((edge_src2, put_src), (edge_dst2, put_dst)):
                            g.indirect_dma_start(out=table, out_offset=bass.IndirectOffsetOnAxis(ap=put_at[0:EP, 0:1], axis=0),
                                                 in_=value[0:EP, :], in_offset=None, bounds_check=E - 1,
                                                 oob_is_err=False).then_inc(u_put, 16)
                        alone(pool, u_put, (c + 1) * 32)

            @block.tensor
            def _(pe):
                pe.wait_ge(u_sum, 1)
                nc.tensor.matmul(pS[:, 0:1], all_one[:, :], falls[:, 0:1], start=True, stop=True).then_inc(u_sum, 1)

            @block.vector
            def _(dve):
                v_ = nc.vector
                count = [0]

                def link(ins):
                    count[0] += 1
                    ins.then_inc(u_step, 1)
                    dve.wait_ge(u_step, count[0])

                dve.wait_ge(u_set, 3)
                dve.wait_ge(u_ld, 16 * 4)
                v_.tensor_copy(e_number[:, :], e_number_i[:, :])
                v_.tensor_copy(e_next_f[0:EP, :], e_next[0:EP, :])
                v_.memset(falls[:, :], 0.0)
                v_.memset(rank_f[:, :], 0.0)
                link(v_.tensor_copy(e_dst_f[0:EP, :], e_dst[0:EP, :]))
                v_.scalar_tensor_tensor(out=rank_f[0:EP, :], in0=e_next_f[0:EP, :], scalar=1.0, in1=e_dst_f[0:EP, :],
                                        op0=ALU.mult, op1=ALU.is_lt, accum_out=falls[0:EP, 0:1]).then_inc(u_sum, 1)
                dve.wait_ge(u_sum, 2)
                v_.tensor_scalar(unsorted_i[:, :], pS[:, 0:1], 1.0, None, ALU.min).then_inc(u_ready, 1)
                dve.wait_ge(u_ready, 1)
                unsorted = dve.value_load(unsorted_i[0:1, 0:1], min_val=0, max_val=1)
                with dve.If(unsorted > 0):
                    dve.wait_ge(o_num, 1)
                    v_.memset(rank_f[:, :], 0.0)
                    link(v_.tensor_copy(other_nf[:, :], other_n[:, :]))
                    dve.sem_inc(o_used, 1)
                    with dve.Fori(0, E // CHUNK) as b:
                        alone(dve, o_ld, (b + 1) * 16)
                        v_.tensor_copy(other_f[:, :], other_i[:, :]).then_inc(o_ready, 1)
                        alone(dve, o_ready, b + 1)
                        with dve.Fori(0, EC) as c:
                            step = (b * EC + c) * 4 + count[0]
                            v_.tensor_scalar(less[0:EP, :], other_f[0:EP, :], e_dst_f[0:EP, bass.ds(c, 1)], 0.0, ALU.is_lt,
                                             ALU.add, accum_out=n_less[0:EP, 0:1])
                            v_.tensor_scalar(before_it[0:EP, :], other_nf[0:EP, :], e_number[0:EP, bass.ds(c, 1)], None,
                                             ALU.is_lt).then_inc(u_step, 1)
                            alone(dve, u_step, step + 1)
                            v_.scalar_tensor_tensor(out=less[0:EP, :], in0=other_f[0:EP, :],
                                                    scalar=e_dst_f[0:EP, bass.ds(c, 1)], in1=before_it[0:EP, :],
                                                    op0=ALU.is_equal, op1=ALU.mult, accum_out=n_same[0:EP, 0:1]
                                                    ).then_inc(u_step, 1)
                            alone(dve, u_step, step + 2)
                            v_.tensor_tensor(n_less[0:EP, :], n_less[0:EP, :], n_same[0:EP, :], ALU.add).then_inc(u_step, 1)
                            alone(dve, u_step, step + 3)
                            v_.tensor_tensor(rank_f[0:EP, bass.ds(c, 1)], rank_f[0:EP, bass.ds(c, 1)], n_less[0:EP, :],
                                             ALU.add).then_inc(u_step, 1)
                            alone(dve, u_step, step + 4)
                        v_.tensor_scalar(other_nf[:, :], other_nf[:, :], float(CHUNK), None, ALU.add).then_inc(o_used, 1)
                        alone(dve, o_used, b + 2)
                    v_.tensor_copy(rank_i[0:EP, :], rank_f[0:EP, :]).then_inc(u_rank, 1)

        sort_mem.close()

        with phase() as block:
            def pair_rows(dram_rows, n, width=D):
                return dram_rows.rearrange("(j p s) d -> j p (s d)", p=P, s=2)[n]

            src_v, dst_v = edge_src, edge_dst
            ext3 = [None] + [r[EXT:ROWS, :].rearrange("(t p) d -> t p d", p=P) for r in rows[1:]]
            node3 = [r[0:EXT, :] for r in rows]

            p0_ld, p0_st = sems("p0_ld"), sems("p0_st")
            p0_free, p0_stats, p0_mv, p0_sd, p0_rs, p0_rstd, p0_norm = (sem(f"p0_{k}") for k in
                ("free", "stats", "mv", "sd", "rs", "rstd", "norm"))
            dr_ld, so_st = sem("dr_ld"), sem("so_st")
            so_done = sem("so_done")
            da_got = sems("da_got")
            da_idx, da_kept = sem("da_idx"), sem("da_kept")

            x_last = x[(NP - 1) * 2 * P:N, :].rearrange("(p s) d -> p (s d)", s=2)
            x_full = x[0:(NP - 1) * 2 * P, :]

            @block.sync
            def _(sp):
                sp.wait_ge(s_pad, 3)
                full = (ET - 1 - TC) * P
                for k, a in ((0, src_v), (1, dst_v)):
                    sp.dma_start(nat_i[0:TC, k, 0, :], a[0:TC * P].rearrange("(t e) -> t e", e=P)).then_inc(s_nat, 16)
                    sp.dma_start(nat_i[0:TC - 1, k, 1, :], a[TC * P:TC * P + full].rearrange("(t e) -> t e", e=P)).then_inc(s_nat, 16)
                    sp.dma_start(nat_i[TC - 1:TC, k, 1, 0:LAST_E], a[TC * P + full:E].rearrange("(t e) -> t e", t=1)).then_inc(s_nat, 16)
                sp.dma_start(nat_i[0:TC, 2, 0, :], dst_v[1:TC * P + 1].rearrange("(t e) -> t e", e=P)).then_inc(s_nat, 16)
                sp.dma_start(nat_i[0:TC - 1, 2, 1, :], dst_v[TC * P + 1:TC * P + full + 1].rearrange("(t e) -> t e", e=P)).then_inc(s_nat, 16)
                sp.dma_start(nat_i[TC - 1:TC, 2, 1, 0:LAST_E - 1], dst_v[TC * P + full + 1:E].rearrange("(t e) -> t e", t=1)).then_inc(s_nat, 16)
                with nc.allow_non_contiguous_dma(reason="one edge of each tile"):
                    sp.dma_start(prev_i[1:TC, 0:1],
                                 dst_v[0:(TC - 1) * P].rearrange("(t e) -> t e", e=P)[:, P - 1:P]).then_inc(s_nat, 16)
                    sp.dma_start(prev_i[0:TC, 1:2],
                                 dst_v[(TC - 1) * P:(2 * TC - 1) * P].rearrange("(t e) -> t e", e=P)[:, P - 1:P]).then_inc(s_nat, 16)

                def load_x(v):
                    at_least(sp, p0_norm, v.n - RING + 1)
                    if isinstance(v.n, int) and v.n == NP - 1:
                        sp.dma_start(xin[0:LAST_P, v.slot, :], x_last).then_inc(p0_ld[v.slot], 16)
                    else:
                        sp.dma_start(xin[:, v.slot, :], pair_rows(x_full, v.n)).then_inc(p0_ld[v.slot], 16)

                def load_dst_rows(v):
                    at_least(sp, so_done, v.round)
                    sp.dma_start(dst_row[:, :], bcast_rows(v)).then_inc(dr_ld, 16)

                td = turned_dst.rearrange("(g r) e -> g (r e)", r=RING)

                def bcast_rows(v):
                    return td[v.round].rearrange("(o f) -> o f", o=1).to_broadcast([P, RING * P])

                for v in range(RING):
                    load_x(At(0, v))
                sp.wait_ge(s_back, 1)
                sp.dma_start(turned_dst.rearrange("(c t) e -> t c e", c=2), back[0:TC, :, :]).then_inc(s_turned_st, 16)
                sp.wait_ge(s_turned_st, 16)
                sp.wait_ge(s_lin, 1)
                sp.dma_start(row_of.rearrange("(p c) o -> p (c o)", p=P), lin_id[:, :]).then_inc(s_lin, 16)
                sp.wait_ge(s_inv_t, 2)
                sp.dma_start(inv_root.rearrange("(c t e) o -> t c (e o)", c=4, e=P), inv_t[0:HC, :, :]).then_inc(s_inv_st, 16)

                def load_x_later(v):
                    if not (isinstance(v.n, int) and v.n < RING):
                        load_x(v)
                steps(sp, NP, [(load_dst_rows, 0, 0), (load_x_later, 0)], peel=1)

            @block.gpsimd
            def _(pool):
                g = nc.gpsimd
                g.memset(nat_i[:, 0, :, :], 0).then_inc(s_pad, 1)
                g.memset(nat_i[:, 1:3, :, :], PAD_DST).then_inc(s_pad, 1)
                g.memset(prev_i[:, :], -1).then_inc(s_pad, 1)
                g.memset(ident[:, :], 0.0).then_inc(s_const, 1)
                g.memset(turn[:, :], 0.0).then_inc(s_const, 1)
                g.memset(ones[:, :], 1.0).then_inc(s_const, 1)
                pool.wait_ge(s_const, 3)
                g.affine_select(out=ident[:, :], in_=ident[:, :], compare_op=ALU.not_equal, fill=1.0, base=0,
                                pattern=[[-1, P]], channel_multiplier=1).then_inc(s_const, 1)
                g.affine_select(out=turn[:, :], in_=turn[:, :], compare_op=ALU.not_equal, fill=1.0, base=-(P - 1),
                                pattern=[[1, P]], channel_multiplier=1).then_inc(s_const, 1)
                g.affine_select(out=below[:, :], in_=ones[:, :], compare_op=ALU.is_gt, fill=0.0, base=0,
                                pattern=[[1, P]], channel_multiplier=-1).then_inc(s_const, 1)
                g.iota(iota_i[:, :], pattern=[[1, COLS]], base=0, channel_multiplier=0).then_inc(s_const, 1)
                g.iota(node_i[:, :], pattern=[[2 * P, NP], [1, 2]], base=1, channel_multiplier=2).then_inc(s_const, 1)
                g.iota(ext_id[:, :], pattern=[[P, ET]], base=EXT, channel_multiplier=1).then_inc(s_const, 1)
                g.memset(eps_t[:, :], EPS).then_inc(s_const, 1)
                g.iota(lin_id[:, :], pattern=[[1, COLS]], base=0, channel_multiplier=COLS).then_inc(s_lin, 1)

                pool.wait_ge(s_inv_st, 16)

                def ask(v):
                    at_least(pool, da_kept, v.n - RING + 1)
                    g.tensor_copy(idx_a[:, v.slot:v.slot + 1], table_i[:, bass.ds(v.n, 1)]).then_inc(da_idx, 1)
                    alone(pool, da_idx, v.n + 1)
                    g.indirect_dma_start(out=got_a[:, v.slot:v.slot + 1], out_offset=None, in_=inv_root,
                                         in_offset=bass.IndirectOffsetOnAxis(ap=idx_a[:, v.slot:v.slot + 1], axis=0)
                                         ).then_inc(da_got[v.slot], 16)

                def keep(v):
                    pool.wait_ge(da_got[v.slot], 16 * (v.round + 1))
                    g.tensor_copy(inv_dst[:, bass.ds(v.n, 1)], got_a[:, v.slot:v.slot + 1]).then_inc(da_kept, 1)

                def root_of(v):
                    pool.wait_ge(p0_sd, v.n + 1)
                    g.tensor_tensor(rs[:, v.slot, :], veps[:, v.slot, :], half[:, 0:2], ALU.pow).then_inc(p0_rs, 1)

                steps(pool, ET, [(root_of, 0), (keep, 3), (ask, 0)])

            @block.scalar
            def _(act):
                act.wait_ge(s_root, 1)
                nc.scalar.activation(inv[:, :], root[:, :], ACT.Sqrt).then_inc(s_root, 1)

                def add_eps(v):
                    act.wait_ge(p0_mv, v.n + 1)
                    nc.scalar.activation(veps[:, v.slot, :], mv[:, v.slot, :, 1], ACT.Identity,
                                         bias=eps_t[:, 0:1]).then_inc(p0_sd, 1)

                def store(v):
                    act.wait_ge(p0_norm, v.n + 1)
                    act.dma_start(pair_rows(node3[0], v.n), gout[:, v.slot, :]).then_inc(p0_st[v.slot], 16)

                def store_same(v):
                    act.wait_ge(so_done, v.round + 1)
                    act.dma_start(same_dram.rearrange("(g r) e f -> g e r f", r=RING)[v.round],
                                  same_out[:, :, :]).then_inc(so_st, 16)

                steps(act, NP, [(add_eps, 0), (store_same, 1, 1), (store, 2)])
                for s in range(RING):
                    act.wait_ge(p0_st[s], 16 * NP // RING)
                act.wait_ge(so_st, 16 * NP // RING)

            @block.vector
            def _(dve):
                v_ = nc.vector
                count = [0]

                def link(ins):
                    count[0] += 1
                    ins.then_inc(s_pro, 1)
                    dve.wait_ge(s_pro, count[0])

                link(v_.memset(pW[:, :], 0.0))
                dve.wait_ge(s_nat, 16 * 11)
                dve.wait_ge(s_const, 10)
                link(v_.tensor_copy(nat_f[:, 0:2, :, :], nat_i[:, 0:2, :, :]))
                link(v_.tensor_copy(nat_next[:, :, :], nat_i[:, 2, :, :]))
                link(v_.tensor_copy(prev_f[:, :], prev_i[:, :]))
                link(v_.tensor_tensor(nat_f[:, 2, :, :], nat_next[:, :, :], nat_f[:, 1, :, :], ALU.is_equal))
                link(v_.scalar_tensor_tensor(out=nat_f[:, 2, :, :], in0=nat_f[:, 2, :, :], scalar=float(FAR),
                                             in1=nat_f[:, 1, :, :], op0=ALU.mult, op1=ALU.add))
                link(v_.memset(nat_f[:, 3, :, :], 0.0))
                v_.tensor_tensor(nat_f[:, 3, :, 0], prev_f[:, :], nat_f[:, 1, :, 0], ALU.is_equal).then_inc(s_flip, 1)
                dve.wait_ge(s_flipped, 1)
                link(v_.tensor_copy(turned[:, 0:2, :], pT[0][:, 0:2 * ET]))
                v_.tensor_copy(turned[:, 2:4, :], pT[1][:, 0:2 * ET]).then_inc(s_flip, 1)
                dve.wait_ge(s_flipped, 2)
                for k in range(4):
                    ps = pO[k // 2][:, (k % 2) * ET:(k % 2 + 1) * ET].rearrange("p (t o) -> p t o", o=2)[:, :, 1]
                    last = v_.tensor_copy(turned[:, k, :].rearrange("p (t o) -> p t o", o=2)[:, :, 1], ps)
                last.then_inc(s_flip, 1)
                dve.wait_ge(s_flip, 3)
                v_.tensor_copy(src_i[:, :], turned[:, 0, :])
                v_.tensor_copy(emit_i[:, :], turned[:, 2, :])
                link(v_.tensor_copy(dst_i[:, :], turned[:, 1, :]))
                link(v_.tensor_scalar(lo_i[:, :], dst_i[:, :], 1, P - 1, ALU.logical_shift_right, ALU.bitwise_and))
                link(v_.tensor_scalar(hi_i[:, :], dst_i[:, :], 8, 1, ALU.logical_shift_right, ALU.logical_shift_left))
                link(v_.tensor_scalar(odd_i[:, :], dst_i[:, :], 1, None, ALU.bitwise_and))
                link(v_.tensor_tensor(hi_i[:, :], hi_i[:, :], odd_i[:, :], ALU.bitwise_or))
                link(v_.tensor_copy(lo_f[:, :], lo_i[:, :]))
                link(v_.tensor_copy(hi_f[:, :], hi_i[:, :]))
                link(v_.tensor_copy(iota_p16[:, :], iota_i[:, 0:P]))
                link(v_.tensor_copy(iota_c16[:, :], iota_i[:, :]))
                link(v_.tensor_copy(iota_f[:, :], iota_i[:, :]))
                link(v_.tensor_scalar(dst_safe[:, :], turned[:, 1, :], float(N - 1), None, ALU.min))
                link(v_.tensor_scalar(emit_f[:, :], turned[:, 2, :], float(N), 1024.0, ALU.is_ge, ALU.mult))
                link(v_.tensor_tensor(hi_emit[:, :], emit_f[:, :], hi_f[:, :], ALU.add))
                link(v_.scalar_tensor_tensor(out=table_f[:, :], in0=hi_f[:, :], scalar=float(P), in1=lo_f[:, :],
                                             op0=ALU.mult, op1=ALU.add))
                link(v_.tensor_scalar(table_i[:, :], table_f[:, :], float(COLS * P - 1), None, ALU.min))
                dve.wait_ge(s_flipped, 3)
                v_.tensor_copy(back[0:TC, :, :], pO[0][0:TC, 0:2 * P].rearrange("t (c e) -> t c e", c=2)).then_inc(s_back, 1)

                def hots(v):
                    at_least(dve, s_count, v.n - RING + 1)
                    v_.tensor_scalar(hot_lo[:, v.slot, :], iota_p16[:, :], lo_f[:, bass.ds(v.n, 1)], None, ALU.is_equal)
                    v_.tensor_scalar(hot_hi[:, v.slot, :], iota_c16[:, :], hi_f[:, bass.ds(v.n, 1)], None,
                                     ALU.is_equal).then_inc(s_hot, 1)

                steps(dve, ET, [(hots, 0)])
                dve.wait_ge(s_count, ET)
                v_.tensor_scalar(root[:, :], pW[:, 0:COLS], 1.0, None, ALU.add).then_inc(s_root, 1)
                dve.wait_ge(s_root, 2)
                link(v_.reciprocal(inv[:, :], inv[:, :]))
                link(v_.tensor_tensor(half[:, :], inv[:, :], inv[:, :], ALU.mult))
                link(v_.tensor_tensor(half[:, :], half[:, :], root[:, :], ALU.mult))
                link(v_.tensor_scalar(half[:, :], half[:, :], -0.5, 1.5, ALU.mult, ALU.add))
                link(v_.tensor_tensor(inv[:, :], inv[:, :], half[:, :], ALU.mult))
                v_.memset(half[:, :], -0.5).then_inc(s_inv_t, 1)
                dve.wait_ge(s_flipped, 4)
                v_.tensor_copy(inv_t[0:HC, :, :], pO[1][0:HC, 0:4 * P].rearrange("t (c e) -> t c e", c=4)).then_inc(s_inv_t, 1)

                def statistics(v):
                    dve.wait_ge(p0_ld[v.slot], 16 * (v.round + 1))
                    for s in range(2):
                        last = v_.bn_stats(stats[:, v.slot, s, :], xin[:, v.slot, s * D:(s + 1) * D])
                    last.then_inc(p0_stats, 1)
                    alone(dve, p0_stats, v.n + 1)
                    for s in range(2):
                        last = v_.bn_aggr(mv[:, v.slot, s, :], stats[:, v.slot, s, :])
                    last.then_inc(p0_mv, 1)

                def normalise(v):
                    dve.wait_ge(p0_rs, v.n + 1)
                    v_.tensor_tensor(rstd[:, v.slot, :], rs[:, v.slot, :], inv[:, bass.ds(v.n * 2, 2)],
                                     ALU.mult).then_inc(p0_rstd, 1)
                    dve.wait_ge(p0_rstd, v.n + 1)
                    at_least(dve, p0_st[v.slot], 16 * v.round)
                    for s in range(2):
                        last = v_.tensor_scalar(gout[:, v.slot, s * D:(s + 1) * D], xin[:, v.slot, s * D:(s + 1) * D],
                                                mv[:, v.slot, s, 0:1], rstd[:, v.slot, s:s + 1], ALU.subtract, ALU.mult)
                    last.then_inc(p0_norm, 1)

                def same(v):
                    dve.wait_ge(dr_ld, 16 * (v.round + 1))
                    at_least(dve, so_st, 16 * v.round)
                    v_.tensor_tensor(same_out[:, :, :], dst_row[:, :].rearrange("p (r e) -> p r e", r=RING),
                                     turned[:, 1, bass.ds(v.n, RING)].rearrange("p (r o) -> p r o", o=1).to_broadcast([P, RING, P]),
                                     ALU.is_equal).then_inc(so_done, 1)

                steps(dve, NP, [(statistics, 0), (normalise, 1), (same, 0, 0)])

            @block.tensor
            def _(pe):
                t_ = nc.tensor
                pe.wait_ge(s_const, 10)
                pe.wait_ge(s_flip, 1)
                for k in range(4):
                    for c in range(2):
                        o = (k % 2) * ET + c * TC
                        last = t_.transpose(pT[k // 2][:, o:o + TC], nat_f[0:TC, k, c, :], ident[0:TC, 0:TC])
                last.then_inc(s_flipped, 1)
                pe.wait_ge(s_flip, 2)
                for k in range(2):
                    last = t_.matmul(pO[k][:, 0:2 * ET], turn[:, :], turned[:, 2 * k:2 * k + 2, :], start=True, stop=True)
                last.then_inc(s_flipped, 1)
                pe.wait_ge(s_flip, 3)
                for c in range(2):
                    last = t_.transpose(pO[0][0:TC, c * P:(c + 1) * P], turned[:, 1, c * TC:(c + 1) * TC], ident[:, :])
                last.then_inc(s_flipped, 1)

                def tally(v):
                    pe.wait_ge(s_hot, v.n + 1)
                    t_.matmul(pW[:, 0:COLS], hot_lo[:, v.slot, :], hot_hi[:, v.slot, :], start=False, stop=False,
                              skip_group_check=True).then_inc(s_count, 1)

                steps(pe, ET, [(tally, 0)])
                pe.wait_ge(s_inv_t, 1)
                for c in range(4):
                    last = t_.transpose(pO[1][0:HC, c * P:(c + 1) * P], inv[:, c * HC:(c + 1) * HC], ident[:, :])
                last.then_inc(s_flipped, 1)

        G_LD, G_ST = sems("g_ld"), sems("g_st")
        E_ST = sems("e_st")
        S_LD, O_LD, OG_LD, M_LD = sems("s_ld"), sems("o_ld"), sems("og_ld"), sems("m_ld")
        R_ST, R_LD = sems("r_st"), sems("r_ld")
        (w_got, w_split, b_got, t_done, xh_done, xl_done, o_done, z_done, h_done, carry_done, sum_done, tot_done,
         et_done, eh_done, el_done, pz_done, ez_done, eg_done, eo_done, i_m, i_s, i_r, r_kept) = (sem(k) for k in (
            "w_got", "w_split", "b_got", "t_done", "xh_done", "xl_done", "o_done", "z_done", "h_done", "carry_done",
            "sum_done", "tot_done", "et_done", "eh_done", "el_done", "pz_done", "ez_done", "eg_done", "eo_done",
            "i_m", "i_s", "i_r", "r_kept"))

        (x2_done, x2e_done, xe_b, st_done, mv_done, ve_done, r_pow, r_done, n_done, d_done, w_done, i_x, hot_done,
         w_tally, nb_zero, last_step) = (sem(k) for k in (
            "x2_done", "x2e_done", "xe_b", "st_done", "mv_done", "ve_done", "r_pow", "r_done", "n_done", "d_done",
            "w_done", "i_x", "hot_done", "w_tally", "nb_zero", "last_step"))
        X_LD, X_ST, N_ST, XE_LD, NE_ST, OE_ST = (sems("xr_ld"), sems("out_st"), sems("nb_st"), sems("xe_ld"),
                                                 sems("nbe_st"), sems("oute_st"))

        def total(layer, v):
            return v.n + layer * NP

        def rounds(layer, v):
            return v.round + layer * (NP // RING)

        def turn_pair(pe, layer):
            def stage(v):
                n = total(layer, v)
                pe.wait_ge(G_LD[v.slot], 16 * (rounds(layer, v) + 1))
                at_least(pe, xl_done, n - 1)
                for s in range(2):
                    for k in range(KC):
                        o = (s * KC + k) * P
                        last = nc.tensor.transpose(pT[v.two][:, o:o + P], xin[:, v.slot, o:o + P], ident[:, :])
                last.then_inc(t_done, 1)
            return stage

        def three_passes(out_ps, hi, lo, whi, wlo, add=False):
            for k in range(KC):
                nc.tensor.matmul(out_ps, hi(k), whi(k), start=(k == 0 and not add), stop=False, skip_group_check=add)
                nc.tensor.matmul(out_ps, hi(k), wlo(k), start=False, stop=False, skip_group_check=add)
                last = nc.tensor.matmul(out_ps, lo(k), whi(k), start=False, stop=(k == KC - 1), skip_group_check=add)
            return last

        def multiply_pair(pe, layer):
            def stage(v):
                n = total(layer, v)
                pe.wait_ge(xl_done, n + 1)
                if layer < 2:
                    at_least(pe, z_done, n - 1)
                else:
                    if isinstance(v.n, int) and v.n < 2:
                        pe.wait_ge(z_done, 2 * NP)
                    at_least(pe, x2_done, v.n - 1)
                    pe.wait_ge(X_LD[v.slot], 16 * (v.round + 1))
                    nc.tensor.matmul(pO[v.two][:, :], ident[:, :], xres[:, v.slot, :], start=True, stop=False,
                                     skip_group_check=True)
                    nc.tensor.matmul(pO[v.two][:, :], one_r[0:2, :], bias_mix[0:2, :], start=False, stop=False,
                                     skip_group_check=True)
                for s in range(2):
                    last = three_passes(pO[v.two][:, s * D:(s + 1) * D],
                                        lambda k: xt_hi[:, v.two, s, k, :], lambda k: xt_lo[:, v.two, s, k, :],
                                        lambda k: w_hi[:, layer, k, :], lambda k: w_lo[:, layer, k, :], layer == 2)
                last.then_inc(o_done, 1)
            return stage

        def sum_tile(pe, layer):
            def stage(v):
                n = total(layer, v)
                pe.wait_ge(S_LD[v.slot], 16 * (rounds(layer, v) + 1))
                pe.wait_ge(carry_done, n + 1)
                at_least(pe, tot_done, n)
                nc.tensor.matmul(pS[:, 0:D], same_t[:, v.slot, :], msg[:, v.slot, :], start=True,
                                 stop=True).then_inc(sum_done, 1)
            return stage

        def turn_tile(pe, layer):
            def stage(v):
                n = total(layer, v)
                pe.wait_ge(tot_done, n + 1)
                at_least(pe, el_done, n)
                for k in range(KC):
                    last = nc.tensor.transpose(pE[:, k * P:(k + 1) * P], tot[:, v.two, k * P:(k + 1) * P], ident[:, :])
                last.then_inc(et_done, 1)
            return stage

        def multiply_tile(pe, layer):
            def stage(v):
                n = total(layer, v)
                pe.wait_ge(el_done, n + 1)
                at_least(pe, ez_done if layer < 2 else x2e_done, n if layer < 2 else v.n)
                three_passes(pZ[:, 0:D], lambda k: et_hi[:, v.two, k, :], lambda k: et_lo[:, v.two, k, :],
                             lambda k: w_hi[:, layer, k, :], lambda k: w_lo[:, layer, k, :]).then_inc(pz_done, 1)
            return stage

        def high_pair(act, layer):
            def stage(v):
                n = total(layer, v)
                act.wait_ge(t_done, n + 1)
                at_least(act, o_done, n - 1)
                nc.scalar.activation(xt_hi[:, v.two, :, :, :].rearrange("p s k c -> p (s k c)"), pT[v.two][:, :],
                                     ACT.Copy).then_inc(xh_done, 1)
            return stage

        def low_pair(dve, layer):
            def stage(v):
                n = total(layer, v)
                dve.wait_ge(xh_done, n + 1)
                nc.vector.tensor_tensor(xt_lo[:, v.two, :, :, :].rearrange("p s k c -> p (s k c)"), pT[v.two][:, :],
                                        xt_hi[:, v.two, :, :, :].rearrange("p s k c -> p (s k c)").bitcast(F32),
                                        ALU.subtract).then_inc(xl_done, 1)
            return stage

        def high_tile(act, layer):
            def stage(v):
                n = total(layer, v)
                act.wait_ge(et_done, n + 1)
                at_least(act, pz_done, n - 1)
                nc.scalar.activation(et_hi[:, v.two, :, :].rearrange("p k c -> p (k c)"), pE[:, 0:D],
                                     ACT.Copy).then_inc(eh_done, 1)
            return stage

        def low_tile(dve, layer):
            def stage(v):
                n = total(layer, v)
                dve.wait_ge(eh_done, n + 1)
                nc.vector.tensor_tensor(et_lo[:, v.two, :, :].rearrange("p k c -> p (k c)"), pE[:, 0:D],
                                        et_hi[:, v.two, :, :].rearrange("p k c -> p (k c)").bitcast(F32),
                                        ALU.subtract).then_inc(el_done, 1)
            return stage

        def carry(dve, layer):
            def stage(v):
                n = total(layer, v)
                dve.wait_ge(M_LD[v.slot], 16 * (rounds(layer, v) + 1))
                if isinstance(v.n, int) and v.n == 0:
                    nc.vector.engine_nop().then_inc(carry_done, 1)
                    return
                dve.wait_ge(sum_done, n)
                nc.vector.scalar_tensor_tensor(out=msg[:, v.slot, :], in0=pS[:, 0:D],
                                               scalar=turned[:, 3, bass.ds(v.n, 1)], in1=msg[:, v.slot, :],
                                               op0=ALU.mult, op1=ALU.add).then_inc(carry_done, 1)
            return stage

        def add_own(dve, layer):
            def stage(v):
                n = total(layer, v)
                if layer == 0:
                    dve.wait_ge(OG_LD[v.slot], 16 * (v.round + 1))
                else:
                    dve.wait_ge(O_LD[v.slot], 16 * (rounds(layer - 1, v) + 1))
                dve.wait_ge(sum_done, n + 1)
                at_least(dve, et_done, n - 1)
                nc.vector.tensor_tensor(tot[:, v.two, :], pS[:, 0:D], own[:, v.slot, :], ALU.add).then_inc(tot_done, 1)
            return stage

        def fetch_first(pool):
            def stage(v):
                g = nc.gpsimd
                at_least(pool, sum_done, v.n - RING + 1)
                g.tensor_copy(idx_m[:, v.slot:v.slot + 1], src_i[:, bass.ds(v.n, 1)]).then_inc(i_m, 1)
                at_least(pool, tot_done, v.n - RING + 1)
                g.tensor_copy(idx_s[:, v.slot:v.slot + 1], dst_safe[:, bass.ds(v.n, 1)]).then_inc(i_s, 1)
                at_least(pool, R_ST[v.slot], 16 * v.round)
                g.tensor_copy(idx_r[:, v.slot:v.slot + 1], emit_i[:, bass.ds(v.n, 1)])
                g.tensor_copy(val_r[:, v.slot:v.slot + 1], ext_id[:, bass.ds(v.n, 1)]).then_inc(i_r, 1)
                alone(pool, i_m, v.n + 1)
                g.indirect_dma_start(out=msg[:, v.slot, :], out_offset=None, in_=rows[0],
                                     in_offset=bass.IndirectOffsetOnAxis(ap=idx_m[:, v.slot:v.slot + 1], axis=0)
                                     ).then_inc(M_LD[v.slot], 16)
                alone(pool, i_s, v.n + 1)
                g.indirect_dma_start(out=own[:, v.slot, :], out_offset=None, in_=rows[0],
                                     in_offset=bass.IndirectOffsetOnAxis(ap=idx_s[:, v.slot:v.slot + 1], axis=0)
                                     ).then_inc(OG_LD[v.slot], 16)
                alone(pool, i_r, v.n + 1)
                g.indirect_dma_start(out=row_of, out_offset=bass.IndirectOffsetOnAxis(ap=idx_r[:, v.slot:v.slot + 1], axis=0),
                                     in_=val_r[:, v.slot:v.slot + 1], in_offset=None, bounds_check=N - 1,
                                     oob_is_err=False).then_inc(R_ST[v.slot], 16)
            return stage

        def ask_row(pool):
            def stage(v):
                g = nc.gpsimd
                at_least(pool, M_LD[v.slot], 16 * rounds(1, v))
                at_least(pool, r_kept, v.n - RING + 1)
                g.tensor_copy(idx_r[:, v.slot:v.slot + 1], src_i[:, bass.ds(v.n, 1)]).then_inc(i_r, 1)
                alone(pool, i_r, ET + v.n + 1)
                g.indirect_dma_start(out=got_r[:, v.slot:v.slot + 1], out_offset=None, in_=row_of,
                                     in_offset=bass.IndirectOffsetOnAxis(ap=idx_r[:, v.slot:v.slot + 1], axis=0)
                                     ).then_inc(R_LD[v.slot], 16)
            return stage

        def fetch_second(pool):
            def stage(v):
                g = nc.gpsimd
                pool.wait_ge(R_LD[v.slot], 16 * (v.round + 1))
                g.tensor_copy(src_row[:, bass.ds(v.n, 1)], got_r[:, v.slot:v.slot + 1]).then_inc(r_kept, 1)
                alone(pool, sum_done, ET + v.n - RING + 1)
                g.indirect_dma_start(out=msg[:, v.slot, :], out_offset=None, in_=rows[1],
                                     in_offset=bass.IndirectOffsetOnAxis(ap=got_r[:, v.slot:v.slot + 1], axis=0)
                                     ).then_inc(M_LD[v.slot], 16)
            return stage

        def load_pair(sp, layer):
            def stage(v):
                at_least(sp, t_done, total(layer, v) - RING + 1)
                sp.dma_start(xin[:, v.slot, :], pair_rows(node3[layer], v.n)).then_inc(G_LD[v.slot], 16)
            return stage

        def load_same(sp, layer):
            def stage(v):
                at_least(sp, sum_done, total(layer, v) - RING + 1)
                sp.dma_start(same_t[:, v.slot, :], same_dram[v.n]).then_inc(S_LD[v.slot], 16)
            return stage

        def load_own(sp, layer):
            def stage(v):
                at_least(sp, tot_done, total(layer, v) - RING + 1)
                sp.dma_start(own[:, v.slot, :], ext3[layer][v.n]).then_inc(O_LD[v.slot], 16)
            return stage

        def stored(eng, layer):
            for s in range(RING):
                if layer == 0:
                    eng.wait_ge(p0_st[s], 16 * NP // RING)
                else:
                    eng.wait_ge(G_ST[s], 16 * layer * NP // RING)
                    eng.wait_ge(E_ST[s], 16 * layer * ET // RING)

        def halves(w, k):
            return w.rearrange("(k p) n -> p k n", p=P)

        with phase() as block:
            @block.sync
            def _(sp):
                for l, w in enumerate((W1, W2, W3)):
                    at_least(sp, w_split, 2 * l)
                    sp.dma_start(w_in[:, :, :], halves(w, KC)).then_inc(w_got, 16)
                for l, b in enumerate((b1, b2, b3)):
                    for s in range(2):
                        sp.dma_start(bias[:, l, s * D:(s + 1) * D],
                                     b.rearrange("(o n) -> o n", o=1).to_broadcast([P, D])).then_inc(b_got, 16)
                sp.dma_start(wr_row[:, :], wr.rearrange("n o -> o n").to_broadcast([P, D])).then_inc(b_got, 16)
                sp.dma_start(br_col[:, :], br.rearrange("(o n) -> o n", o=1).to_broadcast([P, 1])).then_inc(b_got, 16)

                def store_tile(layer):
                    def stage(v):
                        sp.wait_ge(eo_done, total(layer, v) + 1)
                        sp.dma_start(ext3[layer + 1][v.n], eo[:, v.slot, :]).then_inc(E_ST[v.slot], 16)
                    return stage

                for layer in range(2):
                    stored(sp, layer)
                    own_stage = [(load_own(sp, layer), 0)] if layer else []
                    steps(sp, NP, [(load_pair(sp, layer), 0), (load_same(sp, layer), 0), *own_stage,
                                   (store_tile(layer), 6)])

            @block.gpsimd
            def _(pool):
                stored(pool, 0)
                steps(pool, ET, [(fetch_first(pool), 0)])
                for s in range(RING):
                    pool.wait_ge(R_ST[s], 16 * ET // RING)
                stored(pool, 1)
                steps(pool, ET, [(fetch_second(pool), 2), (ask_row(pool), 0)])

            @block.tensor
            def _(pe):
                for layer in range(2):
                    steps(pe, NP, [(turn_pair(pe, layer), 0), (multiply_pair(pe, layer), 1), (sum_tile(pe, layer), 0),
                                   (turn_tile(pe, layer), 1), (multiply_tile(pe, layer), 2)])

            @block.scalar
            def _(act):
                nc.scalar.preload_act_table(ACT.Gelu_apprx_tanh)

                def gelu_pair(layer):
                    def stage(v):
                        n = total(layer, v)
                        act.wait_ge(z_done, n + 1)
                        at_least(act, G_ST[v.slot], 16 * rounds(layer, v))
                        nc.scalar.activation(gout[:, v.slot, :], zb[:, v.two, :], ACT.Gelu_apprx_tanh).then_inc(h_done, 1)
                    return stage

                def store_pair(layer):
                    def stage(v):
                        act.wait_ge(h_done, total(layer, v) + 1)
                        act.dma_start(pair_rows(node3[layer + 1], v.n), gout[:, v.slot, :]).then_inc(G_ST[v.slot], 16)
                    return stage

                def gelu_tile(layer):
                    def stage(v):
                        n = total(layer, v)
                        act.wait_ge(ez_done, n + 1)
                        at_least(act, eo_done, n - 1)
                        nc.scalar.activation(eh[:, v.two, :], ez[:, v.two, :], ACT.Gelu_apprx_tanh).then_inc(eg_done, 1)
                    return stage

                for layer in range(2):
                    steps(act, NP, [(high_pair(act, layer), 0), (gelu_tile(layer), 4), (gelu_pair(layer), 3),
                                    (store_pair(layer), 4), (high_tile(act, layer), 1)])
                for s in range(RING):
                    act.wait_ge(G_ST[s], 16 * 2 * NP // RING)
                    act.wait_ge(E_ST[s], 16 * 2 * ET // RING)

            @block.vector
            def _(dve):
                v_ = nc.vector
                for l in range(3):
                    dve.wait_ge(w_got, 16 * (l + 1))
                    v_.tensor_copy(w_hi[:, l, :, :], w_in[:, :, :]).then_inc(w_split, 1)
                    dve.wait_ge(w_split, 2 * l + 1)
                    v_.tensor_tensor(w_lo[:, l, :, :], w_in[:, :, :], w_hi[:, l, :, :].bitcast(F32),
                                     ALU.subtract).then_inc(w_split, 1)
                dve.wait_ge(b_got, 16 * 8)

                def bias_pair(layer):
                    def stage(v):
                        n = total(layer, v)
                        dve.wait_ge(o_done, n + 1)
                        at_least(dve, h_done, n - 1)
                        v_.tensor_tensor(zb[:, v.two, :], pO[v.two][:, :], bias[:, layer, :], ALU.add).then_inc(z_done, 1)
                    return stage

                def bias_tile(layer):
                    def stage(v):
                        n = total(layer, v)
                        dve.wait_ge(pz_done, n + 1)
                        at_least(dve, eg_done, n - 1)
                        v_.scalar_tensor_tensor(out=ez[:, v.two, :], in0=pZ[:, 0:D], scalar=inv_dst[:, bass.ds(v.n, 1)],
                                                in1=bias[:, layer, 0:D], op0=ALU.mult, op1=ALU.add).then_inc(ez_done, 1)
                    return stage

                def scale_tile(layer):
                    def stage(v):
                        n = total(layer, v)
                        dve.wait_ge(eg_done, n + 1)
                        at_least(dve, E_ST[v.slot], 16 * rounds(layer, v))
                        v_.tensor_scalar(eo[:, v.slot, :], eh[:, v.two, :], inv_dst[:, bass.ds(v.n, 1)], None,
                                         ALU.mult).then_inc(eo_done, 1)
                    return stage

                for layer in range(2):
                    steps(dve, NP, [(add_own(dve, layer), 1), (carry(dve, layer), 0), (low_tile(dve, layer), 2),
                                    (low_pair(dve, layer), 0), (bias_tile(layer), 3), (bias_pair(layer), 2),
                                    (scale_tile(layer), 5)])

        out_full = out[0:(NP - 1) * 2 * P, :]
        out_last = out[(NP - 1) * 2 * P:N, :].rearrange("(p s) d -> p (s d)", s=2)
        normed3 = normed[EXT:ROWS, :].rearrange("(t p) d -> t p d", p=P)
        ext_out3 = ext_out.rearrange("(t p) d -> t p d", p=P)
        L = 2

        def is_last(v):
            return isinstance(v.n, int) and v.n == NP - 1

        with phase() as block:
            @block.sync
            def _(sp):
                stored(sp, L)

                def load_x_pair(v):
                    at_least(sp, o_done, total(L, v) - RING + 1)
                    if is_last(v):
                        sp.dma_start(xres[0:LAST_P, v.slot, :], x_last).then_inc(X_LD[v.slot], 16)
                    else:
                        sp.dma_start(xres[:, v.slot, :], pair_rows(x_full, v.n)).then_inc(X_LD[v.slot], 16)

                def store_normed(v):
                    sp.wait_ge(w_done, v.n + 1)
                    sp.dma_start(pair_rows(normed[0:EXT, :], v.n), nb[:, v.slot, 0:2, :].rearrange("p s d -> p (s d)")
                                  ).then_inc(N_ST[v.slot], 16)

                def store_out(v):
                    sp.wait_ge(n_done, v.n + 1)
                    pair = x2n[:, v.slot, 0:2, :].rearrange("p s d -> p (s d)")
                    if is_last(v):
                        sp.dma_start(out_last, pair[0:LAST_P, :]).then_inc(X_ST[v.slot], 16)
                    else:
                        sp.dma_start(pair_rows(out_full, v.n), pair).then_inc(X_ST[v.slot], 16)

                def store_normed_tile(v):
                    sp.wait_ge(w_done, v.n + 1)
                    sp.dma_start(normed3[v.n], nb[:, v.slot, 2, :]).then_inc(NE_ST[v.slot], 16)

                def store_out_tile(v):
                    sp.wait_ge(n_done, v.n + 1)
                    sp.dma_start(ext_out3[v.n], x2n[:, v.slot, 2, :]).then_inc(OE_ST[v.slot], 16)

                steps(sp, NP, [(load_pair(sp, L), 0), (load_same(sp, L), 0), (load_own(sp, L), 0), (load_x_pair, 0),
                               (store_out, 7), (store_out_tile, 7),
                               (store_normed, 8), (store_normed_tile, 8)], peel=1)
                for s in range(RING):
                    sp.wait_ge(NE_ST[s], 16 * ET // RING)
                    sp.wait_ge(OE_ST[s], 16 * ET // RING)

            @block.gpsimd
            def _(pool):
                g = nc.gpsimd
                stored(pool, L)

                def fetch_third(v):
                    alone(pool, sum_done, 2 * ET + v.n - RING + 1)
                    g.tensor_copy(idx_m[:, v.slot:v.slot + 1], src_row[:, bass.ds(v.n, 1)]).then_inc(i_m, 1)
                    alone(pool, i_m, ET + v.n + 1)
                    g.indirect_dma_start(out=msg[:, v.slot, :], out_offset=None, in_=rows[2],
                                         in_offset=bass.IndirectOffsetOnAxis(ap=idx_m[:, v.slot:v.slot + 1], axis=0)
                                         ).then_inc(M_LD[v.slot], 16)

                def fetch_residual(v):
                    alone(pool, x2e_done, v.n - RING + 1)
                    g.tensor_copy(idx_s[:, v.slot:v.slot + 1], dst_safe[:, bass.ds(v.n, 1)]).then_inc(i_s, 1)
                    alone(pool, i_s, ET + v.n + 1)
                    g.indirect_dma_start(out=xe[:, v.slot, :], out_offset=None, in_=x,
                                         in_offset=bass.IndirectOffsetOnAxis(ap=idx_s[:, v.slot:v.slot + 1], axis=0)
                                         ).then_inc(XE_LD[v.slot], 16)

                def root_of(v):
                    pool.wait_ge(ve_done, v.n + 1)
                    g.tensor_tensor(rs3[:, v.slot, :], veps3[:, v.slot, :], half[:, 0:3], ALU.pow).then_inc(r_pow, 1)
                    pool.wait_ge(r_pow, 2 * v.n + 1)
                    g.tensor_tensor(shift3[:, v.slot, :], mv3[:, v.slot, :, 0], rs3[:, v.slot, :], ALU.mult).then_inc(r_pow, 1)
                    g.tensor_scalar(one_rs3[:, v.slot, :], rs3[:, v.slot, :], 1.0, None, ALU.add)
                    alone(pool, r_pow, 2 * v.n + 2)
                    g.tensor_scalar(shift3[:, v.slot, :], shift3[:, v.slot, :], -1.0, None, ALU.mult).then_inc(r_done, 1)

                def add_bias(v):
                    pool.wait_ge(XE_LD[v.slot], 16 * (v.round + 1))
                    g.tensor_tensor(xe[:, v.slot, :], xe[:, v.slot, :], bias[:, L, 0:D], ALU.add).then_inc(xe_b, 1)

                steps(pool, ET, [(fetch_third, 0), (fetch_residual, 1), (root_of, 5), (add_bias, 2)])

            @block.tensor
            def _(pe):
                pe.wait_ge(nb_zero, 1)

                def tally_w(v):
                    pe.wait_ge(hot_done, v.n + 1)
                    nc.tensor.matmul(pW[:, 0:COLS], hot_lo_f[:, v.two, :], hot_w[:, v.two, :], start=False, stop=False,
                                     skip_group_check=True).then_inc(w_tally, 1)

                steps(pe, NP, [(turn_pair(pe, L), 0), (multiply_pair(pe, L), 1), (sum_tile(pe, L), 0),
                               (turn_tile(pe, L), 1), (multiply_tile(pe, L), 2), (tally_w, 9)])

            @block.scalar
            def _(act):
                def keep_pair(v):
                    act.wait_ge(o_done, total(L, v) + 1)
                    at_least(act, n_done, v.n - RING + 1)
                    nc.scalar.activation(x2[:, v.slot, 0:2, :].rearrange("p s d -> p (s d)"), pO[v.two][:, :],
                                         ACT.Copy).then_inc(x2_done, 1)

                def add_eps(v):
                    act.wait_ge(mv_done, v.n + 1)
                    nc.scalar.activation(veps3[:, v.slot, :], mv3[:, v.slot, :, 1], ACT.Identity,
                                         bias=eps_t[:, 0:1]).then_inc(ve_done, 1)

                def normalise(v):
                    act.wait_ge(r_done, v.n + 1)
                    at_least(act, N_ST[v.slot], 16 * v.round)
                    at_least(act, NE_ST[v.slot], 16 * v.round)
                    at_least(act, hot_done, v.n - RING + 1)
                    for s in range(3):
                        last = nc.scalar.activation(nb[:, v.slot, s, 0:D], x2[:, v.slot, s, :], ACT.Identity,
                                                    bias=shift3[:, v.slot, s:s + 1], scale=rs3[:, v.slot, s:s + 1])
                    at_least(act, X_ST[v.slot], 16 * v.round)
                    at_least(act, OE_ST[v.slot], 16 * v.round)
                    for s in range(3):
                        last = nc.scalar.activation(x2n[:, v.slot, s, :], x2[:, v.slot, s, :], ACT.Identity,
                                                    bias=shift3[:, v.slot, s:s + 1], scale=one_rs3[:, v.slot, s:s + 1])
                    last.then_inc(n_done, 1)

                def weigh(v):
                    act.wait_ge(d_done, v.n + 1)
                    nc.scalar.activation(w_all[:, bass.ds(v.n * 2, 2)], dot3[:, v.slot, 0:2], ACT.Identity,
                                         bias=br_col[:, 0:1])
                    nc.scalar.activation(nb[:, v.slot, :, D], dot3[:, v.slot, :], ACT.Identity,
                                         bias=br_col[:, 0:1]).then_inc(w_done, 1)

                steps(act, NP, [(keep_pair, 3), (high_pair(act, L), 0), (add_eps, 5), (normalise, 6), (high_tile(act, L), 1),
                                (weigh, 7)])
                for s in range(RING):
                    act.wait_ge(X_ST[s], 16 * NP // RING)
                    act.wait_ge(N_ST[s], 16 * NP // RING)

            @block.vector
            def _(dve):
                v_ = nc.vector
                v_.memset(nb[:, :, :, :], 0.0)
                v_.tensor_copy(one_r[:, :], ones[:, :])
                v_.tensor_copy(bias_hi[:, :], bias[:, L, :]).then_inc(last_step, 1)
                dve.wait_ge(last_step, 1)
                v_.tensor_tensor(bias_mix[:, :], bias[:, L, :], bias_hi[:, :].bitcast(F32), ALU.subtract).then_inc(last_step, 1)
                dve.wait_ge(last_step, 2)
                v_.tensor_copy(bias_mix[0:1, :], bias_hi[0:1, :])
                v_.memset(pW[:, :], 0.0).then_inc(nb_zero, 1)
                dve.wait_ge(nb_zero, 1)

                def residual_tile(v):
                    dve.wait_ge(xe_b, v.n + 1)
                    at_least(dve, n_done, v.n - RING + 1)
                    dve.wait_ge(pz_done, total(L, v) + 1)
                    v_.scalar_tensor_tensor(out=x2[:, v.slot, 2, :], in0=pZ[:, 0:D], scalar=inv_dst[:, bass.ds(v.n, 1)],
                                            in1=xe[:, v.slot, :], op0=ALU.mult, op1=ALU.add).then_inc(x2e_done, 1)

                def statistics(v):
                    dve.wait_ge(x2_done, v.n + 1)
                    dve.wait_ge(x2e_done, v.n + 1)
                    for s in range(3):
                        last = v_.bn_stats(stats3[:, v.slot, s, :], x2[:, v.slot, s, :])
                    last.then_inc(st_done, 1)

                def aggregate(v):
                    alone(dve, st_done, v.n + 1)
                    for s in range(3):
                        last = v_.bn_aggr(mv3[:, v.slot, s, :], stats3[:, v.slot, s, :])
                    last.then_inc(mv_done, 1)

                def route(v):
                    dve.wait_ge(n_done, v.n + 1)
                    at_least(dve, w_done, v.n - RING + 1)
                    at_least(dve, d_done, v.n)
                    for s in range(3):
                        last = v_.scalar_tensor_tensor(out=junk[:, s, :], in0=nb[:, v.slot, s, 0:D], scalar=1.0,
                                                       in1=wr_row[:, :], op0=ALU.mult, op1=ALU.mult,
                                                       accum_out=dot3[:, v.slot, s:s + 1])
                    last.then_inc(d_done, 1)

                def spread_w(v):
                    dve.wait_ge(w_done, v.n + 1)
                    at_least(dve, w_tally, v.n - 1)
                    v_.tensor_scalar(hot_lo_f[:, v.two, :], iota_f[:, 0:P], lo_f[:, bass.ds(v.n, 1)], None, ALU.is_equal)
                    v_.tensor_scalar(hot_w[:, v.two, :], iota_f[:, :], hi_emit[:, bass.ds(v.n, 1)],
                                     nb[:, v.slot, 2, D:D + 1], ALU.is_equal, ALU.mult).then_inc(hot_done, 1)

                steps(dve, NP, [(add_own(dve, L), 1), (carry(dve, L), 0), (route, 7), (low_tile(dve, L), 2),
                                (low_pair(dve, L), 0), (statistics, 4), (residual_tile, 3), (spread_w, 8),
                                (aggregate, 4)])

        rings.close()
        with phase() as block:
            @block.gpsimd
            def _(pool):
                nc.clear_and_free_semaphores(semaphores)

        PASSED[0] = sem("passed_on")

        w_sel = sb("w_sel", [P, COLS])
        w_flag = sb("w_flag", [P, COLS], I32)
        least = sb("least", [P, COLS])
        node_f = sb("node_f", [P, COLS])
        bits = sb("bits", [P, 32], I32)
        shifts = sb("shifts", [P, 32], I32)
        heavier = sb("heavier", [P, COLS])
        equal = sb("equal", [P, COLS])
        pair_eq = sb("pair_eq", [P, NP])
        pair_tot = sb("pair_tot", [P, NP])
        pair_run = sb("pair_run", [P, NP])
        pair_one = sb("pair_one", [P, NP])
        rank = sb("rank", [P, NP, 2])
        need = sb("need", [P, 1])
        cnt = sb("cnt", [P, 1])
        best = sb("best", [P, 1], I32)
        cand = sb("cand", [P, 1], I32)
        flip = sb("flip", [P, 1], I32)
        thresh = sb("thresh", [P, 1], I32)
        enough = sb("enough", [P, 1], I32)
        keys = sb("keys", [P, COLS])
        turns_i = sb("turns_i", [P, 1], I32)
        BASE = K_SEL // (P * 8) + 1
        SPILL = 4
        REST = -(-COLS // 8) - BASE - SPILL
        ALL = BASE + SPILL + REST + 1
        lists = sb("lists", [P, ALL * 8])
        lists_i = sb("lists_i", [P, ALL * 8], I32)
        none = sb("none", [P, ALL * 8])
        spill_dram = dram("spill_dram", (2 * P * SPILL * 8,))
        spill = sb("spill", [P, SPILL * 8])
        spread = sb("spread", [P, SPILL * 8])
        top8 = sb("top8", [P, 8])
        counts = sb("counts", [P, 2])
        tallies = sb("tallies", [P, 3])
        tallies_i = sb("tallies_i", [P, 2], I32)
        ext_t = sb("ext_t", [P, 2, RING, D])
        idx_o = sb("idx_o", [P, 2 * RING], I32)
        f1_in = sb("f1_in", [P, KC, H])
        f1_hi = sb("f1_hi", [P, KC, H], F32R)
        f1_lo = sb("f1_lo", [P, KC, H], F32R)
        f2_in = sb("f2_in", [P, FH, D])
        f2_hi = sb("f2_hi", [P, FH, D], F32R)
        f2_lo = sb("f2_lo", [P, FH, D], F32R)
        fb1_col = sb("fb1_col", [P, FH])
        fb2_row = sb("fb2_row", [P, D])
        ask_i = sb("ask_i", [P, 2, RING], I32)
        put_i = sb("put_i", [P, 2, RING], I32)
        at_row = sb("at_row", [P, 2, RING], I32)
        nx = sb("nx", [P, 2, RING, DW])
        wq = sb("wq", [P, 2, RING])
        fx_hi = sb("fx_hi", [P, 2, KC, 4 * P], F32R)
        fx_lo = sb("fx_lo", [P, 2, KC, 4 * P], F32R)
        hid = sb("hid", [P, 2, 4 * P])
        hid_hi = sb("hid_hi", [P, 4, 4 * P], F32R)
        hid_lo = sb("hid_lo", [P, 4, 4 * P], F32R)
        y_sum = sb("y_sum", [P, 2, D])
        y = sb("y", [P, 2, RING, D])

        OX_LD, OI, OX_ST = sems("ox_ld"), sem("ox_i"), sems("ox_st")
        (f_got, f_split, c_step, c_cnt, c_tot, c_bits, c_ready, c_take, c_spill, c_spill_st, c_spread) = (sem(k) for k in (
            "f_got", "f_split", "c_step", "c_cnt", "c_tot", "c_bits", "c_ready", "c_take", "c_spill", "c_spill_st",
            "c_spread"))
        ext_quads = ext_out.rearrange("(g r p) d -> g p r d", r=RING, p=P)
        QUADS = ET // RING

        with phase() as block:
            @block.sync
            def _(sp):
                sp.dma_start(f1_in[:, :, :], w1.rearrange("(k p) n -> p k n", p=P)).then_inc(f_got, 16)
                sp.dma_start(f2_in[:, :, :], w2.rearrange("(k p) n -> p k n", p=P)).then_inc(f_got, 16)
                with nc.allow_non_contiguous_dma(reason="a bias to columns"):
                    sp.dma_start(fb1_col[:, :], fb1.rearrange("(k p) -> p k", p=P)).then_inc(f_got, 16)
                sp.dma_start(fb2_row[:, :], fb2.rearrange("(o n) -> o n", o=1).to_broadcast([P, D])).then_inc(f_got, 16)
                for q in range(2):
                    sp.dma_start(ext_t[:, q, :, :], ext_quads[q]).then_inc(OX_LD[q], 16)
                with sp.Fori(1, QUADS // 2) as two:
                    for q in range(2):
                        sp.wait_ge(OX_ST[q], two * 16 * RING)
                        sp.dma_start(ext_t[:, q, :, :], ext_quads[two * 2 + q]).then_inc(OX_LD[q], 16)
                if QUADS % 2:
                    sp.wait_ge(OX_ST[0], QUADS // 2 * 16 * RING)
                    sp.dma_start(ext_t[:, 0, :, :], ext_quads[QUADS - 1]).then_inc(OX_LD[0], 16)

            @block.scalar
            def _(act):
                act.wait_ge(f_got, 16 * 4)
                nc.scalar.activation(f1_hi[:, :, :].rearrange("p k n -> p (k n)"),
                                     f1_in[:, :, :].rearrange("p k n -> p (k n)"), ACT.Copy).then_inc(f_split, 1)
                nc.scalar.activation(f2_hi[:, :, :].rearrange("p k n -> p (k n)"),
                                     f2_in[:, :, :].rearrange("p k n -> p (k n)"), ACT.Copy).then_inc(f_split, 1)
                SW = SPILL * 8
                act.wait_ge(c_spill, 1)
                for half in range(2):
                    act.dma_start(spill_dram[half * P * SW:(half + 1) * P * SW].rearrange("(p r) -> p r", r=SW),
                                  spill[:, :]).then_inc(c_spill_st, 16)
                act.wait_ge(c_spill_st, 32)
                diagonal = bass.AP(tensor=spill_dram.tensor, offset=spill_dram.offset, ap=[[SW, P], [SW + 1, SW]])
                with nc.allow_non_contiguous_dma(reason="a few thousand spilled keys"):
                    act.dma_start(spread[:, :], diagonal).then_inc(c_spread, 16)

            @block.gpsimd
            def _(pool):
                g = nc.gpsimd
                g.memset(bits[:, :], 1).then_inc(c_bits, 1)
                g.iota(shifts[:, :], pattern=[[-1, 32]], base=31, channel_multiplier=0).then_inc(c_bits, 1)

                def put_quad(q, uses, n):
                    pool.wait_ge(OX_LD[q], (uses + 1) * 16)
                    if not isinstance(uses, int) or uses:
                        pool.wait_ge(OX_ST[q], uses * 16 * RING)
                    for r in range(RING):
                        slot = q * RING + r
                        g.tensor_copy(idx_o[:, slot:slot + 1], emit_i[:, bass.ds(n * RING + r, 1)]).then_inc(OI, 1)
                    alone(pool, OI, (n + 1) * RING)
                    for r in range(RING):
                        slot = q * RING + r
                        g.indirect_dma_start(out=out, out_offset=bass.IndirectOffsetOnAxis(ap=idx_o[:, slot:slot + 1], axis=0),
                                             in_=ext_t[:, q, r, :], in_offset=None, bounds_check=N - 1,
                                             oob_is_err=False).then_inc(OX_ST[q], 16)

                for q in range(2):
                    put_quad(q, 0, q)
                with pool.Fori(1, QUADS // 2) as two:
                    for q in range(2):
                        put_quad(q, two, two * 2 + q)
                if QUADS % 2:
                    put_quad(0, QUADS // 2, QUADS - 1)
                for q in range(2):
                    pool.wait_ge(OX_ST[q], (QUADS + 1 - q) // 2 * 16 * RING)

            @block.tensor
            def _(pe):
                t_ = nc.tensor
                with pe.Fori(0, 32) as b:
                    pe.wait_ge(c_cnt, b + 1)
                    t_.matmul(pS[:, 0:1], ones[:, :], cnt[:, 0:1], start=True, stop=True).then_inc(c_tot, 1)
                pe.wait_ge(c_cnt, 33)
                t_.matmul(pS[:, 0:1], ones[:, :], cnt[:, 0:1], start=True, stop=True)
                t_.matmul(pE[:, 0:NP], below[:, :], pair_eq[:, :], start=True, stop=True)
                t_.matmul(pZ[:, 0:NP], ones[:, :], pair_eq[:, :], start=True, stop=True).then_inc(c_tot, 1)
                pe.wait_ge(c_cnt, 34)
                for k in range(2):
                    last = t_.transpose(pT[0][0:1, k * P:(k + 1) * P], counts[:, k:k + 1], ident[:, :])
                last.then_inc(c_tot, 1)

            @block.vector
            def _(dve):
                v_ = nc.vector
                count = [0]

                def link(ins):
                    count[0] += 1
                    ins.then_inc(c_step, 1)
                    dve.wait_ge(c_step, count[0])

                dve.wait_ge(c_bits, 2)
                link(v_.tensor_tensor(bits[:, :], bits[:, :], shifts[:, :], ALU.logical_shift_left))
                v_.memset(best[:, :], 0)
                v_.memset(least[:, :], -3.0e38)
                v_.memset(pair_one[:, :], 1.0)
                v_.tensor_copy(node_f[:, :], node_i[:, :])
                v_.tensor_copy(w_sel[:, :], w_all[:, :])
                link(v_.tensor_scalar(w_flag[:, :], root[:, :], 1.5, None, ALU.is_ge))
                link(v_.copy_predicated(w_sel[:, :], w_flag[:, :], pW[:, 0:COLS]))
                link(v_.tensor_scalar(w_flag[:, :], node_f[:, :], float(N), None, ALU.is_gt))
                link(v_.copy_predicated(w_sel[:, :], w_flag[:, :], least[:, :]))

                def as_float():
                    yield v_.tensor_scalar(flip[:, :], cand[:, :], 31, -1, ALU.arith_shift_right, ALU.bitwise_xor)
                    yield v_.tensor_scalar(flip[:, :], flip[:, :], -2147483648, None, ALU.bitwise_or)
                    yield v_.tensor_tensor(thresh[:, :], cand[:, :], flip[:, :], ALU.bitwise_xor)

                SEARCH = 5
                with dve.Fori(0, 32) as b:
                    before = b * SEARCH + count[0]
                    v_.tensor_tensor(cand[:, :], best[:, :], bits[:, bass.ds(b, 1)], ALU.bitwise_or).then_inc(c_step, 1)
                    alone(dve, c_step, before + 1)
                    for k, ins in enumerate(as_float()):
                        ins.then_inc(c_step, 1)
                        alone(dve, c_step, before + 2 + k)
                    v_.tensor_scalar(heavier[:, :], w_sel[:, :], thresh[:, 0:1].bitcast(F32), 0.0, ALU.is_ge, ALU.add,
                                     accum_out=cnt[:, 0:1]).then_inc(c_cnt, 1)
                    alone(dve, c_tot, b + 1)
                    v_.tensor_scalar(enough[:, :], pS[:, 0:1], float(K_SEL), None, ALU.is_ge).then_inc(c_ready, 1)
                    alone(dve, c_ready, b + 1)
                    v_.copy_predicated(best[:, :], enough[:, :], cand[:, :]).then_inc(c_step, 1)
                    alone(dve, c_step, before + SEARCH)
                count[0] += 32 * SEARCH
                link(v_.tensor_copy(cand[:, :], best[:, :]))
                for ins in as_float():
                    link(ins)
                v_.tensor_scalar(heavier[:, :], w_sel[:, :], thresh[:, 0:1].bitcast(F32), 0.0, ALU.is_gt, ALU.add,
                                 accum_out=cnt[:, 0:1])
                link(v_.tensor_scalar(equal[:, :], w_sel[:, :], thresh[:, 0:1].bitcast(F32), None, ALU.is_equal))
                eq3 = equal[:, :].rearrange("p (j s) -> p j s", s=2)
                v_.tensor_tensor(pair_eq[:, :], eq3[:, :, 0], eq3[:, :, 1], ALU.add).then_inc(c_cnt, 1)
                dve.wait_ge(c_tot, 33)
                v_.tensor_scalar(need[:, :], pS[:, 0:1], -1.0, float(K_SEL), ALU.mult, ALU.add)
                link(v_.tensor_copy(pair_tot[:, :], pZ[:, 0:NP]))
                link(v_.tensor_tensor_scan(pair_run[:, :], pair_one[:, :], pair_tot[:, :], 0.0, ALU.mult, ALU.add))
                link(v_.tensor_tensor(pair_run[:, :], pair_run[:, :], pair_tot[:, :], ALU.subtract))
                link(v_.tensor_tensor(rank[:, :, 0], pair_run[:, :], pE[:, 0:NP], ALU.add))
                link(v_.tensor_tensor(rank[:, :, 1], rank[:, :, 0], eq3[:, :, 0], ALU.add))
                rank2 = rank[:, :, :].rearrange("p j s -> p (j s)")
                link(v_.tensor_scalar(rank2, rank2, need[:, 0:1], None, ALU.is_lt))
                link(v_.tensor_tensor(equal[:, :], equal[:, :], rank2, ALU.mult))
                link(v_.tensor_tensor(heavier[:, :], heavier[:, :], equal[:, :], ALU.add))
                link(v_.tensor_tensor(keys[:, :], heavier[:, :], node_f[:, :], ALU.mult))
                with dve.Fori(0, BASE) as t:
                    v_.max(top8[:, :], keys[:, :]).then_inc(c_take, 1)
                    alone(dve, c_take, t * 2 + 1)
                    v_.tensor_copy(lists[:, bass.ds(t * 8, 8)], top8[:, :])
                    v_.match_replace(keys[:, :], top8[:, :], keys[:, :], 0.0).then_inc(c_take, 1)
                    alone(dve, c_take, t * 2 + 2)
                for k in range(SPILL):
                    link(v_.max(spill[:, k * 8:(k + 1) * 8], keys[:, :]))
                    link(v_.match_replace(keys[:, :], spill[:, k * 8:(k + 1) * 8], keys[:, :], 0.0))
                dve.sem_inc(c_spill, 1)
                v_.memset(nx[:, :, :, :], 0.0)
                v_.memset(at_row[:, :, :], 0)
                dve.wait_ge(f_split, 2)
                v_.tensor_tensor(f1_lo[:, :, :], f1_in[:, :, :], f1_hi[:, :, :].bitcast(F32), ALU.subtract)
                v_.tensor_tensor(f2_lo[:, :, :], f2_in[:, :, :], f2_hi[:, :, :].bitcast(F32), ALU.subtract)
                dve.wait_ge(c_spread, 16)
                link(v_.tensor_scalar(equal[:, :], keys[:, :], 0.0, 0.0, ALU.is_gt, ALU.add, accum_out=counts[:, 0:1]))
                v_.tensor_scalar(equal[:, 0:SPILL * 8], spread[:, :], 0.0, 0.0, ALU.is_gt, ALU.add,
                                 accum_out=counts[:, 1:2]).then_inc(c_cnt, 1)
                dve.wait_ge(c_tot, 34)
                for k in range(2):
                    last = v_.reduce_max(tallies[0:1, k:k + 1], pT[0][0:1, k * P:(k + 1) * P], axis=AX_X)
                link(last)
                link(v_.tensor_scalar(tallies_i[0:1, 0:2], tallies[0:1, 0:2], 7.0, None, ALU.add))
                link(v_.tensor_scalar(tallies_i[0:1, 0:2], tallies_i[0:1, 0:2], 3, None, ALU.logical_shift_right))
                link(v_.tensor_copy(tallies[0:1, 0:2], tallies_i[0:1, 0:2]))
                v_.tensor_tensor(tallies[0:1, 2:3], tallies[0:1, 0:1], tallies[0:1, 1:2], ALU.add).then_inc(c_cnt, 1)
                dve.wait_ge(c_cnt, 35)
                link(v_.tensor_scalar(turns_i[0:1, :], tallies[0:1, 2:3], float(BASE - 1), None, ALU.add))
                v_.memset(lists[:, BASE * 8:], 0.0)
                link(v_.memset(top8[:, :], 0.0))
                spread_turns = dve.value_load(tallies_i[0:1, 1:2], min_val=0, max_val=SPILL)
                rest_turns = dve.value_load(tallies_i[0:1, 0:1], min_val=0, max_val=REST)
                taken = BASE * 2
                for k in range(SPILL):
                    link(v_.max(lists[:, (BASE + k) * 8:(BASE + k + 1) * 8], spread[:, :]))
                    link(v_.match_replace(spread[:, :], lists[:, (BASE + k) * 8:(BASE + k + 1) * 8], spread[:, :], 0.0))
                with dve.If(rest_turns > 0):
                    with dve.Fori(0, rest_turns) as t:
                        v_.max(top8[:, :], keys[:, :]).then_inc(c_take, 1)
                        alone(dve, c_take, t * 2 + (taken + 1))
                        v_.tensor_copy(lists[:, bass.ds((t + spread_turns) * 8 + BASE * 8, 8)], top8[:, :])
                        v_.match_replace(keys[:, :], top8[:, :], keys[:, :], 0.0).then_inc(c_take, 1)
                        alone(dve, c_take, t * 2 + (taken + 2))
                link(v_.tensor_scalar(none[:, :], lists[:, :], 0.0, float(FAR), ALU.is_equal, ALU.mult))
                v_.scalar_tensor_tensor(out=lists_i[:, :], in0=lists[:, :], scalar=-1.0, in1=none[:, :],
                                        op0=ALU.add, op1=ALU.add)

        QR = 4 * P
        NX_LD, RO_LD, Y_ST = [sem("nx_ld0"), sem("nx_ld1")], [sem("ro_ld0"), sem("ro_ld1")], [sem("y_st0"), sem("y_st1")]
        (q_idx, q_put, x_turned, x_hi, x_lo, l1_done, act_done, hh_done, hl_done, l2_done, y_add,
         y_done) = (sem(k) for k in ("q_idx", "q_put", "x_turned", "x_hi", "x_lo",
                                     "l1_done", "act_done", "hh_done", "hl_done", "l2_done", "y_add", "y_done"))
        pA = [pS, pE]
        pY = [[pO[0], pO[1]], [pZ, pW]]
        CH = 2 * FH
        Y_FREE = [sem("y_free0"), sem("y_free1")]
        MIN_TURNS, MAX_TURNS = BASE, BASE + SPILL + REST

        def turns(eng, body):
            n = eng.value_load(turns_i[0:1, 0:1], min_val=MIN_TURNS - 1, max_val=MAX_TURNS - 1)
            body(0)
            with eng.Fori(0, n) as t:
                body(t + 1)
            return n

        with phase() as block:
            @block.gpsimd
            def _(pool):
                g = nc.gpsimd

                def fetch(t, k):
                    if not (isinstance(t, int) and t == 0):
                        alone(pool, Y_ST[k], (t - 1) * 16 * RING)
                        pool.sem_inc(Y_FREE[k], 1)
                        g.tensor_copy(put_i[:, k, :], ask_i[:, k, :]).then_inc(q_put, 1)
                        alone(pool, q_put, (t - 1) * 2 + k + 1)
                    g.tensor_copy(ask_i[:, k, :], lists_i[:, bass.ds(t * 8 + k * RING, RING)]).then_inc(q_idx, 1)
                    alone(pool, q_idx, t * 2 + k + 1)
                    for r in range(RING):
                        g.indirect_dma_start(out=at_row[:, k, r:r + 1], out_offset=None, in_=row_of,
                                             in_offset=bass.IndirectOffsetOnAxis(ap=ask_i[:, k, r:r + 1], axis=0),
                                             bounds_check=EXT - 1, oob_is_err=False).then_inc(RO_LD[k], 16)
                    alone(pool, RO_LD[k], (t + 1) * 16 * RING)
                    if not (isinstance(t, int) and t == 0):
                        alone(pool, x_lo, t * 2 + k - 1)
                    for r in range(RING):
                        g.indirect_dma_start(out=nx[:, k, r, :], out_offset=None, in_=normed,
                                             in_offset=bass.IndirectOffsetOnAxis(ap=at_row[:, k, r:r + 1], axis=0)
                                             ).then_inc(NX_LD[k], 16)

                def put(t, k):
                    for r in range(RING):
                        alone(pool, y_done, (t * 2 + k) * RING + r + 1)
                        g.indirect_dma_start(out=out, out_offset=bass.IndirectOffsetOnAxis(ap=put_i[:, k, r:r + 1], axis=0),
                                             in_=y[:, k, r, :], in_offset=None, bounds_check=N - 1, oob_is_err=False,
                                             compute_op=ALU.add).then_inc(Y_ST[k], 16)

                for k in range(2):
                    fetch(0, k)

                def turn_body(t):
                    for k in range(2):
                        fetch(t + 1, k)
                        put(t, k)

                last_turn = turns(pool, turn_body)
                for k in range(2):
                    pool.wait_ge(Y_ST[k], (last_turn + 1) * (16 * RING))
                    pool.wait_ge(NX_LD[k], (last_turn + 2) * (16 * RING))

            @block.tensor
            def _(pe):
                t_ = nc.tensor

                def turn_rows(t, k):
                    q = t * 2 + k
                    pe.wait_ge(NX_LD[k], (t + 1) * 16 * RING)
                    at_least(pe, x_lo, q)
                    for c in range(KC):
                        for r in range(RING):
                            last = t_.transpose(pT[c][:, r * P:(r + 1) * P], nx[:, k, r, c * P:(c + 1) * P], ident[:, :])
                    last.then_inc(x_turned, 1)

                def hidden(t, k, f):
                    c = t * CH + k * FH + f
                    if f == 0:
                        pe.wait_ge(x_lo, t * 2 + k + 1)
                    at_least(pe, act_done, c - 1)
                    u = slice(f * P, (f + 1) * P)
                    for i in range(KC):
                        t_.matmul(pA[f % 2][:, :], f1_hi[:, i, u], fx_hi[:, k, i, :], start=(i == 0), stop=False)
                        t_.matmul(pA[f % 2][:, :], f1_lo[:, i, u], fx_hi[:, k, i, :], start=False, stop=False)
                        last = t_.matmul(pA[f % 2][:, :], f1_hi[:, i, u], fx_lo[:, k, i, :], start=False, stop=(i == KC - 1))
                    last.then_inc(l1_done, 1)

                def output(t, k, f):
                    c = t * CH + k * FH + f
                    pe.wait_ge(hl_done, c + 1)
                    if f == 0:
                        at_least(pe, y_add, (t * 2 + k - 1) * RING)
                    for r in range(RING):
                        bank = pY[k][r // 2][:, (r % 2) * D:(r % 2 + 1) * D]
                        rr = slice(r * P, (r + 1) * P)
                        s = f % 4
                        last_f = f == FH - 1
                        t_.matmul(bank, hid_hi[:, s, rr], f2_hi[:, f, :], start=(f == 0 and r % 2 == 0), stop=False,
                                  skip_group_check=True)
                        t_.matmul(bank, hid_lo[:, s, rr], f2_hi[:, f, :], start=False, stop=False, skip_group_check=True)
                        last = t_.matmul(bank, hid_hi[:, s, rr], f2_lo[:, f, :], start=False, stop=last_f,
                                         skip_group_check=True)
                    last.then_inc(l2_done, 1)

                turn_rows(0, 0)

                def turn_body(t):
                    for k in range(2):
                        for f in range(FH):
                            hidden(t, k, f)
                            if f == FH // 2:
                                turn_rows(t + k, 1 - k)
                            if f >= 2:
                                output(t, k, f - 2)
                            elif k:
                                output(t, 0, FH - 2 + f)
                            elif not isinstance(t, int):
                                output(t - 1, 1, FH - 2 + f)

                last_turn = turns(pe, turn_body)
                for f in range(FH - 2, FH):
                    output(last_turn, 1, f)

            @block.scalar
            def _(act):
                nc.scalar.preload_act_table(ACT.Gelu_apprx_tanh)

                def high_rows(t, k):
                    act.wait_ge(x_turned, t * 2 + k + 1)
                    for c in range(KC):
                        last = nc.scalar.activation(fx_hi[:, k, c, :], pT[c][:, :], ACT.Copy)
                    last.then_inc(x_hi, 1)

                def gelu(t, k, f):
                    c = t * CH + k * FH + f
                    act.wait_ge(l1_done, c + 1)
                    at_least(act, hl_done, c - 1)
                    nc.scalar.activation(hid[:, f % 2, :], pA[f % 2][:, :], ACT.Gelu_apprx_tanh,
                                         bias=fb1_col[:, f:f + 1]).then_inc(act_done, 1)
                    act.wait_ge(act_done, c + 1)
                    at_least(act, l2_done, c - 3)
                    nc.scalar.activation(hid_hi[:, f % 4, :], hid[:, f % 2, :], ACT.Copy).then_inc(hh_done, 1)

                high_rows(0, 0)

                def turn_body(t):
                    for k in range(2):
                        for f in range(FH):
                            gelu(t, k, f)
                            if f == FH // 2:
                                high_rows(t + k, 1 - k)

                turns(act, turn_body)

            @block.vector
            def _(dve):
                v_ = nc.vector

                def low_rows(t, k):
                    q = t * 2 + k
                    dve.wait_ge(x_hi, q + 1)
                    for c in range(KC):
                        v_.tensor_tensor(fx_lo[:, k, c, :], pT[c][:, :], fx_hi[:, k, c, :].bitcast(F32), ALU.subtract)
                    at_least(dve, y_done, (q - 1) * RING)
                    v_.tensor_copy(wq[:, k, :], nx[:, k, :, D]).then_inc(x_lo, 1)

                def low_hidden(t, k, f):
                    c = t * CH + k * FH + f
                    dve.wait_ge(hh_done, c + 1)
                    v_.tensor_tensor(hid_lo[:, f % 4, :], hid[:, f % 2, :], hid_hi[:, f % 4, :].bitcast(F32),
                                     ALU.subtract).then_inc(hl_done, 1)

                def weigh(t, k):
                    q = t * 2 + k
                    dve.wait_ge(l2_done, (q + 1) * FH)
                    dve.wait_ge(Y_FREE[k], t + 1)
                    for r in range(RING):
                        bank = pY[k][r // 2][:, (r % 2) * D:(r % 2 + 1) * D]
                        v_.tensor_tensor(y_sum[:, r % 2, :], bank, fb2_row[:, :], ALU.add).then_inc(y_add, 1)
                        alone(dve, y_add, q * RING + r + 1)
                        v_.tensor_scalar(y[:, k, r, :], y_sum[:, r % 2, :], wq[:, k, r:r + 1], None,
                                         ALU.mult).then_inc(y_done, 1)

                low_rows(0, 0)

                def turn_body(t):
                    for k in range(2):
                        for f in range(FH):
                            low_hidden(t, k, f)
                            if f == 2:
                                if k:
                                    weigh(t, 0)
                                elif not isinstance(t, int):
                                    weigh(t - 1, 1)
                            if f == FH // 2:
                                low_rows(t + k, 1 - k)

                last_turn = turns(dve, turn_body)
                weigh(last_turn, 1)


_INS = ['x', 'src', 'dst', 'L0_gnn_W1', 'L0_gnn_b1', 'L0_gnn_W2', 'L0_gnn_b2', 'L0_gnn_W3', 'L0_gnn_b3',
        'L0_ffn_wr', 'L0_ffn_br', 'L0_ffn_w1', 'L0_ffn_b1', 'L0_ffn_w2', 'L0_ffn_b2']


def kernel(**inputs):
    import numpy as _np
    import concourse.bacc as _bacc
    from concourse import mybir as _mybir
    from concourse.bass_utils import run_bass_kernel_spmd as _run

    nc = _bacc.Bacc("TRN2", target_bir_lowering=False, num_devices=1)
    arrays, args = {}, []
    for name in _INS:
        a = _np.ascontiguousarray(inputs[name])
        arrays[f"in_{name}_dram"] = a
        args.append(nc.dram_tensor(f"in_{name}_dram", a.shape, _mybir.dt.from_np(a.dtype), kind="ExternalInput").ap())
    args.append(nc.dram_tensor("out_0_dram", inputs['x'].shape, _mybir.dt.float32, kind="ExternalOutput").ap())
    gnn_ffn(nc, *args)
    r = _run(nc, [arrays], core_ids=[0])
    return r.results[0]["out_0_dram"]
```

```python
from contextlib import ExitStack

import concourse.bass as bass
from concourse import mybir

ALU = mybir.AluOpType
ACT = mybir.ActivationFunctionType
AX_X = mybir.AxisListType.X
F32 = mybir.dt.float32
F32R = mybir.dt.float32r
F16 = mybir.dt.float16
I32 = mybir.dt.int32
RMAX = bass.bass_isa.ReduceOp.max

P = 128
RING = 4
WARM = 12
EPS = 1e-5
FAR = 1 << 20


class At:

    def __init__(self, group, off):
        self.n = group * RING + off
        self.slot = off % RING
        self.two = off % 2
        self.round = group + off // RING


def steps(eng, count, stages, peel=0):
    stages = [s if len(s) == 3 else (*s, None) for s in stages]

    def one(group, off, static):
        for stage, lag, only in stages:
            if only is not None and (off - lag) % RING != only:
                continue
            if static and not 0 <= off - lag < count:
                continue
            stage(At(group, off - lag))

    for v in range(WARM):
        one(0, v, True)
    with eng.Fori(WARM // RING, count // RING - peel) as group:
        for off in range(RING):
            one(group, off, False)
    lags = max(lag for _, lag, _ in stages)
    for v in range(count - RING * peel, count + lags):
        one(0, v, True)


def at_least(eng, sem, value):
    if not isinstance(value, int) or value > 0:
        eng.wait_ge(sem, value)


def alone(eng, sem, value):
    if not isinstance(value, int):
        eng.wait_ge(sem, value)
        eng.sem_inc(PASSED[0], 1)
    elif value > 0:
        eng.wait_ge(sem, value)


PASSED = [None]


def gnn_ffn(nc, x, src, dst, W1, b1, W2, b2, W3, b3, wr, br, w1, fb1, w2, fb2, out):
    N, D = x.shape
    E = src.shape[0]
    H = w1.shape[1]
    K_SEL = N // 2 - 1
    ET = -(-E // P)
    NP = -(-N // (2 * P))
    EXT = NP * 2 * P
    ROWS = EXT + ET * P
    COLS = 2 * NP
    HC = COLS // 4
    LAST_P = (N - (NP - 1) * 2 * P) // 2
    TC = ET // 2
    LAST_E = E - (ET - 1) * P
    KC = D // P
    FH = H // P
    DW = D + 8
    PAD_DST = 70000
    assert D == 256 and ET == NP and ET % RING == 0 and TC % 2 == 0 and COLS <= 512 and PAD_DST > ROWS - ET * P

    with ExitStack() as ctx:
        def sb(name, shape, dt=F32):
            return ctx.enter_context(nc.sbuf_tensor(name, shape, dt))

        def pb(name, shape=(P, 512), dt=F32):
            return ctx.enter_context(nc.psum_tensor(name, list(shape), dt))

        semaphores = []

        def sem(name):
            semaphores.append(nc.alloc_semaphore(name=name))
            return semaphores[-1]

        def sems(name):
            return [sem(f"{name}{i}") for i in range(RING)]

        def dram(name, shape, dt=F32):
            return nc.dram_tensor(name, shape, dt, kind="Internal").ap()

        rows = [dram(f"rows{l}", (ROWS if l else EXT, D)) for l in range(3)]
        normed = dram("normed", (ROWS, DW))
        ext_out = dram("ext_out", (ET * P, D))
        same_dram = dram("same_dram", (ET, P, P))
        turned_dst = dram("turned_dst", (ET, P))
        inv_root = dram("inv_root", (COLS * P, 1))
        row_of = dram("row_of", (EXT, 1), I32)
        edge_src2 = dram("edge_src", (E, 1), I32)
        edge_dst2 = dram("edge_dst", (E, 1), I32)
        edge_src, edge_dst = (a.rearrange("e o -> (e o)") for a in (edge_src2, edge_dst2))

        ident = sb("ident", [P, P])
        turn = sb("turn", [P, P])
        ones = sb("ones", [P, P])
        iota_p16 = sb("iota_p16", [P, P], F16)
        iota_c16 = sb("iota_c16", [P, COLS], F16)
        iota_i = sb("iota_i", [P, COLS], I32)
        node_i = sb("node_i", [P, COLS], I32)
        ext_id = sb("ext_id", [P, ET], I32)
        lin_id = sb("lin_id", [P, COLS], I32)
        eps_t = sb("eps_t", [P, 1])
        half = sb("half", [P, COLS])

        nat_i = sb("nat_i", [P, 3, 2, P], I32)
        prev_i = sb("prev_i", [P, 2], I32)
        nat_f = sb("nat_f", [P, 4, 2, P])
        nat_next = sb("nat_next", [P, 2, P])
        prev_f = sb("prev_f", [P, 2])
        turned = sb("turned", [P, 4, ET])
        src_i = sb("src_i", [P, ET], I32)
        emit_i = sb("emit_i", [P, ET], I32)
        dst_i = sb("dst_i", [P, ET], I32)
        dst_safe = sb("dst_safe", [P, ET], I32)
        tile_ids = sb("tile_ids", [P, ET, 4], I32)
        lo_i = sb("lo_i", [P, ET], I32)
        hi_i = sb("hi_i", [P, ET], I32)
        odd_i = sb("odd_i", [P, ET], I32)
        lo_f = sb("lo_f", [P, ET])
        hi_f = sb("hi_f", [P, ET])
        table_i = sb("table_i", [P, ET], I32)
        table_f = sb("table_f", [P, ET])
        hot_lo = sb("hot_lo", [P, RING, P], F16)
        hot_hi = sb("hot_hi", [P, RING, COLS], F16)
        back = sb("back", [P, 2, P])
        root = sb("root", [P, COLS])
        inv = sb("inv", [P, COLS])
        inv_t = sb("inv_t", [P, 4, P])
        inv_dst = sb("inv_dst", [P, ET])

        w_all = sb("w_all", [P, 3 * NP])

        rings = ctx.enter_context(ExitStack())

        def ring(name, shape, dt=F32):
            return rings.enter_context(nc.sbuf_tensor(name, shape, dt))

        xin = ring("xin", [P, RING, 2 * D])
        gout = ring("gout", [P, RING, 2 * D])
        stats = ring("stats", [P, RING, 2, 6])
        mv = ring("mv", [P, RING, 2, 2])
        veps = ring("veps", [P, RING, 2])
        rstd = ring("rstd", [P, RING, 2])
        rs = ring("rs", [P, RING, 2])
        dst_row = ring("dst_row", [P, RING * P])
        same_out = ring("same_out", [P, RING, P])
        idx_a = ring("idx_a", [P, RING], I32)
        got_a = ring("got_a", [P, RING])

        w_in = ring("w_in", [P, KC, D])
        w_hi = ring("w_hi", [P, 3, KC, D], F32R)
        w_lo = ring("w_lo", [P, 3, KC, D], F32R)
        bias = ring("bias", [P, 3, 2 * D])
        wr_row = ring("wr_row", [P, D])
        br_col = ring("br_col", [P, 1])
        xt_hi = ring("xt_hi", [P, 2, 2, KC, P], F32R)
        xt_lo = ring("xt_lo", [P, 2, 2, KC, P], F32R)
        zb = ring("zb", [P, 2, 2 * D])
        same_t = ring("same_t", [P, RING, P])
        ids_now = ring("ids_now", [P, RING, 4], I32)
        ids_flat = tile_ids[:, :, :].rearrange("p t k -> p (t k)")
        idx_m = ring("idx_m", [P, RING], I32)
        idx_s = ring("idx_s", [P, RING], I32)
        idx_r = ring("idx_r", [P, RING], I32)
        got_r = ring("got_r", [P, RING], I32)
        src_row = ring("src_row", [P, ET], I32)
        msg = ring("msg", [P, RING, D])
        own = ring("own", [P, RING, D])
        tot = ring("tot", [P, 2, D])
        et_hi = ring("et_hi", [P, 2, KC, P], F32R)
        et_lo = ring("et_lo", [P, 2, KC, P], F32R)
        ez = ring("ez", [P, 2, D])
        eh = ring("eh", [P, 2, D])
        eo = ring("eo", [P, RING, D])

        xres = ring("xres", [P, RING, 2 * D])
        xe = ring("xe", [P, RING, D])
        x2 = ring("x2", [P, RING, 3, D])
        stats3 = ring("stats3", [P, RING, 3, 6])
        mv3 = ring("mv3", [P, RING, 3, 2])
        veps3 = ring("veps3", [P, RING, 3])
        rs3 = ring("rs3", [P, RING, 3])
        one_rs3 = ring("one_rs3", [P, RING, 3])
        shift3 = ring("shift3", [P, RING, 3])
        nb = ring("nb", [P, RING, 3, DW])
        x2n = ring("x2n", [P, RING, 3, D])
        dot3 = ring("dot3", [P, RING, 3])
        junk = ring("junk", [P, 3, D])
        one_r = ring("one_r", [P, P], F32R)
        bias_hi = ring("bias_hi", [P, 2 * D], F32R)
        bias_mix = ring("bias_mix", [P, 2 * D], F32R)

        pT = [pb("pT0"), pb("pT1")]
        pO = [pb("pO0"), pb("pO1")]
        pS, pE, pZ, pW = pb("pS"), pb("pE"), pb("pZ"), pb("pW")

        PASSED[0] = sem("passed")
        s_const = sem("s_const")
        s_pad = sem("s_pad")
        s_nat = sem("s_nat")
        s_pro = sem("s_pro")
        s_flip = sem("s_flip")
        s_flipped = sem("s_flipped")
        s_back = sem("s_back")
        s_turned_st = sem("s_turned_st")
        s_hot = sem("s_hot")
        s_count = sem("s_count")
        s_root = sem("s_root")
        s_inv_t = sem("s_inv_t")
        s_inv_st = sem("s_inv_st")
        s_lin = sem("s_lin")

        def phase():
            return nc.Block()

        EC = next(c for c in range(-(-E // P), E + 1) if E % c == 0)
        EP = E // EC
        CHUNK = next(c for c in range(700, 0, -1) if E % c == 0)
        sort_mem = ctx.enter_context(ExitStack())

        def tmp(name, shape, dt=F32):
            return sort_mem.enter_context(nc.sbuf_tensor(name, shape, dt))

        e_src, e_dst, e_next = tmp("e_src", [P, EC], I32), tmp("e_dst", [P, EC], I32), tmp("e_next", [P, EC], I32)
        e_dst_f, e_next_f, e_number = tmp("e_dst_f", [P, EC]), tmp("e_next_f", [P, EC]), tmp("e_number", [P, EC])
        e_number_i = tmp("e_number_i", [P, EC], I32)
        falls = tmp("falls", [P, 1])
        unsorted_i = tmp("unsorted_i", [P, 1], I32)
        all_one = tmp("all_one", [P, P])
        rank_f, rank_i = tmp("rank_f", [P, EC]), tmp("rank_i", [P, EC], I32)
        other_i, other_n = tmp("other_i", [P, CHUNK], I32), tmp("other_n", [P, CHUNK], I32)
        other_f, other_nf = tmp("other_f", [P, CHUNK]), tmp("other_nf", [P, CHUNK])
        less, before_it = tmp("less", [P, CHUNK]), tmp("before_it", [P, CHUNK])
        n_less, n_same = tmp("n_less", [P, 1]), tmp("n_same", [P, 1])
        put_at = tmp("put_at", [P, 1], I32)
        put_src, put_dst = tmp("put_src", [P, 1], I32), tmp("put_dst", [P, 1], I32)
        (u_copy, u_ld, u_set, u_step, u_sum, u_ready, o_ld, o_num, o_ready, o_used, u_rank, u_pos, u_put) = (
            sem(k) for k in ("u_copy", "u_ld", "u_set", "u_step", "u_sum", "u_ready", "o_ld", "o_num", "o_ready",
                             "o_used", "u_rank", "u_pos", "u_put"))

        with phase() as block:
            @block.sync
            def _(sp):
                def line(a, n):
                    return a.rearrange("(o n) -> o n", o=1)[:, 0:n]

                sp.dma_start(e_dst[0:EP, :], dst.rearrange("(p c) -> p c", c=EC)).then_inc(u_ld, 16)
                sp.wait_ge(u_set, 1)
                sp.dma_start(e_next[0:EP - 1, :], dst[1:E - EC + 1].rearrange("(p c) -> p c", c=EC)).then_inc(u_ld, 16)
                sp.dma_start(e_next[EP - 1:EP, 0:EC - 1], line(dst[E - EC + 1:E], EC - 1)).then_inc(u_ld, 16)
                sp.dma_start(e_src[0:EP, :], src.rearrange("(p c) -> p c", c=EC)).then_inc(u_ld, 16)
                sp.dma_start(edge_dst.rearrange("(p c) -> p c", c=EC), dst.rearrange("(p c) -> p c", c=EC)).then_inc(u_copy, 16)
                sp.dma_start(edge_src.rearrange("(p c) -> p c", c=EC), src.rearrange("(p c) -> p c", c=EC)).then_inc(u_copy, 16)
                sp.wait_ge(u_copy, 32)
                sp.wait_ge(u_ready, 1)
                unsorted = sp.value_load(unsorted_i[0:1, 0:1], min_val=0, max_val=1)
                with sp.If(unsorted > 0):
                    with sp.Fori(0, E // CHUNK) as b:
                        sp.wait_ge(o_used, b + 1)
                        sp.dma_start(other_i[:, :], dst.rearrange("(b f) -> b f", f=CHUNK)[b].rearrange("(o f) -> o f", o=1)
                                     .to_broadcast([P, CHUNK])).then_inc(o_ld, 16)

            @block.gpsimd
            def _(pool):
                g = nc.gpsimd
                g.memset(e_next[:, :], PAD_DST).then_inc(u_set, 1)
                g.memset(all_one[:, :], 1.0).then_inc(u_set, 1)
                g.iota(e_number_i[:, :], pattern=[[1, EC]], base=0, channel_multiplier=EC).then_inc(u_set, 1)
                pool.wait_ge(u_ready, 1)
                unsorted = pool.value_load(unsorted_i[0:1, 0:1], min_val=0, max_val=1)
                with pool.If(unsorted > 0):
                    g.iota(other_n[:, :], pattern=[[1, CHUNK]], base=0, channel_multiplier=0).then_inc(o_num, 1)
                    pool.wait_ge(u_rank, 1)
                    pool.wait_ge(u_copy, 32)
                    with pool.Fori(0, EC) as c:
                        g.tensor_copy(put_at[0:EP, :], rank_i[0:EP, bass.ds(c, 1)])
                        g.tensor_copy(put_src[0:EP, :], e_src[0:EP, bass.ds(c, 1)])
                        g.tensor_copy(put_dst[0:EP, :], e_dst[0:EP, bass.ds(c, 1)]).then_inc(u_pos, 1)
                        alone(pool, u_pos, c + 1)
                        for table, value in ((edge_src2, put_src), (edge_dst2, put_dst)):
                            g.indirect_dma_start(out=table, out_offset=bass.IndirectOffsetOnAxis(ap=put_at[0:EP, 0:1], axis=0),
                                                 in_=value[0:EP, :], in_offset=None, bounds_check=E - 1,
                                                 oob_is_err=False).then_inc(u_put, 16)
                        alone(pool, u_put, (c + 1) * 32)

            @block.tensor
            def _(pe):
                pe.wait_ge(u_sum, 1)
                nc.tensor.matmul(pS[:, 0:1], all_one[:, :], falls[:, 0:1], start=True, stop=True).then_inc(u_sum, 1)

            @block.vector
            def _(dve):
                v_ = nc.vector
                count = [0]

                def link(ins):
                    count[0] += 1
                    ins.then_inc(u_step, 1)
                    dve.wait_ge(u_step, count[0])

                dve.wait_ge(u_set, 3)
                dve.wait_ge(u_ld, 16 * 4)
                v_.tensor_copy(e_number[:, :], e_number_i[:, :])
                v_.tensor_copy(e_next_f[0:EP, :], e_next[0:EP, :])
                v_.memset(falls[:, :], 0.0)
                v_.memset(rank_f[:, :], 0.0)
                link(v_.tensor_copy(e_dst_f[0:EP, :], e_dst[0:EP, :]))
                v_.scalar_tensor_tensor(out=rank_f[0:EP, :], in0=e_next_f[0:EP, :], scalar=1.0, in1=e_dst_f[0:EP, :],
                                        op0=ALU.mult, op1=ALU.is_lt, accum_out=falls[0:EP, 0:1]).then_inc(u_sum, 1)
                dve.wait_ge(u_sum, 2)
                v_.tensor_scalar(unsorted_i[:, :], pS[:, 0:1], 1.0, None, ALU.min).then_inc(u_ready, 1)
                dve.wait_ge(u_ready, 1)
                unsorted = dve.value_load(unsorted_i[0:1, 0:1], min_val=0, max_val=1)
                with dve.If(unsorted > 0):
                    dve.wait_ge(o_num, 1)
                    v_.memset(rank_f[:, :], 0.0)
                    link(v_.tensor_copy(other_nf[:, :], other_n[:, :]))
                    dve.sem_inc(o_used, 1)
                    with dve.Fori(0, E // CHUNK) as b:
                        alone(dve, o_ld, (b + 1) * 16)
                        v_.tensor_copy(other_f[:, :], other_i[:, :]).then_inc(o_ready, 1)
                        alone(dve, o_ready, b + 1)
                        with dve.Fori(0, EC) as c:
                            step = (b * EC + c) * 4 + count[0]
                            v_.tensor_scalar(less[0:EP, :], other_f[0:EP, :], e_dst_f[0:EP, bass.ds(c, 1)], 0.0, ALU.is_lt,
                                             ALU.add, accum_out=n_less[0:EP, 0:1])
                            v_.tensor_scalar(before_it[0:EP, :], other_nf[0:EP, :], e_number[0:EP, bass.ds(c, 1)], None,
                                             ALU.is_lt).then_inc(u_step, 1)
                            alone(dve, u_step, step + 1)
                            v_.scalar_tensor_tensor(out=less[0:EP, :], in0=other_f[0:EP, :],
                                                    scalar=e_dst_f[0:EP, bass.ds(c, 1)], in1=before_it[0:EP, :],
                                                    op0=ALU.is_equal, op1=ALU.mult, accum_out=n_same[0:EP, 0:1]
                                                    ).then_inc(u_step, 1)
                            alone(dve, u_step, step + 2)
                            v_.tensor_tensor(n_less[0:EP, :], n_less[0:EP, :], n_same[0:EP, :], ALU.add).then_inc(u_step, 1)
                            alone(dve, u_step, step + 3)
                            v_.tensor_tensor(rank_f[0:EP, bass.ds(c, 1)], rank_f[0:EP, bass.ds(c, 1)], n_less[0:EP, :],
                                             ALU.add).then_inc(u_step, 1)
                            alone(dve, u_step, step + 4)
                        v_.tensor_scalar(other_nf[:, :], other_nf[:, :], float(CHUNK), None, ALU.add).then_inc(o_used, 1)
                        alone(dve, o_used, b + 2)
                    v_.tensor_copy(rank_i[0:EP, :], rank_f[0:EP, :]).then_inc(u_rank, 1)

        sort_mem.close()

        with phase() as block:
            def pair_rows(dram_rows, n, width=D):
                return dram_rows.rearrange("(j p s) d -> j p (s d)", p=P, s=2)[n]

            ext3 = [None] + [r[EXT:ROWS, :].rearrange("(t p) d -> t p d", p=P) for r in rows[1:]]
            node3 = [r[0:EXT, :] for r in rows]

            p0_ld, p0_st = sems("p0_ld"), sems("p0_st")
            p0_free, p0_stats, p0_mv, p0_sd, p0_rs, p0_rstd, p0_norm = (sem(f"p0_{k}") for k in
                ("free", "stats", "mv", "sd", "rs", "rstd", "norm"))
            dr_ld, so_st = sem("dr_ld"), sem("so_st")
            so_done = sem("so_done")
            da_got = sems("da_got")
            da_idx, da_kept = sem("da_idx"), sem("da_kept")

            x_last = x[(NP - 1) * 2 * P:N, :].rearrange("(p s) d -> p (s d)", s=2)
            x_full = x[0:(NP - 1) * 2 * P, :]

            @block.sync
            def _(sp):
                sp.wait_ge(s_pad, 3)
                full = (ET - 1 - TC) * P
                for k, a in ((0, edge_src), (1, edge_dst)):
                    sp.dma_start(nat_i[0:TC, k, 0, :], a[0:TC * P].rearrange("(t e) -> t e", e=P)).then_inc(s_nat, 16)
                    sp.dma_start(nat_i[0:TC - 1, k, 1, :], a[TC * P:TC * P + full].rearrange("(t e) -> t e", e=P)).then_inc(s_nat, 16)
                    sp.dma_start(nat_i[TC - 1:TC, k, 1, 0:LAST_E], a[TC * P + full:E].rearrange("(t e) -> t e", t=1)).then_inc(s_nat, 16)
                sp.dma_start(nat_i[0:TC, 2, 0, :], edge_dst[1:TC * P + 1].rearrange("(t e) -> t e", e=P)).then_inc(s_nat, 16)
                sp.dma_start(nat_i[0:TC - 1, 2, 1, :], edge_dst[TC * P + 1:TC * P + full + 1].rearrange("(t e) -> t e", e=P)).then_inc(s_nat, 16)
                sp.dma_start(nat_i[TC - 1:TC, 2, 1, 0:LAST_E - 1], edge_dst[TC * P + full + 1:E].rearrange("(t e) -> t e", t=1)).then_inc(s_nat, 16)
                with nc.allow_non_contiguous_dma(reason="one edge of each tile"):
                    sp.dma_start(prev_i[1:TC, 0:1],
                                 edge_dst[0:(TC - 1) * P].rearrange("(t e) -> t e", e=P)[:, P - 1:P]).then_inc(s_nat, 16)
                    sp.dma_start(prev_i[0:TC, 1:2],
                                 edge_dst[(TC - 1) * P:(2 * TC - 1) * P].rearrange("(t e) -> t e", e=P)[:, P - 1:P]).then_inc(s_nat, 16)

                def load_x(v):
                    at_least(sp, p0_norm, v.n - RING + 1)
                    if isinstance(v.n, int) and v.n == NP - 1:
                        sp.dma_start(xin[0:LAST_P, v.slot, :], x_last).then_inc(p0_ld[v.slot], 16)
                    else:
                        sp.dma_start(xin[:, v.slot, :], pair_rows(x_full, v.n)).then_inc(p0_ld[v.slot], 16)

                def load_dst_rows(v):
                    at_least(sp, so_done, v.round)
                    sp.dma_start(dst_row[:, :], bcast_rows(v)).then_inc(dr_ld, 16)

                td = turned_dst.rearrange("(g r) e -> g (r e)", r=RING)

                def bcast_rows(v):
                    return td[v.round].rearrange("(o f) -> o f", o=1).to_broadcast([P, RING * P])

                for v in range(RING):
                    load_x(At(0, v))
                sp.wait_ge(s_back, 1)
                sp.dma_start(turned_dst.rearrange("(c t) e -> t c e", c=2), back[0:TC, :, :]).then_inc(s_turned_st, 16)
                sp.wait_ge(s_turned_st, 16)
                sp.wait_ge(s_lin, 1)
                sp.dma_start(row_of.rearrange("(p c) o -> p (c o)", p=P), lin_id[:, :]).then_inc(s_lin, 16)
                sp.wait_ge(s_inv_t, 2)
                sp.dma_start(inv_root.rearrange("(c t e) o -> t c (e o)", c=4, e=P), inv_t[0:HC, :, :]).then_inc(s_inv_st, 16)

                def load_x_later(v):
                    if not (isinstance(v.n, int) and v.n < RING):
                        load_x(v)
                steps(sp, NP, [(load_dst_rows, 0, 0), (load_x_later, 0)], peel=1)

            @block.gpsimd
            def _(pool):
                g = nc.gpsimd
                g.memset(nat_i[:, 0, :, :], 0).then_inc(s_pad, 1)
                g.memset(nat_i[:, 1:3, :, :], PAD_DST).then_inc(s_pad, 1)
                g.memset(prev_i[:, :], -1).then_inc(s_pad, 1)
                g.memset(ident[:, :], 0.0).then_inc(s_const, 1)
                g.memset(turn[:, :], 0.0).then_inc(s_const, 1)
                g.memset(ones[:, :], 1.0).then_inc(s_const, 1)
                pool.wait_ge(s_const, 3)
                g.affine_select(out=ident[:, :], in_=ident[:, :], compare_op=ALU.not_equal, fill=1.0, base=0,
                                pattern=[[-1, P]], channel_multiplier=1).then_inc(s_const, 1)
                g.affine_select(out=turn[:, :], in_=turn[:, :], compare_op=ALU.not_equal, fill=1.0, base=-(P - 1),
                                pattern=[[1, P]], channel_multiplier=1).then_inc(s_const, 1)
                g.iota(iota_i[:, :], pattern=[[1, COLS]], base=0, channel_multiplier=0).then_inc(s_const, 1)
                g.iota(node_i[:, :], pattern=[[2 * P, NP], [1, 2]], base=1, channel_multiplier=2).then_inc(s_const, 1)
                g.iota(ext_id[:, :], pattern=[[P, ET]], base=EXT, channel_multiplier=1).then_inc(s_const, 1)
                g.memset(eps_t[:, :], EPS).then_inc(s_const, 1)
                g.iota(lin_id[:, :], pattern=[[1, COLS]], base=0, channel_multiplier=COLS).then_inc(s_lin, 1)

                pool.wait_ge(s_inv_st, 16)

                def ask(v):
                    at_least(pool, da_kept, v.n - RING + 1)
                    g.tensor_copy(idx_a[:, v.slot:v.slot + 1], table_i[:, bass.ds(v.n, 1)]).then_inc(da_idx, 1)
                    alone(pool, da_idx, v.n + 1)
                    g.indirect_dma_start(out=got_a[:, v.slot:v.slot + 1], out_offset=None, in_=inv_root,
                                         in_offset=bass.IndirectOffsetOnAxis(ap=idx_a[:, v.slot:v.slot + 1], axis=0)
                                         ).then_inc(da_got[v.slot], 16)

                def root_of(v):
                    pool.wait_ge(p0_sd, v.n + 1)
                    g.tensor_tensor(rs[:, v.slot, :], veps[:, v.slot, :], half[:, 0:2], ALU.pow).then_inc(p0_rs, 1)

                steps(pool, ET, [(root_of, 0), (ask, 0)])

            @block.scalar
            def _(act):
                act.wait_ge(s_root, 1)
                nc.scalar.activation(inv[:, :], root[:, :], ACT.Sqrt).then_inc(s_root, 1)

                def add_eps(v):
                    act.wait_ge(p0_mv, v.n + 1)
                    nc.scalar.activation(veps[:, v.slot, :], mv[:, v.slot, :, 1], ACT.Identity,
                                         bias=eps_t[:, 0:1]).then_inc(p0_sd, 1)

                def store(v):
                    act.wait_ge(p0_norm, v.n + 1)
                    act.dma_start(pair_rows(node3[0], v.n), gout[:, v.slot, :]).then_inc(p0_st[v.slot], 16)

                def store_same(v):
                    act.wait_ge(so_done, v.round + 1)
                    act.dma_start(same_dram.rearrange("(g r) e f -> g e r f", r=RING)[v.round],
                                  same_out[:, :, :]).then_inc(so_st, 16)

                def keep(v):
                    act.wait_ge(da_got[v.slot], 16 * (v.round + 1))
                    nc.scalar.activation(inv_dst[:, bass.ds(v.n, 1)], got_a[:, v.slot:v.slot + 1],
                                         ACT.Copy).then_inc(da_kept, 1)

                steps(act, NP, [(add_eps, 0), (store_same, 1, 1), (store, 2), (keep, 2)])
                for s in range(RING):
                    act.wait_ge(p0_st[s], 16 * NP // RING)
                act.wait_ge(so_st, 16 * NP // RING)

            @block.vector
            def _(dve):
                v_ = nc.vector
                count = [0]

                def link(ins):
                    count[0] += 1
                    ins.then_inc(s_pro, 1)
                    dve.wait_ge(s_pro, count[0])

                link(v_.memset(pW[:, :], 0.0))
                dve.wait_ge(s_nat, 16 * 11)
                dve.wait_ge(s_const, 9)
                link(v_.tensor_copy(nat_f[:, 0:2, :, :], nat_i[:, 0:2, :, :]))
                link(v_.tensor_copy(nat_next[:, :, :], nat_i[:, 2, :, :]))
                link(v_.tensor_copy(prev_f[:, :], prev_i[:, :]))
                link(v_.tensor_tensor(nat_f[:, 2, :, :], nat_next[:, :, :], nat_f[:, 1, :, :], ALU.is_equal))
                link(v_.scalar_tensor_tensor(out=nat_f[:, 2, :, :], in0=nat_f[:, 2, :, :], scalar=float(FAR),
                                             in1=nat_f[:, 1, :, :], op0=ALU.mult, op1=ALU.add))
                link(v_.memset(nat_f[:, 3, :, :], 0.0))
                v_.tensor_tensor(nat_f[:, 3, :, 0], prev_f[:, :], nat_f[:, 1, :, 0], ALU.is_equal).then_inc(s_flip, 1)
                dve.wait_ge(s_flipped, 1)
                link(v_.tensor_copy(turned[:, 0:2, :], pT[0][:, 0:2 * ET]))
                v_.tensor_copy(turned[:, 2:4, :], pT[1][:, 0:2 * ET]).then_inc(s_flip, 1)
                dve.wait_ge(s_flipped, 2)
                for k in range(4):
                    ps = pO[k // 2][:, (k % 2) * ET:(k % 2 + 1) * ET].rearrange("p (t o) -> p t o", o=2)[:, :, 1]
                    last = v_.tensor_copy(turned[:, k, :].rearrange("p (t o) -> p t o", o=2)[:, :, 1], ps)
                last.then_inc(s_flip, 1)
                dve.wait_ge(s_flip, 3)
                v_.tensor_copy(src_i[:, :], turned[:, 0, :])
                v_.tensor_copy(emit_i[:, :], turned[:, 2, :])
                link(v_.tensor_copy(dst_i[:, :], turned[:, 1, :]))
                link(v_.tensor_scalar(lo_i[:, :], dst_i[:, :], 1, P - 1, ALU.logical_shift_right, ALU.bitwise_and))
                link(v_.tensor_scalar(hi_i[:, :], dst_i[:, :], 8, 1, ALU.logical_shift_right, ALU.logical_shift_left))
                link(v_.tensor_scalar(odd_i[:, :], dst_i[:, :], 1, None, ALU.bitwise_and))
                link(v_.tensor_tensor(hi_i[:, :], hi_i[:, :], odd_i[:, :], ALU.bitwise_or))
                link(v_.tensor_copy(lo_f[:, :], lo_i[:, :]))
                link(v_.tensor_copy(hi_f[:, :], hi_i[:, :]))
                link(v_.tensor_copy(iota_p16[:, :], iota_i[:, 0:P]))
                link(v_.tensor_copy(iota_c16[:, :], iota_i[:, :]))
                link(v_.tensor_scalar(dst_safe[:, :], turned[:, 1, :], float(N - 1), None, ALU.min))
                for k, ids in enumerate((src_i, dst_safe, emit_i, ext_id)):
                    v_.tensor_copy(tile_ids[:, :, k], ids[:, :])
                link(v_.scalar_tensor_tensor(out=table_f[:, :], in0=hi_f[:, :], scalar=float(P), in1=lo_f[:, :],
                                             op0=ALU.mult, op1=ALU.add))
                link(v_.tensor_scalar(table_i[:, :], table_f[:, :], float(COLS * P - 1), None, ALU.min))
                dve.wait_ge(s_flipped, 3)
                v_.tensor_copy(back[0:TC, :, :], pO[0][0:TC, 0:2 * P].rearrange("t (c e) -> t c e", c=2)).then_inc(s_back, 1)

                def hots(v):
                    at_least(dve, s_count, v.n - RING + 1)
                    v_.tensor_scalar(hot_lo[:, v.slot, :], iota_p16[:, :], lo_f[:, bass.ds(v.n, 1)], None, ALU.is_equal)
                    v_.tensor_scalar(hot_hi[:, v.slot, :], iota_c16[:, :], hi_f[:, bass.ds(v.n, 1)], None,
                                     ALU.is_equal).then_inc(s_hot, 1)

                steps(dve, ET, [(hots, 0)])
                dve.wait_ge(s_count, ET)
                v_.tensor_scalar(root[:, :], pW[:, 0:COLS], 1.0, None, ALU.add).then_inc(s_root, 1)
                dve.wait_ge(s_root, 2)
                link(v_.reciprocal(inv[:, :], inv[:, :]))
                link(v_.tensor_tensor(half[:, :], inv[:, :], inv[:, :], ALU.mult))
                link(v_.tensor_tensor(half[:, :], half[:, :], root[:, :], ALU.mult))
                link(v_.tensor_scalar(half[:, :], half[:, :], -0.5, 1.5, ALU.mult, ALU.add))
                link(v_.tensor_tensor(inv[:, :], inv[:, :], half[:, :], ALU.mult))
                v_.memset(half[:, :], -0.5).then_inc(s_inv_t, 1)
                dve.wait_ge(s_flipped, 4)
                v_.tensor_copy(inv_t[0:HC, :, :], pO[1][0:HC, 0:4 * P].rearrange("t (c e) -> t c e", c=4)).then_inc(s_inv_t, 1)

                def statistics(v):
                    dve.wait_ge(p0_ld[v.slot], 16 * (v.round + 1))
                    for s in range(2):
                        last = v_.bn_stats(stats[:, v.slot, s, :], xin[:, v.slot, s * D:(s + 1) * D])
                    last.then_inc(p0_stats, 1)
                    alone(dve, p0_stats, v.n + 1)
                    for s in range(2):
                        last = v_.bn_aggr(mv[:, v.slot, s, :], stats[:, v.slot, s, :])
                    last.then_inc(p0_mv, 1)

                def normalise(v):
                    dve.wait_ge(p0_rs, v.n + 1)
                    v_.tensor_tensor(rstd[:, v.slot, :], rs[:, v.slot, :], inv[:, bass.ds(v.n * 2, 2)],
                                     ALU.mult).then_inc(p0_rstd, 1)
                    dve.wait_ge(p0_rstd, v.n + 1)
                    at_least(dve, p0_st[v.slot], 16 * v.round)
                    for s in range(2):
                        last = v_.tensor_scalar(gout[:, v.slot, s * D:(s + 1) * D], xin[:, v.slot, s * D:(s + 1) * D],
                                                mv[:, v.slot, s, 0:1], rstd[:, v.slot, s:s + 1], ALU.subtract, ALU.mult)
                    last.then_inc(p0_norm, 1)

                def same(v):
                    dve.wait_ge(dr_ld, 16 * (v.round + 1))
                    at_least(dve, so_st, 16 * v.round)
                    v_.tensor_tensor(same_out[:, :, :], dst_row[:, :].rearrange("p (r e) -> p r e", r=RING),
                                     turned[:, 1, bass.ds(v.n, RING)].rearrange("p (r o) -> p r o", o=1).to_broadcast([P, RING, P]),
                                     ALU.is_equal).then_inc(so_done, 1)

                steps(dve, NP, [(statistics, 0), (normalise, 1), (same, 0, 0)])

            @block.tensor
            def _(pe):
                t_ = nc.tensor
                pe.wait_ge(s_const, 9)
                pe.wait_ge(s_flip, 1)
                for k in range(4):
                    for c in range(2):
                        o = (k % 2) * ET + c * TC
                        last = t_.transpose(pT[k // 2][:, o:o + TC], nat_f[0:TC, k, c, :], ident[0:TC, 0:TC])
                last.then_inc(s_flipped, 1)
                pe.wait_ge(s_flip, 2)
                for k in range(2):
                    last = t_.matmul(pO[k][:, 0:2 * ET], turn[:, :], turned[:, 2 * k:2 * k + 2, :], start=True, stop=True)
                last.then_inc(s_flipped, 1)
                pe.wait_ge(s_flip, 3)
                for c in range(2):
                    last = t_.transpose(pO[0][0:TC, c * P:(c + 1) * P], turned[:, 1, c * TC:(c + 1) * TC], ident[:, :])
                last.then_inc(s_flipped, 1)

                def tally(v):
                    pe.wait_ge(s_hot, v.n + 1)
                    t_.matmul(pW[:, 0:COLS], hot_lo[:, v.slot, :], hot_hi[:, v.slot, :], start=False, stop=False,
                              skip_group_check=True).then_inc(s_count, 1)

                steps(pe, ET, [(tally, 0)])
                pe.wait_ge(s_inv_t, 1)
                for c in range(4):
                    last = t_.transpose(pO[1][0:HC, c * P:(c + 1) * P], inv[:, c * HC:(c + 1) * HC], ident[:, :])
                last.then_inc(s_flipped, 1)

        G_LD, G_ST = sems("g_ld"), sems("g_st")
        E_ST = sems("e_st")
        S_LD, O_LD, OG_LD, M_LD = sems("s_ld"), sems("o_ld"), sems("og_ld"), sems("m_ld")
        R_ST, R_LD = sems("r_st"), sems("r_ld")
        (w_got, w_split, b_got, t_done, xh_done, xl_done, o_done, z_done, h_done, carry_done, sum_done, tot_done,
         et_done, eh_done, el_done, pz_done, ez_done, eg_done, eo_done, i_m, i_s, i_r, r_kept) = (sem(k) for k in (
            "w_got", "w_split", "b_got", "t_done", "xh_done", "xl_done", "o_done", "z_done", "h_done", "carry_done",
            "sum_done", "tot_done", "et_done", "eh_done", "el_done", "pz_done", "ez_done", "eg_done", "eo_done",
            "i_m", "i_s", "i_r", "r_kept"))

        (x2_done, x2e_done, xe_b, st_done, mv_done, ve_done, r_pow, r_done, n_done, d_done, w_done, nb_zero, last_step) = (sem(k) for k in (
            "x2_done", "x2e_done", "xe_b", "st_done", "mv_done", "ve_done", "r_pow", "r_done", "n_done", "d_done",
            "w_done", "nb_zero", "last_step"))
        X_LD, X_ST, N_ST, XE_LD, NE_ST, OE_ST = (sems("xr_ld"), sems("out_st"), sems("nb_st"), sems("xe_ld"),
                                                 sems("nbe_st"), sems("oute_st"))

        def total(layer, v):
            return v.n + layer * NP

        def rounds(layer, v):
            return v.round + layer * (NP // RING)

        def turn_pair(pe, layer):
            def stage(v):
                n = total(layer, v)
                pe.wait_ge(G_LD[v.slot], 16 * (rounds(layer, v) + 1))
                at_least(pe, xl_done, n - 1)
                for s in range(2):
                    for k in range(KC):
                        o = (s * KC + k) * P
                        last = nc.tensor.transpose(pT[v.two][:, o:o + P], xin[:, v.slot, o:o + P], ident[:, :])
                last.then_inc(t_done, 1)
            return stage

        def three_passes(out_ps, hi, lo, whi, wlo, add=False):
            for k in range(KC):
                nc.tensor.matmul(out_ps, hi(k), whi(k), start=(k == 0 and not add), stop=False, skip_group_check=add)
                nc.tensor.matmul(out_ps, hi(k), wlo(k), start=False, stop=False, skip_group_check=add)
                last = nc.tensor.matmul(out_ps, lo(k), whi(k), start=False, stop=(k == KC - 1), skip_group_check=add)
            return last

        def multiply_pair(pe, layer):
            def stage(v):
                n = total(layer, v)
                pe.wait_ge(xl_done, n + 1)
                if layer < 2:
                    at_least(pe, z_done, n - 1)
                else:
                    if isinstance(v.n, int) and v.n < 2:
                        pe.wait_ge(z_done, 2 * NP)
                    at_least(pe, x2_done, v.n - 1)
                    pe.wait_ge(X_LD[v.slot], 16 * (v.round + 1))
                    nc.tensor.matmul(pO[v.two][:, :], ident[:, :], xres[:, v.slot, :], start=True, stop=False,
                                     skip_group_check=True)
                    nc.tensor.matmul(pO[v.two][:, :], one_r[0:2, :], bias_mix[0:2, :], start=False, stop=False,
                                     skip_group_check=True)
                for s in range(2):
                    last = three_passes(pO[v.two][:, s * D:(s + 1) * D],
                                        lambda k: xt_hi[:, v.two, s, k, :], lambda k: xt_lo[:, v.two, s, k, :],
                                        lambda k: w_hi[:, layer, k, :], lambda k: w_lo[:, layer, k, :], layer == 2)
                last.then_inc(o_done, 1)
            return stage

        def sum_tile(pe, layer):
            def stage(v):
                n = total(layer, v)
                pe.wait_ge(S_LD[v.slot], 16 * (rounds(layer, v) + 1))
                pe.wait_ge(carry_done, n + 1)
                at_least(pe, tot_done, n)
                nc.tensor.matmul(pS[:, 0:D], same_t[:, v.slot, :], msg[:, v.slot, :], start=True,
                                 stop=True).then_inc(sum_done, 1)
            return stage

        def turn_tile(pe, layer):
            def stage(v):
                n = total(layer, v)
                pe.wait_ge(tot_done, n + 1)
                at_least(pe, el_done, n)
                for k in range(KC):
                    last = nc.tensor.transpose(pE[:, k * P:(k + 1) * P], tot[:, v.two, k * P:(k + 1) * P], ident[:, :])
                last.then_inc(et_done, 1)
            return stage

        def multiply_tile(pe, layer):
            def stage(v):
                n = total(layer, v)
                pe.wait_ge(el_done, n + 1)
                at_least(pe, ez_done if layer < 2 else x2e_done, n if layer < 2 else v.n)
                three_passes(pZ[:, 0:D], lambda k: et_hi[:, v.two, k, :], lambda k: et_lo[:, v.two, k, :],
                             lambda k: w_hi[:, layer, k, :], lambda k: w_lo[:, layer, k, :]).then_inc(pz_done, 1)
            return stage

        def high_pair(act, layer):
            def stage(v):
                n = total(layer, v)
                act.wait_ge(t_done, n + 1)
                at_least(act, o_done, n - 1)
                nc.scalar.activation(xt_hi[:, v.two, :, :, :].rearrange("p s k c -> p (s k c)"), pT[v.two][:, :],
                                     ACT.Copy).then_inc(xh_done, 1)
            return stage

        def low_pair(dve, layer):
            def stage(v):
                n = total(layer, v)
                dve.wait_ge(xh_done, n + 1)
                nc.vector.tensor_tensor(xt_lo[:, v.two, :, :, :].rearrange("p s k c -> p (s k c)"), pT[v.two][:, :],
                                        xt_hi[:, v.two, :, :, :].rearrange("p s k c -> p (s k c)").bitcast(F32),
                                        ALU.subtract).then_inc(xl_done, 1)
            return stage

        def high_tile(act, layer):
            def stage(v):
                n = total(layer, v)
                act.wait_ge(et_done, n + 1)
                at_least(act, pz_done, n - 1)
                nc.scalar.activation(et_hi[:, v.two, :, :].rearrange("p k c -> p (k c)"), pE[:, 0:D],
                                     ACT.Copy).then_inc(eh_done, 1)
            return stage

        def low_tile(dve, layer):
            def stage(v):
                n = total(layer, v)
                dve.wait_ge(eh_done, n + 1)
                nc.vector.tensor_tensor(et_lo[:, v.two, :, :].rearrange("p k c -> p (k c)"), pE[:, 0:D],
                                        et_hi[:, v.two, :, :].rearrange("p k c -> p (k c)").bitcast(F32),
                                        ALU.subtract).then_inc(el_done, 1)
            return stage

        def carry(dve, layer):
            def stage(v):
                n = total(layer, v)
                dve.wait_ge(M_LD[v.slot], 16 * (rounds(layer, v) + 1))
                if isinstance(v.n, int) and v.n == 0:
                    nc.vector.engine_nop().then_inc(carry_done, 1)
                    return
                dve.wait_ge(sum_done, n)
                nc.vector.scalar_tensor_tensor(out=msg[:, v.slot, :], in0=pS[:, 0:D],
                                               scalar=turned[:, 3, bass.ds(v.n, 1)], in1=msg[:, v.slot, :],
                                               op0=ALU.mult, op1=ALU.add).then_inc(carry_done, 1)
            return stage

        def add_own(dve, layer):
            def stage(v):
                n = total(layer, v)
                if layer == 0:
                    dve.wait_ge(OG_LD[v.slot], 16 * (v.round + 1))
                else:
                    dve.wait_ge(O_LD[v.slot], 16 * (rounds(layer - 1, v) + 1))
                dve.wait_ge(sum_done, n + 1)
                at_least(dve, et_done, n - 1)
                nc.vector.tensor_tensor(tot[:, v.two, :], pS[:, 0:D], own[:, v.slot, :], ALU.add).then_inc(tot_done, 1)
            return stage

        def fetch_first(pool):
            def stage(v):
                g = nc.gpsimd
                at_least(pool, sum_done, v.n - RING + 1)
                at_least(pool, tot_done, v.n - RING + 1)
                at_least(pool, R_ST[v.slot], 16 * v.round)
                g.tensor_copy(ids_now[:, v.slot, :], ids_flat[:, bass.ds(v.n * 4, 4)]).then_inc(i_m, 1)
                alone(pool, i_m, v.n + 1)
                g.indirect_dma_start(out=msg[:, v.slot, :], out_offset=None, in_=rows[0],
                                     in_offset=bass.IndirectOffsetOnAxis(ap=ids_now[:, v.slot, 0:1], axis=0)
                                     ).then_inc(M_LD[v.slot], 16)
                g.indirect_dma_start(out=own[:, v.slot, :], out_offset=None, in_=rows[0],
                                     in_offset=bass.IndirectOffsetOnAxis(ap=ids_now[:, v.slot, 1:2], axis=0)
                                     ).then_inc(OG_LD[v.slot], 16)
                g.indirect_dma_start(out=row_of, out_offset=bass.IndirectOffsetOnAxis(ap=ids_now[:, v.slot, 2:3], axis=0),
                                     in_=ids_now[:, v.slot, 3:4], in_offset=None, bounds_check=N - 1,
                                     oob_is_err=False).then_inc(R_ST[v.slot], 16)
            return stage

        def ask_row(pool):
            def stage(v):
                g = nc.gpsimd
                at_least(pool, M_LD[v.slot], 16 * rounds(1, v))
                at_least(pool, r_kept, v.n - RING + 1)
                g.tensor_copy(idx_r[:, v.slot:v.slot + 1], src_i[:, bass.ds(v.n, 1)]).then_inc(i_r, 1)
                alone(pool, i_r, v.n + 1)
                g.indirect_dma_start(out=got_r[:, v.slot:v.slot + 1], out_offset=None, in_=row_of,
                                     in_offset=bass.IndirectOffsetOnAxis(ap=idx_r[:, v.slot:v.slot + 1], axis=0)
                                     ).then_inc(R_LD[v.slot], 16)
            return stage

        def fetch_second(pool):
            def stage(v):
                g = nc.gpsimd
                pool.wait_ge(R_LD[v.slot], 16 * (v.round + 1))
                g.tensor_copy(src_row[:, bass.ds(v.n, 1)], got_r[:, v.slot:v.slot + 1]).then_inc(r_kept, 1)
                alone(pool, sum_done, ET + v.n - RING + 1)
                g.indirect_dma_start(out=msg[:, v.slot, :], out_offset=None, in_=rows[1],
                                     in_offset=bass.IndirectOffsetOnAxis(ap=got_r[:, v.slot:v.slot + 1], axis=0)
                                     ).then_inc(M_LD[v.slot], 16)
            return stage

        def load_pair(sp, layer):
            def stage(v):
                at_least(sp, t_done, total(layer, v) - RING + 1)
                sp.dma_start(xin[:, v.slot, :], pair_rows(node3[layer], v.n)).then_inc(G_LD[v.slot], 16)
            return stage

        def load_same(sp, layer):
            def stage(v):
                at_least(sp, sum_done, total(layer, v) - RING + 1)
                sp.dma_start(same_t[:, v.slot, :], same_dram[v.n]).then_inc(S_LD[v.slot], 16)
            return stage

        def load_own(sp, layer):
            def stage(v):
                at_least(sp, tot_done, total(layer, v) - RING + 1)
                sp.dma_start(own[:, v.slot, :], ext3[layer][v.n]).then_inc(O_LD[v.slot], 16)
            return stage

        def stored(eng, layer):
            for s in range(RING):
                if layer == 0:
                    eng.wait_ge(p0_st[s], 16 * NP // RING)
                else:
                    eng.wait_ge(G_ST[s], 16 * layer * NP // RING)
                    eng.wait_ge(E_ST[s], 16 * layer * ET // RING)

        def halves(w, k):
            return w.rearrange("(k p) n -> p k n", p=P)

        with phase() as block:
            @block.sync
            def _(sp):
                for l, w in enumerate((W1, W2, W3)):
                    at_least(sp, w_split, 2 * l)
                    sp.dma_start(w_in[:, :, :], halves(w, KC)).then_inc(w_got, 16)
                for l, b in enumerate((b1, b2, b3)):
                    for s in range(2):
                        sp.dma_start(bias[:, l, s * D:(s + 1) * D],
                                     b.rearrange("(o n) -> o n", o=1).to_broadcast([P, D])).then_inc(b_got, 16)
                sp.dma_start(wr_row[:, :], wr.rearrange("n o -> o n").to_broadcast([P, D])).then_inc(b_got, 16)
                sp.dma_start(br_col[:, :], br.rearrange("(o n) -> o n", o=1).to_broadcast([P, 1])).then_inc(b_got, 16)

                def store_tile(layer):
                    def stage(v):
                        sp.wait_ge(eo_done, total(layer, v) + 1)
                        sp.dma_start(ext3[layer + 1][v.n], eo[:, v.slot, :]).then_inc(E_ST[v.slot], 16)
                    return stage

                for layer in range(2):
                    stored(sp, layer)
                    own_stage = [(load_own(sp, layer), 0)] if layer else []
                    steps(sp, NP, [(load_pair(sp, layer), 0), (load_same(sp, layer), 0), *own_stage,
                                   (store_tile(layer), 6)])

            @block.gpsimd
            def _(pool):
                stored(pool, 0)
                steps(pool, ET, [(fetch_first(pool), 0)])
                for s in range(RING):
                    pool.wait_ge(R_ST[s], 16 * ET // RING)
                stored(pool, 1)
                steps(pool, ET, [(fetch_second(pool), 2), (ask_row(pool), 0)])

            @block.tensor
            def _(pe):
                for layer in range(2):
                    steps(pe, NP, [(turn_pair(pe, layer), 0), (multiply_pair(pe, layer), 1), (sum_tile(pe, layer), 0),
                                   (turn_tile(pe, layer), 1), (multiply_tile(pe, layer), 2)])

            @block.scalar
            def _(act):
                nc.scalar.preload_act_table(ACT.Gelu_apprx_tanh)

                def gelu_pair(layer):
                    def stage(v):
                        n = total(layer, v)
                        act.wait_ge(z_done, n + 1)
                        at_least(act, G_ST[v.slot], 16 * rounds(layer, v))
                        nc.scalar.activation(gout[:, v.slot, :], zb[:, v.two, :], ACT.Gelu_apprx_tanh).then_inc(h_done, 1)
                    return stage

                def store_pair(layer):
                    def stage(v):
                        act.wait_ge(h_done, total(layer, v) + 1)
                        act.dma_start(pair_rows(node3[layer + 1], v.n), gout[:, v.slot, :]).then_inc(G_ST[v.slot], 16)
                    return stage

                def gelu_tile(layer):
                    def stage(v):
                        n = total(layer, v)
                        act.wait_ge(ez_done, n + 1)
                        at_least(act, eo_done, n - 1)
                        nc.scalar.activation(eh[:, v.two, :], ez[:, v.two, :], ACT.Gelu_apprx_tanh).then_inc(eg_done, 1)
                    return stage

                for layer in range(2):
                    steps(act, NP, [(high_pair(act, layer), 0), (gelu_tile(layer), 4), (gelu_pair(layer), 3),
                                    (store_pair(layer), 4), (high_tile(act, layer), 1)])
                for s in range(RING):
                    act.wait_ge(G_ST[s], 16 * 2 * NP // RING)
                    act.wait_ge(E_ST[s], 16 * 2 * ET // RING)

            @block.vector
            def _(dve):
                v_ = nc.vector
                for l in range(3):
                    dve.wait_ge(w_got, 16 * (l + 1))
                    v_.tensor_copy(w_hi[:, l, :, :], w_in[:, :, :]).then_inc(w_split, 1)
                    dve.wait_ge(w_split, 2 * l + 1)
                    v_.tensor_tensor(w_lo[:, l, :, :], w_in[:, :, :], w_hi[:, l, :, :].bitcast(F32),
                                     ALU.subtract).then_inc(w_split, 1)
                dve.wait_ge(b_got, 16 * 8)

                def bias_pair(layer):
                    def stage(v):
                        n = total(layer, v)
                        dve.wait_ge(o_done, n + 1)
                        at_least(dve, h_done, n - 1)
                        v_.tensor_tensor(zb[:, v.two, :], pO[v.two][:, :], bias[:, layer, :], ALU.add).then_inc(z_done, 1)
                    return stage

                def bias_tile(layer):
                    def stage(v):
                        n = total(layer, v)
                        dve.wait_ge(pz_done, n + 1)
                        at_least(dve, eg_done, n - 1)
                        v_.scalar_tensor_tensor(out=ez[:, v.two, :], in0=pZ[:, 0:D], scalar=inv_dst[:, bass.ds(v.n, 1)],
                                                in1=bias[:, layer, 0:D], op0=ALU.mult, op1=ALU.add).then_inc(ez_done, 1)
                    return stage

                def scale_tile(layer):
                    def stage(v):
                        n = total(layer, v)
                        dve.wait_ge(eg_done, n + 1)
                        at_least(dve, E_ST[v.slot], 16 * rounds(layer, v))
                        v_.tensor_scalar(eo[:, v.slot, :], eh[:, v.two, :], inv_dst[:, bass.ds(v.n, 1)], None,
                                         ALU.mult).then_inc(eo_done, 1)
                    return stage

                for layer in range(2):
                    steps(dve, NP, [(low_pair(dve, layer), 1), (add_own(dve, layer), 1), (carry(dve, layer), 0),
                                    (low_tile(dve, layer), 2), (bias_tile(layer), 3), (bias_pair(layer), 2),
                                    (scale_tile(layer), 5)])

        out_full = out[0:(NP - 1) * 2 * P, :]
        out_last = out[(NP - 1) * 2 * P:N, :].rearrange("(p s) d -> p (s d)", s=2)
        normed3 = normed[EXT:ROWS, :].rearrange("(t p) d -> t p d", p=P)
        ext_out3 = ext_out.rearrange("(t p) d -> t p d", p=P)
        L = 2

        def is_last(v):
            return isinstance(v.n, int) and v.n == NP - 1

        with phase() as block:
            @block.sync
            def _(sp):
                stored(sp, L)

                def load_x_pair(v):
                    at_least(sp, o_done, total(L, v) - RING + 1)
                    if is_last(v):
                        sp.dma_start(xres[0:LAST_P, v.slot, :], x_last).then_inc(X_LD[v.slot], 16)
                    else:
                        sp.dma_start(xres[:, v.slot, :], pair_rows(x_full, v.n)).then_inc(X_LD[v.slot], 16)

                def store_normed(v):
                    sp.wait_ge(w_done, v.n + 1)
                    sp.dma_start(pair_rows(normed[0:EXT, :], v.n), nb[:, v.slot, 0:2, :].rearrange("p s d -> p (s d)")
                                  ).then_inc(N_ST[v.slot], 16)

                def store_out(v):
                    sp.wait_ge(n_done, v.n + 1)
                    pair = x2n[:, v.slot, 0:2, :].rearrange("p s d -> p (s d)")
                    if is_last(v):
                        sp.dma_start(out_last, pair[0:LAST_P, :]).then_inc(X_ST[v.slot], 16)
                    else:
                        sp.dma_start(pair_rows(out_full, v.n), pair).then_inc(X_ST[v.slot], 16)

                def store_normed_tile(v):
                    sp.wait_ge(w_done, v.n + 1)
                    sp.dma_start(normed3[v.n], nb[:, v.slot, 2, :]).then_inc(NE_ST[v.slot], 16)

                def store_out_tile(v):
                    sp.wait_ge(n_done, v.n + 1)
                    sp.dma_start(ext_out3[v.n], x2n[:, v.slot, 2, :]).then_inc(OE_ST[v.slot], 16)

                steps(sp, NP, [(load_pair(sp, L), 0), (load_same(sp, L), 0), (load_own(sp, L), 0), (load_x_pair, 0),
                               (store_out, 7), (store_out_tile, 7),
                               (store_normed, 8), (store_normed_tile, 8)], peel=1)
                for s in range(RING):
                    sp.wait_ge(X_ST[s], 16 * NP // RING)
                    sp.wait_ge(N_ST[s], 16 * NP // RING)
                    sp.wait_ge(NE_ST[s], 16 * ET // RING)
                    sp.wait_ge(OE_ST[s], 16 * ET // RING)

            @block.gpsimd
            def _(pool):
                g = nc.gpsimd
                stored(pool, L)

                def fetch_third(v):
                    alone(pool, sum_done, 2 * ET + v.n - RING + 1)
                    g.tensor_copy(idx_m[:, v.slot:v.slot + 1], src_row[:, bass.ds(v.n, 1)]).then_inc(i_m, 1)
                    alone(pool, i_m, ET + v.n + 1)
                    g.indirect_dma_start(out=msg[:, v.slot, :], out_offset=None, in_=rows[2],
                                         in_offset=bass.IndirectOffsetOnAxis(ap=idx_m[:, v.slot:v.slot + 1], axis=0)
                                         ).then_inc(M_LD[v.slot], 16)

                def fetch_residual(v):
                    alone(pool, x2e_done, v.n - RING + 1)
                    g.tensor_copy(idx_s[:, v.slot:v.slot + 1], dst_safe[:, bass.ds(v.n, 1)]).then_inc(i_s, 1)
                    alone(pool, i_s, v.n + 1)
                    g.indirect_dma_start(out=xe[:, v.slot, :], out_offset=None, in_=x,
                                         in_offset=bass.IndirectOffsetOnAxis(ap=idx_s[:, v.slot:v.slot + 1], axis=0)
                                         ).then_inc(XE_LD[v.slot], 16)

                def root_of(v):
                    pool.wait_ge(ve_done, v.n + 1)
                    g.tensor_tensor(rs3[:, v.slot, :], veps3[:, v.slot, :], half[:, 0:3], ALU.pow).then_inc(r_pow, 1)
                    pool.wait_ge(r_pow, 2 * v.n + 1)
                    g.tensor_tensor(shift3[:, v.slot, :], mv3[:, v.slot, :, 0], rs3[:, v.slot, :], ALU.mult).then_inc(r_pow, 1)
                    g.tensor_scalar(one_rs3[:, v.slot, :], rs3[:, v.slot, :], 1.0, None, ALU.add)
                    alone(pool, r_pow, 2 * v.n + 2)
                    g.tensor_scalar(shift3[:, v.slot, :], shift3[:, v.slot, :], -1.0, None, ALU.mult).then_inc(r_done, 1)

                def add_bias(v):
                    pool.wait_ge(XE_LD[v.slot], 16 * (v.round + 1))
                    g.tensor_tensor(xe[:, v.slot, :], xe[:, v.slot, :], bias[:, L, 0:D], ALU.add).then_inc(xe_b, 1)

                steps(pool, ET, [(fetch_third, 0), (fetch_residual, 2), (root_of, 6), (add_bias, 3)])

            @block.tensor
            def _(pe):
                pe.wait_ge(nb_zero, 1)

                steps(pe, NP, [(turn_pair(pe, L), 0), (multiply_pair(pe, L), 1), (sum_tile(pe, L), 0),
                               (turn_tile(pe, L), 1), (multiply_tile(pe, L), 2)])

            @block.scalar
            def _(act):
                def keep_pair(v):
                    act.wait_ge(o_done, total(L, v) + 1)
                    at_least(act, n_done, v.n - RING + 1)
                    nc.scalar.activation(x2[:, v.slot, 0:2, :].rearrange("p s d -> p (s d)"), pO[v.two][:, :],
                                         ACT.Copy).then_inc(x2_done, 1)

                def normalise(v):
                    act.wait_ge(r_done, v.n + 1)
                    at_least(act, N_ST[v.slot], 16 * v.round)
                    at_least(act, NE_ST[v.slot], 16 * v.round)
                    for s in range(3):
                        last = nc.scalar.activation(nb[:, v.slot, s, 0:D], x2[:, v.slot, s, :], ACT.Identity,
                                                    bias=shift3[:, v.slot, s:s + 1], scale=rs3[:, v.slot, s:s + 1])
                    at_least(act, X_ST[v.slot], 16 * v.round)
                    at_least(act, OE_ST[v.slot], 16 * v.round)
                    for s in range(3):
                        last = nc.scalar.activation(x2n[:, v.slot, s, :], x2[:, v.slot, s, :], ACT.Identity,
                                                    bias=shift3[:, v.slot, s:s + 1], scale=one_rs3[:, v.slot, s:s + 1])
                    last.then_inc(n_done, 1)

                steps(act, NP, [(keep_pair, 3), (high_pair(act, L), 0), (normalise, 6), (high_tile(act, L), 1)])

            @block.vector
            def _(dve):
                v_ = nc.vector
                v_.memset(nb[:, :, :, :], 0.0)
                v_.tensor_copy(one_r[:, :], ones[:, :])
                v_.tensor_copy(bias_hi[:, :], bias[:, L, :]).then_inc(last_step, 1)
                dve.wait_ge(last_step, 1)
                v_.tensor_tensor(bias_mix[:, :], bias[:, L, :], bias_hi[:, :].bitcast(F32), ALU.subtract).then_inc(last_step, 1)
                dve.wait_ge(last_step, 2)
                v_.tensor_copy(bias_mix[0:1, :], bias_hi[0:1, :]).then_inc(nb_zero, 1)
                dve.wait_ge(nb_zero, 1)

                def residual_tile(v):
                    dve.wait_ge(xe_b, v.n + 1)
                    at_least(dve, n_done, v.n - RING + 1)
                    dve.wait_ge(pz_done, total(L, v) + 1)
                    v_.scalar_tensor_tensor(out=x2[:, v.slot, 2, :], in0=pZ[:, 0:D], scalar=inv_dst[:, bass.ds(v.n, 1)],
                                            in1=xe[:, v.slot, :], op0=ALU.mult, op1=ALU.add).then_inc(x2e_done, 1)

                def statistics(v):
                    dve.wait_ge(x2_done, v.n + 1)
                    dve.wait_ge(x2e_done, v.n + 1)
                    for s in range(3):
                        last = v_.bn_stats(stats3[:, v.slot, s, :], x2[:, v.slot, s, :])
                    last.then_inc(st_done, 1)

                def aggregate(v):
                    alone(dve, st_done, v.n + 1)
                    for s in range(3):
                        last = v_.bn_aggr(mv3[:, v.slot, s, :], stats3[:, v.slot, s, :])
                    last.then_inc(mv_done, 1)

                def route(v):
                    dve.wait_ge(n_done, v.n + 1)
                    at_least(dve, w_done, v.n - RING + 1)
                    at_least(dve, d_done, v.n)
                    for s in range(3):
                        last = v_.scalar_tensor_tensor(out=junk[:, s, :], in0=nb[:, v.slot, s, 0:D], scalar=1.0,
                                                       in1=wr_row[:, :], op0=ALU.mult, op1=ALU.mult,
                                                       accum_out=dot3[:, v.slot, s:s + 1])
                    last.then_inc(d_done, 1)

                def add_eps(v):
                    dve.wait_ge(mv_done, v.n + 1)
                    v_.tensor_scalar(veps3[:, v.slot, :], mv3[:, v.slot, :, 1], EPS, None, ALU.add).then_inc(ve_done, 1)

                def weigh(v):
                    dve.wait_ge(d_done, v.n + 1)
                    v_.tensor_scalar(w_all[:, bass.ds(v.n * 3, 3)], dot3[:, v.slot, :], br_col[:, 0:1], None, ALU.add)
                    v_.tensor_scalar(nb[:, v.slot, :, D], dot3[:, v.slot, :], br_col[:, 0:1], None, ALU.add
                                     ).then_inc(w_done, 1)

                steps(dve, NP, [(low_pair(dve, L), 1), (add_own(dve, L), 1), (carry(dve, L), 0), (add_eps, 5), (route, 7), (low_tile(dve, L), 2),
                                (statistics, 4), (weigh, 7), (residual_tile, 3), (aggregate, 4)])

        rings.close()
        with phase() as block:
            @block.gpsimd
            def _(pool):
                nc.clear_and_free_semaphores(semaphores)

        PASSED[0] = sem("passed_on")

        CAND = 3 * NP
        w_flag = sb("w_flag", [P, CAND], I32)
        least = sb("least", [P, CAND])
        number = sb("number", [P, NP, 3])
        w_flag_f = w_flag[:, :].bitcast(F32)
        in_edges = sb("in_edges", [P, COLS])
        bits = sb("bits", [P, 32], I32)
        shifts = sb("shifts", [P, 32], I32)
        digits = sb("digits", [P, 16, 3], I32)
        digits_f = sb("digits_f", [P, 16, 3])
        heavier = sb("heavier", [P, CAND])
        equal = sb("equal", [P, CAND])
        equal_no = sb("equal_no", [P, CAND])
        short = sb("short", [P, 3])
        upto, upto_cand = sb("upto", [P, 1]), sb("upto_cand", [P, 3])
        upto_part = sb("upto_part", [P, 1])
        need = sb("need", [P, 1])
        cnt = sb("cnt", [P, 3])
        best = sb("best", [P, 1], I32)
        cand = sb("cand", [P, 3], I32)
        flip = sb("flip", [P, 3], I32)
        thresh = sb("thresh", [P, 3], I32)
        enough = sb("enough", [P, 3], I32)
        keys = sb("keys", [P, CAND])
        turns_i = sb("turns_i", [P, 1], I32)
        BASE = K_SEL // (P * 8) + 1
        SPILL = 4
        REST = -(-CAND // 8) - BASE - SPILL
        ALL = BASE + SPILL + REST + 1
        lists = sb("lists", [P, ALL * 8])
        lists_i = sb("lists_i", [P, ALL * 8], I32)
        none = sb("none", [P, ALL * 8])
        spill_dram = dram("spill_dram", (2 * P * SPILL * 8,))
        spill = sb("spill", [P, SPILL * 8])
        spread = sb("spread", [P, SPILL * 8])
        top8 = sb("top8", [P, 8])
        counts = sb("counts", [P, 2])
        tallies = sb("tallies", [P, 3])
        tallies_i = sb("tallies_i", [P, 2], I32)
        ext_t = sb("ext_t", [P, 3, RING, D])
        idx_o = sb("idx_o", [P, 3 * RING], I32)
        f1_in = sb("f1_in", [P, KC, H])
        f1_hi = sb("f1_hi", [P, KC, H], F32R)
        f1_lo = sb("f1_lo", [P, KC, H], F32R)
        f2_in = sb("f2_in", [P, FH, D])
        f2_hi = sb("f2_hi", [P, FH, D], F32R)
        f2_lo = sb("f2_lo", [P, FH, D], F32R)
        fb1_col = sb("fb1_col", [P, FH])
        fb2_row = sb("fb2_row", [P, D])
        ask_i = sb("ask_i", [P, 2, RING], I32)
        put_i = sb("put_i", [P, 2, RING], I32)
        at_row = sb("at_row", [P, 2, RING], I32)
        nx = sb("nx", [P, 2, RING, DW])
        wq = sb("wq", [P, 2, RING])
        fx_hi = sb("fx_hi", [P, 2, KC, 4 * P], F32R)
        fx_lo = sb("fx_lo", [P, 2, KC, 4 * P], F32R)
        hid = sb("hid", [P, 2, 4 * P])
        hid_hi = sb("hid_hi", [P, 4, 4 * P], F32R)
        hid_lo = sb("hid_lo", [P, 4, 4 * P], F32R)
        y_sum = sb("y_sum", [P, 2, D])
        y = sb("y", [P, 2, RING, D])

        OX_LD, OI, OX_ST = sems("ox_ld"), sem("ox_i"), sems("ox_st")
        (f_got, f_split, c_step, c_cnt, c_tot, c_bits, c_ready, c_take, c_spill, c_spill_st, c_spread,
         c_lift) = (sem(k) for k in (
            "f_got", "f_split", "c_step", "c_cnt", "c_tot", "c_bits", "c_ready", "c_take", "c_spill", "c_spill_st",
            "c_spread", "c_lift"))
        ext_quads = ext_out.rearrange("(g r p) d -> g p r d", r=RING, p=P)
        QUADS = ET // RING
        NUMBER_DIGITS = -(-N.bit_length() // 2)

        with phase() as block:
            @block.sync
            def _(sp):
                sp.dma_start(f1_in[:, :, :], w1.rearrange("(k p) n -> p k n", p=P)).then_inc(f_got, 16)
                sp.dma_start(f2_in[:, :, :], w2.rearrange("(k p) n -> p k n", p=P)).then_inc(f_got, 16)
                with nc.allow_non_contiguous_dma(reason="a bias to columns"):
                    sp.dma_start(fb1_col[:, :], fb1.rearrange("(k p) -> p k", p=P)).then_inc(f_got, 16)
                sp.dma_start(fb2_row[:, :], fb2.rearrange("(o n) -> o n", o=1).to_broadcast([P, D])).then_inc(f_got, 16)
                for q in range(3):
                    sp.dma_start(ext_t[:, q, :, :], ext_quads[q]).then_inc(OX_LD[q], 16)

                def reload(q, uses, n):
                    sp.wait_ge(OX_ST[q], uses * (16 * RING))
                    sp.dma_start(ext_t[:, q, :, :], ext_quads[n]).then_inc(OX_LD[q], 16)

                with sp.Fori(1, QUADS // 3) as three:
                    for q in range(3):
                        reload(q, three, three * 3 + q)
                for q in range(QUADS % 3):
                    reload(q, QUADS // 3, QUADS // 3 * 3 + q)

            @block.scalar
            def _(act):
                act.wait_ge(f_got, 16 * 4)
                nc.scalar.activation(f1_hi[:, :, :].rearrange("p k n -> p (k n)"),
                                     f1_in[:, :, :].rearrange("p k n -> p (k n)"), ACT.Copy).then_inc(f_split, 1)
                nc.scalar.activation(f2_hi[:, :, :].rearrange("p k n -> p (k n)"),
                                     f2_in[:, :, :].rearrange("p k n -> p (k n)"), ACT.Copy).then_inc(f_split, 1)
                SW = SPILL * 8
                act.wait_ge(c_spill, 1)
                for half in range(2):
                    act.dma_start(spill_dram[half * P * SW:(half + 1) * P * SW].rearrange("(p r) -> p r", r=SW),
                                  spill[:, :]).then_inc(c_spill_st, 16)
                act.wait_ge(c_spill_st, 32)
                diagonal = bass.AP(tensor=spill_dram.tensor, offset=spill_dram.offset, ap=[[SW, P], [SW + 1, SW]])
                with nc.allow_non_contiguous_dma(reason="a few thousand spilled keys"):
                    act.dma_start(spread[:, :], diagonal).then_inc(c_spread, 16)

            @block.gpsimd
            def _(pool):
                g = nc.gpsimd
                g.memset(bits[:, :], 1).then_inc(c_bits, 1)
                g.iota(shifts[:, :], pattern=[[-1, 32]], base=31, channel_multiplier=0).then_inc(c_bits, 1)

                def put_quad(q, uses, n):
                    pool.wait_ge(OX_LD[q], (uses + 1) * 16)
                    if not isinstance(uses, int) or uses:
                        pool.wait_ge(OX_ST[q], uses * 16 * RING)
                    g.tensor_copy(idx_o[:, q * RING:(q + 1) * RING], emit_i[:, bass.ds(n * RING, RING)]).then_inc(OI, 1)
                    alone(pool, OI, n + 1)
                    for r in range(RING):
                        slot = q * RING + r
                        g.indirect_dma_start(out=out, out_offset=bass.IndirectOffsetOnAxis(ap=idx_o[:, slot:slot + 1], axis=0),
                                             in_=ext_t[:, q, r, :], in_offset=None, bounds_check=N - 1,
                                             oob_is_err=False).then_inc(OX_ST[q], 16)

                for q in range(3):
                    put_quad(q, 0, q)
                with pool.Fori(1, QUADS // 3) as three:
                    for q in range(3):
                        put_quad(q, three, three * 3 + q)
                for q in range(QUADS % 3):
                    put_quad(q, QUADS // 3, QUADS // 3 * 3 + q)
                for q in range(3):
                    pool.wait_ge(OX_ST[q], (QUADS + 2 - q) // 3 * 16 * RING)

            @block.tensor
            def _(pe):
                t_ = nc.tensor
                with pe.Fori(0, 16) as b:
                    pe.wait_ge(c_cnt, b + 1)
                    t_.matmul(pS[:, 0:3], ones[:, :], cnt[:, :], start=True, stop=True).then_inc(c_tot, 1)
                pe.wait_ge(c_cnt, 17)
                t_.matmul(pS[:, 0:1], ones[:, :], cnt[:, 0:1], start=True, stop=True).then_inc(c_tot, 1)
                with pe.Fori(0, NUMBER_DIGITS) as b:
                    pe.wait_ge(c_cnt, b + 18)
                    t_.matmul(pS[:, 0:3], ones[:, :], cnt[:, :], start=True, stop=True).then_inc(c_tot, 1)
                pe.wait_ge(c_cnt, 18 + NUMBER_DIGITS)
                for k in range(2):
                    last = t_.transpose(pT[0][0:1, k * P:(k + 1) * P], counts[:, k:k + 1], ident[:, :])
                last.then_inc(c_tot, 1)

            @block.vector
            def _(dve):
                v_ = nc.vector
                count = [0]

                def link(ins):
                    count[0] += 1
                    ins.then_inc(c_step, 1)
                    dve.wait_ge(c_step, count[0])

                dve.wait_ge(c_bits, 2)
                link(v_.tensor_tensor(bits[:, :], bits[:, :], shifts[:, :], ALU.logical_shift_left))
                bit2 = bits[:, :].rearrange("p (d b) -> p d b", b=2)
                v_.tensor_copy(digits[:, :, 0], bit2[:, :, 1])
                v_.tensor_copy(digits[:, :, 1], bit2[:, :, 0])
                link(v_.tensor_tensor(digits[:, :, 2], bit2[:, :, 0], bit2[:, :, 1], ALU.bitwise_or))
                v_.tensor_copy(digits_f[:, :, :], digits[:, :, :])
                v_.memset(best[:, :], 0)
                v_.memset(least[:, :], -3.0e38)
                v_.tensor_copy(number[:, :, 0:2], node_i[:, :].rearrange("p (j s) -> p j s", s=2))
                v_.tensor_scalar(number[:, :, 2], turned[:, 2, :], 1.0, None, ALU.add)
                link(v_.tensor_scalar(in_edges[:, :], root[:, :], 1.5, float(FAR), ALU.is_ge, ALU.mult))
                link(v_.tensor_tensor(number[:, :, 0:2], number[:, :, 0:2],
                                      in_edges[:, :].rearrange("p (j s) -> p j s", s=2), ALU.add))
                numbers = number[:, :, :].rearrange("p j s -> p (j s)")
                link(v_.tensor_scalar(w_flag[:, :], numbers, float(N), None, ALU.is_gt))
                link(v_.copy_predicated(w_all[:, :], w_flag[:, :], least[:, :]))

                def as_float():
                    yield v_.tensor_scalar(flip[:, :], cand[:, :], 31, -1, ALU.arith_shift_right, ALU.bitwise_xor)
                    yield v_.tensor_scalar(flip[:, :], flip[:, :], -2147483648, None, ALU.bitwise_or)
                    yield v_.tensor_tensor(thresh[:, :], cand[:, :], flip[:, :], ALU.bitwise_xor)

                digits_flat = digits[:, :, :].rearrange("p d k -> p (d k)")
                digits_f_flat = digits_f[:, :, :].rearrange("p d k -> p (d k)")

                SEARCH = 7
                ge3 = (heavier, equal, keys)
                with dve.Fori(0, 16) as b:
                    before = b * SEARCH + count[0]
                    v_.tensor_tensor(cand[:, :], best[:, 0:1].to_broadcast([P, 3]), digits_flat[:, bass.ds(b * 3, 3)],
                                     ALU.bitwise_or).then_inc(c_step, 1)
                    alone(dve, c_step, before + 1)
                    for k, ins in enumerate(as_float()):
                        ins.then_inc(c_step, 1)
                        alone(dve, c_step, before + 2 + k)
                    for k in range(3):
                        last = v_.tensor_scalar(ge3[k][:, :], w_all[:, :], thresh[:, k:k + 1].bitcast(F32), 0.0, ALU.is_ge,
                                                ALU.add, accum_out=cnt[:, k:k + 1])
                    last.then_inc(c_cnt, 1)
                    alone(dve, c_tot, b + 1)
                    v_.tensor_scalar(enough[:, :], pS[:, 0:3], float(K_SEL), None, ALU.is_ge).then_inc(c_ready, 1)
                    alone(dve, c_ready, b + 1)
                    for k in range(3):
                        v_.copy_predicated(best[:, :], enough[:, k:k + 1], cand[:, k:k + 1]).then_inc(c_step, 1)
                        alone(dve, c_step, before + 5 + k)
                count[0] += 16 * SEARCH
                link(v_.tensor_copy(cand[:, :], best[:, 0:1].to_broadcast([P, 3])))
                for ins in as_float():
                    link(ins)
                v_.tensor_scalar(heavier[:, :], w_all[:, :], thresh[:, 0:1].bitcast(F32), 0.0, ALU.is_gt, ALU.add,
                                 accum_out=cnt[:, 0:1])
                v_.tensor_scalar(equal[:, :], w_all[:, :], thresh[:, 0:1].bitcast(F32), None,
                                 ALU.is_equal).then_inc(c_cnt, 1)
                v_.memset(upto[:, :], 0.0)
                link(v_.tensor_scalar(equal_no[:, :], numbers, -float(FAR), None, ALU.add))
                link(v_.tensor_tensor(equal_no[:, :], equal_no[:, :], equal[:, :], ALU.mult))
                link(v_.tensor_scalar(equal_no[:, :], equal_no[:, :], float(FAR), None, ALU.add))
                dve.wait_ge(c_tot, 17)
                link(v_.tensor_scalar(need[:, :], pS[:, 0:1], -1.0, float(K_SEL), ALU.mult, ALU.add))
                scratch = (keys, equal, w_flag_f)
                with dve.Fori(0, NUMBER_DIGITS) as b:
                    before = b * 3 + count[0]
                    digit = digits_f_flat[:, bass.ds((b + (16 - NUMBER_DIGITS)) * 3, 3)]
                    v_.tensor_scalar(upto_cand[:, :], digit, upto[:, 0:1], None, ALU.add).then_inc(c_step, 1)
                    alone(dve, c_step, before + 1)
                    for k in range(3):
                        last = v_.tensor_scalar(scratch[k][:, :], equal_no[:, :], upto_cand[:, k:k + 1], 0.0, ALU.is_le, ALU.add,
                                                accum_out=cnt[:, k:k + 1])
                    last.then_inc(c_cnt, 1)
                    alone(dve, c_tot, b + 18)
                    v_.tensor_scalar(short[:, :], pS[:, 0:3], need[:, 0:1], None, ALU.is_lt).then_inc(c_step, 1)
                    alone(dve, c_step, before + 2)
                    v_.scalar_tensor_tensor(out=upto_cand[:, :], in0=upto_cand[:, :], scalar=1.0, in1=short[:, :],
                                            op0=ALU.mult, op1=ALU.mult).then_inc(c_ready, 1)
                    alone(dve, c_ready, b + 17)
                    v_.reduce_max(upto_part[:, :], upto_cand[:, :], axis=AX_X).then_inc(c_lift, 1)
                    alone(dve, c_lift, b + 1)
                    v_.tensor_tensor(upto[:, :], upto[:, :], upto_part[:, :], ALU.max).then_inc(c_step, 1)
                    alone(dve, c_step, before + 3)
                count[0] += 3 * NUMBER_DIGITS
                link(v_.tensor_scalar(upto_cand[:, 0:1], upto[:, :], 1.0, None, ALU.add))
                link(v_.tensor_scalar(equal[:, :], equal_no[:, :], upto_cand[:, 0:1], None, ALU.is_le))
                link(v_.tensor_tensor(heavier[:, :], heavier[:, :], equal[:, :], ALU.add))
                link(v_.tensor_tensor(keys[:, :], heavier[:, :], numbers, ALU.mult))
                with dve.Fori(0, BASE) as t:
                    v_.max(top8[:, :], keys[:, :]).then_inc(c_take, 1)
                    alone(dve, c_take, t * 2 + 1)
                    v_.tensor_copy(lists[:, bass.ds(t * 8, 8)], top8[:, :])
                    v_.match_replace(keys[:, :], top8[:, :], keys[:, :], 0.0).then_inc(c_take, 1)
                    alone(dve, c_take, t * 2 + 2)
                for k in range(SPILL):
                    link(v_.max(spill[:, k * 8:(k + 1) * 8], keys[:, :]))
                    link(v_.match_replace(keys[:, :], spill[:, k * 8:(k + 1) * 8], keys[:, :], 0.0))
                dve.sem_inc(c_spill, 1)
                v_.memset(nx[:, :, :, :], 0.0)
                v_.memset(at_row[:, :, :], 0)
                dve.wait_ge(f_split, 2)
                v_.tensor_tensor(f1_lo[:, :, :], f1_in[:, :, :], f1_hi[:, :, :].bitcast(F32), ALU.subtract)
                v_.tensor_tensor(f2_lo[:, :, :], f2_in[:, :, :], f2_hi[:, :, :].bitcast(F32), ALU.subtract)
                dve.wait_ge(c_spread, 16)
                link(v_.tensor_scalar(equal[:, :], keys[:, :], 0.0, 0.0, ALU.is_gt, ALU.add, accum_out=counts[:, 0:1]))
                v_.tensor_scalar(equal[:, 0:SPILL * 8], spread[:, :], 0.0, 0.0, ALU.is_gt, ALU.add,
                                 accum_out=counts[:, 1:2]).then_inc(c_cnt, 1)
                dve.wait_ge(c_tot, 18 + NUMBER_DIGITS)
                for k in range(2):
                    last = v_.reduce_max(tallies[0:1, k:k + 1], pT[0][0:1, k * P:(k + 1) * P], axis=AX_X)
                link(last)
                link(v_.tensor_scalar(tallies_i[0:1, 0:2], tallies[0:1, 0:2], 7.0, None, ALU.add))
                link(v_.tensor_scalar(tallies_i[0:1, 0:2], tallies_i[0:1, 0:2], 3, None, ALU.logical_shift_right))
                link(v_.tensor_copy(tallies[0:1, 0:2], tallies_i[0:1, 0:2]))
                v_.tensor_tensor(tallies[0:1, 2:3], tallies[0:1, 0:1], tallies[0:1, 1:2], ALU.add).then_inc(c_cnt, 1)
                dve.wait_ge(c_cnt, 19 + NUMBER_DIGITS)
                link(v_.tensor_scalar(turns_i[0:1, :], tallies[0:1, 2:3], float(BASE - 1), None, ALU.add))
                v_.memset(lists[:, BASE * 8:], 0.0)
                link(v_.memset(top8[:, :], 0.0))
                spread_turns = dve.value_load(tallies_i[0:1, 1:2], min_val=0, max_val=SPILL)
                rest_turns = dve.value_load(tallies_i[0:1, 0:1], min_val=0, max_val=REST)
                taken = BASE * 2
                for k in range(SPILL):
                    link(v_.max(lists[:, (BASE + k) * 8:(BASE + k + 1) * 8], spread[:, :]))
                    link(v_.match_replace(spread[:, :], lists[:, (BASE + k) * 8:(BASE + k + 1) * 8], spread[:, :], 0.0))
                with dve.If(rest_turns > 0):
                    with dve.Fori(0, rest_turns) as t:
                        v_.max(top8[:, :], keys[:, :]).then_inc(c_take, 1)
                        alone(dve, c_take, t * 2 + (taken + 1))
                        v_.tensor_copy(lists[:, bass.ds((t + spread_turns) * 8 + BASE * 8, 8)], top8[:, :])
                        v_.match_replace(keys[:, :], top8[:, :], keys[:, :], 0.0).then_inc(c_take, 1)
                        alone(dve, c_take, t * 2 + (taken + 2))
                link(v_.tensor_scalar(none[:, :], lists[:, :], 0.0, float(FAR), ALU.is_equal, ALU.mult))
                v_.scalar_tensor_tensor(out=lists_i[:, :], in0=lists[:, :], scalar=-1.0, in1=none[:, :],
                                        op0=ALU.add, op1=ALU.add)

        QR = 4 * P
        NX_LD, RO_LD, Y_ST = [sem("nx_ld0"), sem("nx_ld1")], [sem("ro_ld0"), sem("ro_ld1")], [sem("y_st0"), sem("y_st1")]
        (q_idx, q_put, x_turned, x_hi, x_lo, l1_done, act_done, hh_done, hl_done, l2_done, y_add,
         y_done) = (sem(k) for k in ("q_idx", "q_put", "x_turned", "x_hi", "x_lo",
                                     "l1_done", "act_done", "hh_done", "hl_done", "l2_done", "y_add", "y_done"))
        pA = [pS, pE]
        pY = [[pO[0], pO[1]], [pZ, pW]]
        CH = 2 * FH
        Y_FREE = [sem("y_free0"), sem("y_free1")]
        MIN_TURNS, MAX_TURNS = BASE, BASE + SPILL + REST

        def turns(eng, body):
            n = eng.value_load(turns_i[0:1, 0:1], min_val=MIN_TURNS - 1, max_val=MAX_TURNS - 1)
            body(0)
            with eng.Fori(0, n) as t:
                body(t + 1)
            return n

        with phase() as block:
            @block.gpsimd
            def _(pool):
                g = nc.gpsimd

                def fetch(t, k):
                    if not (isinstance(t, int) and t == 0):
                        alone(pool, Y_ST[k], (t - 1) * 16 * RING)
                        pool.sem_inc(Y_FREE[k], 1)
                        g.tensor_copy(put_i[:, k, :], ask_i[:, k, :]).then_inc(q_put, 1)
                        alone(pool, q_put, (t - 1) * 2 + k + 1)
                    g.tensor_copy(ask_i[:, k, :], lists_i[:, bass.ds(t * 8 + k * RING, RING)]).then_inc(q_idx, 1)
                    alone(pool, q_idx, t * 2 + k + 1)
                    for r in range(RING):
                        g.indirect_dma_start(out=at_row[:, k, r:r + 1], out_offset=None, in_=row_of,
                                             in_offset=bass.IndirectOffsetOnAxis(ap=ask_i[:, k, r:r + 1], axis=0),
                                             bounds_check=EXT - 1, oob_is_err=False).then_inc(RO_LD[k], 16)
                    alone(pool, RO_LD[k], (t + 1) * 16 * RING)
                    if not (isinstance(t, int) and t == 0):
                        alone(pool, x_lo, t * 2 + k - 1)
                    for r in range(RING):
                        g.indirect_dma_start(out=nx[:, k, r, :], out_offset=None, in_=normed,
                                             in_offset=bass.IndirectOffsetOnAxis(ap=at_row[:, k, r:r + 1], axis=0)
                                             ).then_inc(NX_LD[k], 16)

                def put(t, k):
                    for r in range(RING):
                        alone(pool, y_done, (t * 2 + k) * RING + r + 1)
                        g.indirect_dma_start(out=out, out_offset=bass.IndirectOffsetOnAxis(ap=put_i[:, k, r:r + 1], axis=0),
                                             in_=y[:, k, r, :], in_offset=None, bounds_check=N - 1, oob_is_err=False,
                                             compute_op=ALU.add).then_inc(Y_ST[k], 16)

                for k in range(2):
                    fetch(0, k)

                def turn_body(t):
                    for k in range(2):
                        fetch(t + 1, k)
                        put(t, k)

                last_turn = turns(pool, turn_body)
                for k in range(2):
                    pool.wait_ge(Y_ST[k], (last_turn + 1) * (16 * RING))
                    pool.wait_ge(NX_LD[k], (last_turn + 2) * (16 * RING))

            @block.tensor
            def _(pe):
                t_ = nc.tensor

                def turn_rows(t, k):
                    q = t * 2 + k
                    pe.wait_ge(NX_LD[k], (t + 1) * 16 * RING)
                    at_least(pe, x_lo, q)
                    for c in range(KC):
                        for r in range(RING):
                            last = t_.transpose(pT[c][:, r * P:(r + 1) * P], nx[:, k, r, c * P:(c + 1) * P], ident[:, :])
                    last.then_inc(x_turned, 1)

                def hidden(t, k, f):
                    c = t * CH + k * FH + f
                    if f == 0:
                        pe.wait_ge(x_lo, t * 2 + k + 1)
                    at_least(pe, act_done, c - 1)
                    u = slice(f * P, (f + 1) * P)
                    for i in range(KC):
                        t_.matmul(pA[f % 2][:, :], f1_hi[:, i, u], fx_hi[:, k, i, :], start=(i == 0), stop=False)
                        t_.matmul(pA[f % 2][:, :], f1_lo[:, i, u], fx_hi[:, k, i, :], start=False, stop=False)
                        last = t_.matmul(pA[f % 2][:, :], f1_hi[:, i, u], fx_lo[:, k, i, :], start=False, stop=(i == KC - 1))
                    last.then_inc(l1_done, 1)

                def output(t, k, f):
                    c = t * CH + k * FH + f
                    pe.wait_ge(hl_done, c + 1)
                    if f == 0:
                        at_least(pe, y_add, (t * 2 + k - 1) * RING)
                    for r in range(RING):
                        bank = pY[k][r // 2][:, (r % 2) * D:(r % 2 + 1) * D]
                        rr = slice(r * P, (r + 1) * P)
                        s = f % 4
                        last_f = f == FH - 1
                        t_.matmul(bank, hid_hi[:, s, rr], f2_hi[:, f, :], start=(f == 0 and r % 2 == 0), stop=False,
                                  skip_group_check=True)
                        t_.matmul(bank, hid_lo[:, s, rr], f2_hi[:, f, :], start=False, stop=False, skip_group_check=True)
                        last = t_.matmul(bank, hid_hi[:, s, rr], f2_lo[:, f, :], start=False, stop=last_f,
                                         skip_group_check=True)
                    last.then_inc(l2_done, 1)

                turn_rows(0, 0)

                def turn_body(t):
                    for k in range(2):
                        for f in range(FH):
                            hidden(t, k, f)
                            if f == FH // 2:
                                turn_rows(t + k, 1 - k)
                            if f >= 2:
                                output(t, k, f - 2)
                            elif k:
                                output(t, 0, FH - 2 + f)
                            elif not isinstance(t, int):
                                output(t - 1, 1, FH - 2 + f)

                last_turn = turns(pe, turn_body)
                for f in range(FH - 2, FH):
                    output(last_turn, 1, f)

            @block.scalar
            def _(act):
                nc.scalar.preload_act_table(ACT.Gelu_apprx_tanh)

                def high_rows(t, k):
                    act.wait_ge(x_turned, t * 2 + k + 1)
                    for c in range(KC):
                        last = nc.scalar.activation(fx_hi[:, k, c, :], pT[c][:, :], ACT.Copy)
                    last.then_inc(x_hi, 1)

                def gelu(t, k, f):
                    c = t * CH + k * FH + f
                    act.wait_ge(l1_done, c + 1)
                    at_least(act, hl_done, c - 1)
                    nc.scalar.activation(hid[:, f % 2, :], pA[f % 2][:, :], ACT.Gelu_apprx_tanh,
                                         bias=fb1_col[:, f:f + 1]).then_inc(act_done, 1)
                    act.wait_ge(act_done, c + 1)
                    at_least(act, l2_done, c - 3)
                    nc.scalar.activation(hid_hi[:, f % 4, :], hid[:, f % 2, :], ACT.Copy).then_inc(hh_done, 1)

                high_rows(0, 0)

                def turn_body(t):
                    for k in range(2):
                        for f in range(FH):
                            gelu(t, k, f)
                            if f == FH // 2:
                                high_rows(t + k, 1 - k)

                turns(act, turn_body)

            @block.vector
            def _(dve):
                v_ = nc.vector

                def low_rows(t, k):
                    q = t * 2 + k
                    dve.wait_ge(x_hi, q + 1)
                    for c in range(KC):
                        v_.tensor_tensor(fx_lo[:, k, c, :], pT[c][:, :], fx_hi[:, k, c, :].bitcast(F32), ALU.subtract)
                    at_least(dve, y_done, (q - 1) * RING)
                    v_.tensor_copy(wq[:, k, :], nx[:, k, :, D]).then_inc(x_lo, 1)

                def low_hidden(t, k, f):
                    c = t * CH + k * FH + f
                    dve.wait_ge(hh_done, c + 1)
                    v_.tensor_tensor(hid_lo[:, f % 4, :], hid[:, f % 2, :], hid_hi[:, f % 4, :].bitcast(F32),
                                     ALU.subtract).then_inc(hl_done, 1)

                def weigh(t, k):
                    q = t * 2 + k
                    dve.wait_ge(l2_done, (q + 1) * FH)
                    dve.wait_ge(Y_FREE[k], t + 1)
                    for r in range(RING):
                        bank = pY[k][r // 2][:, (r % 2) * D:(r % 2 + 1) * D]
                        v_.tensor_tensor(y_sum[:, r % 2, :], bank, fb2_row[:, :], ALU.add).then_inc(y_add, 1)
                        alone(dve, y_add, q * RING + r + 1)
                        v_.tensor_scalar(y[:, k, r, :], y_sum[:, r % 2, :], wq[:, k, r:r + 1], None,
                                         ALU.mult).then_inc(y_done, 1)

                low_rows(0, 0)

                def turn_body(t):
                    for k in range(2):
                        for f in range(FH):
                            low_hidden(t, k, f)
                            if f == 2:
                                if k:
                                    weigh(t, 0)
                                elif not isinstance(t, int):
                                    weigh(t - 1, 1)
                            if f == FH // 2:
                                low_rows(t + k, 1 - k)

                last_turn = turns(dve, turn_body)
                weigh(last_turn, 1)


_INS = ['x', 'src', 'dst', 'L0_gnn_W1', 'L0_gnn_b1', 'L0_gnn_W2', 'L0_gnn_b2', 'L0_gnn_W3', 'L0_gnn_b3',
        'L0_ffn_wr', 'L0_ffn_br', 'L0_ffn_w1', 'L0_ffn_b1', 'L0_ffn_w2', 'L0_ffn_b2']


def kernel(**inputs):
    import numpy as _np
    import concourse.bacc as _bacc
    from concourse import mybir as _mybir
    from concourse.bass_utils import run_bass_kernel_spmd as _run

    nc = _bacc.Bacc("TRN2", target_bir_lowering=False, num_devices=1)
    arrays, args = {}, []
    for name in _INS:
        a = _np.ascontiguousarray(inputs[name])
        arrays[f"in_{name}_dram"] = a
        args.append(nc.dram_tensor(f"in_{name}_dram", a.shape, _mybir.dt.from_np(a.dtype), kind="ExternalInput").ap())
    args.append(nc.dram_tensor("out_0_dram", inputs['x'].shape, _mybir.dt.float32, kind="ExternalOutput").ap())
    gnn_ffn(nc, *args)
    r = _run(nc, [arrays], core_ids=[0])
    return r.results[0]["out_0_dram"]
```
